# Optimizing a Trainium2 kernel written in Bass

```python
import numpy as np
import jax
import jax.numpy as jnp

def _softmax(x, axis=-1):
    return jax.nn.softmax(x, axis=axis)

def _gelu(x):
    return jax.nn.gelu(x, approximate=True)

def _silu(x):
    return jax.nn.silu(x)

def _sigmoid(x):
    return jax.nn.sigmoid(x)

def _layernorm(x, axis=-1, eps=1e-05):
    m = jnp.mean(x, axis=axis, keepdims=True)
    v = jnp.var(x, axis=axis, keepdims=True)
    return (x - m) / jnp.sqrt(v + eps)

def _scatter_add(tgt, idx, src, axis=0):
    return tgt.at[idx].add(src)

def _segment_sum(src, seg, n):
    return jax.ops.segment_sum(src, seg, n)
kernel_name = 'mk_gnn_preln_d4_gnn_r64_a15955'

def setup_inputs(seed: int=0):
    np.random.seed(seed)
    _w = jnp.asarray

    def _rec_inputs():
        import jax
        import jax.numpy as jnp
        _gk = jax.random.key(seed)
        x = -0.0002117 + 1 * jax.random.normal(jax.random.fold_in(_gk, 1), (10000, 512), jnp.float32)
        src = jax.random.randint(jax.random.fold_in(_gk, 2), (5000,), 0, 10000, jnp.int32)
        dst = jnp.minimum((10000 * jax.random.uniform(jax.random.fold_in(_gk, 3), (5000,)) ** 2.0).astype(jnp.int32), 9999)
        _o = jnp.argsort(dst, stable=True)
        src = src[_o]
        dst = dst[_o]
        edge_attr_512 = -8.16379e-05 + 0.999858 * jax.random.normal(jax.random.fold_in(_gk, 12), (5000, 512), jnp.float32)
        return (x, src, dst, edge_attr_512)
    x, src, dst, edge_attr_512 = _rec_inputs()

    def _L0_gnn_setup():
        import jax, jax.numpy as jnp
        import numpy as np
        BN_EPS = 1e-05

        def batch_norm(h, gamma, beta):
            mu = jnp.mean(h, axis=0)
            var = jnp.var(h, axis=0)
            return (h - mu) * jax.lax.rsqrt(var + BN_EPS) * gamma + beta
        key = jax.random.key(seed)
        ks = jax.random.split(key, 6)
        N, E, dim = (50000, 25000, 512)
        hidden = dim * 2
        x = jax.random.normal(ks[0], (N, dim), dtype=jnp.float32)
        edge_index = jax.random.randint(ks[1], (2, E), 0, N, dtype=jnp.int64)
        s1 = 1.0 / np.sqrt(dim)
        s2 = 1.0 / np.sqrt(hidden)
        return {'x': x, 'edge_index': edge_index, 'eps': jnp.float32(0.0), 'W1': jax.random.uniform(ks[2], (dim, hidden), jnp.float32, -s1, s1), 'b1': jnp.zeros((hidden,), jnp.float32), 'g1': jnp.ones((hidden,), jnp.float32), 'be1': jnp.zeros((hidden,), jnp.float32), 'W2': jax.random.uniform(ks[3], (hidden, dim), jnp.float32, -s2, s2), 'b2': jnp.zeros((dim,), jnp.float32), 'g2': jnp.ones((dim,), jnp.float32), 'be2': jnp.zeros((dim,), jnp.float32)}
    _L0_gnn_all = _L0_gnn_setup()
    _L0_gnn_in = {k: v for k, v in _L0_gnn_all.items() if k in ('eps', 'W1', 'b1', 'g1', 'be1', 'W2', 'b2', 'g2', 'be2')}
    del _L0_gnn_all

    def _L1_gnn_setup():
        import jax, jax.numpy as jnp
        import numpy as np
        N = 10000
        E = 2500
        C_IN = 512
        C_H = 512

        def _gcn_conv(x, W, b, src, dst, n):
            h = x @ W
            deg = jnp.zeros((n,), x.dtype).at[dst].add(1.0)
            dis = jax.lax.rsqrt(jnp.maximum(deg, 1.0))
            norm = dis[src] * dis[dst]
            msg = h[src] * norm[:, None]
            out = jax.ops.segment_sum(msg, dst, num_segments=n)
            return out + b
        key = jax.random.key(seed)
        ks = jax.random.split(key, 4)
        x = jax.random.normal(ks[0], (N, C_IN), dtype=jnp.float32)
        edge_index = jax.random.randint(ks[1], (2, E), 0, N, dtype=jnp.int64)
        W1 = jax.random.normal(ks[2], (C_IN, C_H), dtype=jnp.float32) / np.float32(np.sqrt(C_IN))
        b1 = jnp.zeros((C_H,), dtype=jnp.float32)
        W2 = jax.random.normal(ks[3], (C_H, C_H), dtype=jnp.float32) / np.float32(np.sqrt(C_H))
        b2 = jnp.zeros((C_H,), dtype=jnp.float32)
        return {'x': x, 'edge_index': edge_index, 'W1': W1, 'b1': b1, 'W2': W2, 'b2': b2}
    _L1_gnn_all = _L1_gnn_setup()
    _L1_gnn_in = {k: v for k, v in _L1_gnn_all.items() if k in ('W1', 'b1', 'W2', 'b2')}
    del _L1_gnn_all

    def _L2_gnn_setup():
        import jax, jax.numpy as jnp
        import numpy as np
        N_NODES = 20000
        N_EDGES = 3125
        N_SEG = 16
        EXTENT = 32
        N_PATHS = 64
        OP_SIZE = N_SEG * EXTENT
        key = jax.random.key(seed)
        k1, k2, k3, k4, k5, k6 = jax.random.split(key, 6)
        x_nodes = jax.random.normal(k1, (N_NODES, OP_SIZE), dtype=jnp.float32)
        x_edges = jax.random.normal(k2, (N_EDGES, OP_SIZE), dtype=jnp.float32)
        path_coeffs = jax.random.normal(k3, (N_PATHS,), dtype=jnp.float32)
        src = jax.random.randint(k4, (N_EDGES,), 0, N_NODES, dtype=jnp.int64)
        dst = jax.random.randint(k5, (N_EDGES,), 0, N_NODES, dtype=jnp.int64)
        path_indices = jax.random.randint(k6, (N_PATHS, 3), 0, N_SEG, dtype=jnp.int64)
        return {'x_nodes': x_nodes, 'x_edges': x_edges, 'path_coeffs': path_coeffs, 'src': src, 'dst': dst, 'path_indices': path_indices}
    _L2_gnn_all = _L2_gnn_setup()
    _L2_gnn_in = {k: v for k, v in _L2_gnn_all.items() if k in ('path_coeffs', 'path_indices')}
    del _L2_gnn_all

    def _L3_gnn_setup():
        import jax, jax.numpy as jnp
        import numpy as np
        N_NODES = 50000
        N_EDGES = 2500
        D = 512
        D_OUT = 512

        def _segment_mean(msgs, seg, n):
            s = jax.ops.segment_sum(msgs, seg, num_segments=n)
            c = jax.ops.segment_sum(jnp.ones((seg.shape[0], 1), msgs.dtype), seg, num_segments=n)
            return s / jnp.maximum(c, 1.0)
        key = jax.random.key(seed)
        ks = jax.random.split(key, 16)
        lim = 1.0 / np.sqrt(D)
        lim2 = 1.0 / np.sqrt(2 * D)
        return {'node_embs': jax.random.normal(ks[0], (N_NODES, D), jnp.float32), 'edge_embs': jax.random.normal(ks[1], (N_EDGES, D), jnp.float32), 'src': jax.random.randint(ks[2], (N_EDGES,), 0, N_NODES), 'dst': jax.random.randint(ks[3], (N_EDGES,), 0, N_NODES), 'WO_w': jax.random.uniform(ks[4], (D, D), jnp.float32, -lim, lim), 'WO_b': jax.random.uniform(ks[5], (D,), jnp.float32, -lim, lim), 'WI_w': jax.random.uniform(ks[6], (D, D), jnp.float32, -lim, lim), 'WI_b': jax.random.uniform(ks[7], (D,), jnp.float32, -lim, lim), 'WS_w': jax.random.uniform(ks[8], (D, D), jnp.float32, -lim, lim), 'WS_b': jax.random.uniform(ks[9], (D,), jnp.float32, -lim, lim), 'mlp_w': jax.random.uniform(ks[10], (D_OUT, 2 * D), jnp.float32, -lim2, lim2), 'mlp_b': jax.random.uniform(ks[11], (D_OUT,), jnp.float32, -lim2, lim2), 'prelu_a': jnp.full((1,), 0.25, jnp.float32), 'n_nodes': N_NODES}
    _L3_gnn_all = _L3_gnn_setup()
    _L3_gnn_in = {k: v for k, v in _L3_gnn_all.items() if k in ('WO_w', 'WO_b', 'WI_w', 'WI_b', 'WS_w', 'WS_b', 'mlp_w', 'mlp_b', 'prelu_a')}
    del _L3_gnn_all
    return {'x': x, 'src': src, 'dst': dst, 'edge_attr_512': edge_attr_512, 'L0_gnn_eps': _L0_gnn_in['eps'], 'L0_gnn_W1': _L0_gnn_in['W1'], 'L0_gnn_b1': _L0_gnn_in['b1'], 'L0_gnn_g1': _L0_gnn_in['g1'], 'L0_gnn_be1': _L0_gnn_in['be1'], 'L0_gnn_W2': _L0_gnn_in['W2'], 'L0_gnn_b2': _L0_gnn_in['b2'], 'L0_gnn_g2': _L0_gnn_in['g2'], 'L0_gnn_be2': _L0_gnn_in['be2'], 'L1_gnn_W1': _L1_gnn_in['W1'], 'L1_gnn_b1': _L1_gnn_in['b1'], 'L1_gnn_W2': _L1_gnn_in['W2'], 'L1_gnn_b2': _L1_gnn_in['b2'], 'L2_gnn_path_coeffs': _L2_gnn_in['path_coeffs'], 'L2_gnn_path_indices': _L2_gnn_in['path_indices'], 'L3_gnn_WO_w': _L3_gnn_in['WO_w'], 'L3_gnn_WO_b': _L3_gnn_in['WO_b'], 'L3_gnn_WI_w': _L3_gnn_in['WI_w'], 'L3_gnn_WI_b': _L3_gnn_in['WI_b'], 'L3_gnn_WS_w': _L3_gnn_in['WS_w'], 'L3_gnn_WS_b': _L3_gnn_in['WS_b'], 'L3_gnn_mlp_w': _L3_gnn_in['mlp_w'], 'L3_gnn_mlp_b': _L3_gnn_in['mlp_b'], 'L3_gnn_prelu_a': _L3_gnn_in['prelu_a']}

def reference(x, src, dst, edge_attr_512, L0_gnn_eps, L0_gnn_W1, L0_gnn_b1, L0_gnn_g1, L0_gnn_be1, L0_gnn_W2, L0_gnn_b2, L0_gnn_g2, L0_gnn_be2, L1_gnn_W1, L1_gnn_b1, L1_gnn_W2, L1_gnn_b2, L2_gnn_path_coeffs, L2_gnn_path_indices, L3_gnn_WO_w, L3_gnn_WO_b, L3_gnn_WI_w, L3_gnn_WI_b, L3_gnn_WS_w, L3_gnn_WS_b, L3_gnn_mlp_w, L3_gnn_mlp_b, L3_gnn_prelu_a):
    import jax
    import jax.numpy as jnp

    def _L0_gnn_ref(x, edge_index, eps, W1, b1, g1, be1, W2, b2, g2, be2):
        import jax, jax.numpy as jnp
        import numpy as np
        BN_EPS = 1e-05

        def batch_norm(h, gamma, beta):
            mu = jnp.mean(h, axis=0)
            var = jnp.var(h, axis=0)
            return (h - mu) * jax.lax.rsqrt(var + BN_EPS) * gamma + beta
        N = x.shape[0]
        src, dst = (edge_index[0], edge_index[1])
        agg = jax.ops.segment_sum(x[src], dst, num_segments=N)
        h = (1.0 + eps) * x + agg
        h = jax.nn.relu(batch_norm(h @ W1 + b1, g1, be1))
        h = h @ W2 + b2
        h = jax.nn.relu(batch_norm(h, g2, be2))
        return x + h

    def _L1_gnn_ref(x, edge_index, W1, b1, W2, b2):
        import jax, jax.numpy as jnp
        import numpy as np
        N = 10000
        E = 2500
        C_IN = 512
        C_H = 512

        def _gcn_conv(x, W, b, src, dst, n):
            h = x @ W
            deg = jnp.zeros((n,), x.dtype).at[dst].add(1.0)
            dis = jax.lax.rsqrt(jnp.maximum(deg, 1.0))
            norm = dis[src] * dis[dst]
            msg = h[src] * norm[:, None]
            out = jax.ops.segment_sum(msg, dst, num_segments=n)
            return out + b
        n = x.shape[0]
        loops = jnp.arange(n, dtype=edge_index.dtype)
        src = jnp.concatenate([edge_index[0], loops])
        dst = jnp.concatenate([edge_index[1], loops])
        h = _gcn_conv(x, W1, b1, src, dst, n)
        h = jax.nn.relu(h)
        return _gcn_conv(h, W2, b2, src, dst, n)

    def _L2_gnn_ref(x_nodes, x_edges, path_coeffs, src, dst, path_indices):
        import jax, jax.numpy as jnp
        import numpy as np
        N_NODES = 20000
        N_EDGES = 3125
        N_SEG = 16
        EXTENT = 32
        N_PATHS = 64
        OP_SIZE = N_SEG * EXTENT
        n_nodes = x_nodes.shape[0]
        x1 = x_nodes[src].reshape(-1, N_SEG, EXTENT)
        x2 = x_edges.reshape(-1, N_SEG, EXTENT)
        i1, i2, i3 = (path_indices[:, 0], path_indices[:, 1], path_indices[:, 2])
        contrib = path_coeffs[None, :, None] * x1[:, i1, :] * x2[:, i2, :]
        edge_out = jnp.zeros((x2.shape[0], N_SEG, EXTENT), x_nodes.dtype).at[:, i3, :].add(contrib)
        out = jnp.zeros((n_nodes, OP_SIZE), x_nodes.dtype).at[dst].add(edge_out.reshape(-1, OP_SIZE))
        return out

    def _L3_gnn_ref(node_embs, edge_embs, src, dst, WO_w, WO_b, WI_w, WI_b, WS_w, WS_b, mlp_w, mlp_b, prelu_a, n_nodes):
        import jax, jax.numpy as jnp
        import numpy as np
        N_NODES = 50000
        N_EDGES = 2500
        D = 512
        D_OUT = 512

        def _segment_mean(msgs, seg, n):
            s = jax.ops.segment_sum(msgs, seg, num_segments=n)
            c = jax.ops.segment_sum(jnp.ones((seg.shape[0], 1), msgs.dtype), seg, num_segments=n)
            return s / jnp.maximum(c, 1.0)
        h_out = _segment_mean(node_embs[src] - edge_embs, dst, n_nodes)
        h_in = _segment_mean(node_embs[dst] - edge_embs, src, n_nodes)
        h_neigh = h_out @ WO_w.T + WO_b + (h_in @ WI_w.T + WI_b)
        hs = node_embs @ WS_w.T + WS_b
        z = jnp.concatenate((hs, h_neigh), axis=1) @ mlp_w.T + mlp_b
        return jnp.where(z >= 0, z, prelu_a * z)
    edge_index = jnp.stack([src, dst])
    h = jnp.maximum(_layernorm(x, axis=-1), 0.0)
    x = x + _L0_gnn_ref(h, edge_index, L0_gnn_eps, L0_gnn_W1, L0_gnn_b1, L0_gnn_g1, L0_gnn_be1, L0_gnn_W2, L0_gnn_b2, L0_gnn_g2, L0_gnn_be2)
    h = jnp.maximum(_layernorm(x, axis=-1), 0.0)
    x = x + _L1_gnn_ref(h, edge_index, L1_gnn_W1, L1_gnn_b1, L1_gnn_W2, L1_gnn_b2)
    h = jnp.maximum(_layernorm(x, axis=-1), 0.0)
    x = x + _L2_gnn_ref(h, edge_attr_512, L2_gnn_path_coeffs, src, dst, L2_gnn_path_indices)
    h = jnp.maximum(_layernorm(x, axis=-1), 0.0)
    x = x + _L3_gnn_ref(h, edge_attr_512, src, dst, L3_gnn_WO_w, L3_gnn_WO_b, L3_gnn_WI_w, L3_gnn_WI_b, L3_gnn_WS_w, L3_gnn_WS_b, L3_gnn_mlp_w, L3_gnn_mlp_b, L3_gnn_prelu_a, 10000)
    return x

_drawn_inputs = setup_inputs


def setup_inputs(seed=0):
    import zlib

    import numpy as np

    out = dict(_drawn_inputs(seed))
    spreads = {'L0_gnn_b1': (0.0, 0.8),
     'L0_gnn_g1': (1.0, 0.2),
     'L0_gnn_be1': (0.0, 0.1),
     'L0_gnn_b2': (0.0, 0.8),
     'L0_gnn_g2': (1.0, 0.2),
     'L0_gnn_be2': (0.0, 0.1),
     'L1_gnn_b1': (0.0, 0.1),
     'L1_gnn_b2': (0.0, 0.1)}
    factors = {'L3_gnn_WO_b': 8.0, 'L3_gnn_WI_b': 8.0, 'L3_gnn_WS_b': 8.0, 'L3_gnn_mlp_b': 8.0}
    for name, (base, spread) in spreads.items():
        noise = np.random.default_rng([zlib.crc32(name.encode()), seed]).standard_normal(out[name].shape)
        drawn = base * np.exp(spread * noise) if base else spread * noise
        out[name] = jnp.asarray(drawn.astype(out[name].dtype))
    for name, factor in factors.items():
        out[name] = (out[name] * factor).astype(out[name].dtype)
    return out
```

```python
from contextlib import ExitStack

import numpy as np
import concourse.bass as bass
import concourse.mybir as mybir

F32 = mybir.dt.float32
F32R = mybir.dt.float32r
BF16 = mybir.dt.bfloat16
I32 = mybir.dt.int32
ALU = mybir.AluOpType
ACT = mybir.ActivationFunctionType
DS = bass.ds

P = 128
N = 10000
E = 5000
D = 512
H = 1024
DC = D // P
HC = H // P
GT = 4
GR = GT * P
NG = -(-N // GR)
TAIL = N - (NG - 1) * GR
TAIL_T = -(-TAIL // P)
PAIRS = (NG - 2) // 2
ET = -(-E // P)
EP = ET * P
EG = ET // GT
NB = 80
PADKEY = (NB - 1) * P
ZROW = EP
SPARE = EP + 1
TROWS = EP + 1 + ET
SEG, EXT, PATHS = 16, 32, 64
LN_EPS = 1e-5


def tiles_of(g_is_tail):
    return TAIL_T if g_is_tail else GT


def load_group(eng, dst, dram, g, tail, sem, width=D):
    if not tail:
        eng.dma_start(dst, dram[DS(g * GR, GR), 0:width].rearrange("(k p) d -> p k d", p=P)).then_inc(sem, 16)
        return
    full = TAIL // P
    eng.dma_start(dst[:, 0:full], dram[g * GR:g * GR + full * P, 0:width].rearrange("(k p) d -> p k d", p=P)).then_inc(sem, 16)
    eng.dma_start(dst[0:TAIL - full * P, full], dram[g * GR + full * P:N, 0:width]).then_inc(sem, 16)


def store_group(eng, dram, src, g, tail, sem):
    if not tail:
        eng.dma_start(dram[DS(g * GR, GR), :].rearrange("(k p) d -> p k d", p=P), src).then_inc(sem, 16)
        return
    full = TAIL // P
    eng.dma_start(dram[g * GR:g * GR + full * P, :].rearrange("(k p) d -> p k d", p=P), src[:, 0:full]).then_inc(sem, 16)
    eng.dma_start(dram[g * GR + full * P:N, :], src[0:TAIL - full * P, full]).then_inc(sem, 16)


def loads_done(i, tail):
    return 16 * (i + 1) + (16 if tail else 0)


def node_groups(eng, start, body):
    start(0, 0, 0, False)
    body(0, 0, 0, False, (1, 1, 0, False))
    body(1, 1, 0, False, (2, 0, 1, False))
    with eng.Fori(1, PAIRS) as i:
        body(2 * i, 0, i, False, (2 * i + 1, 1, i, False))
        body(2 * i + 1, 1, i, False, (2 * i + 2, 0, i + 1, False))
    body(NG - 2, 0, PAIRS, False, (NG - 1, 1, PAIRS, True))
    body(NG - 1, 1, PAIRS, True, None)


def edge_groups(eng, start, body):
    start(0, 0, 0)
    body(0, 0, 0, (1, 1, 0))
    body(1, 1, 0, (2, 0, 1))
    with eng.Fori(1, EG // 2 - 1) as i:
        body(2 * i, 0, i, (2 * i + 1, 1, i))
        body(2 * i + 1, 1, i, (2 * i + 2, 0, i + 1))
    last = EG // 2 - 1
    body(EG - 2, 0, last, (EG - 1, 1, last))
    body(EG - 1, 1, last, None)


def wait_uses(eng, sem, value):
    if not isinstance(value, int) or value > 0:
        eng.wait_ge(sem, value)


def nothing(*_):
    return None


def product3(nc, out, wh, wl, ah, al, first, last):
    nc.tensor.matmul(out, wl, ah, start=first, stop=False)
    nc.tensor.matmul(out, wh, al, start=False, stop=False)
    return nc.tensor.matmul(out, wh, ah, start=False, stop=last)


class Tables:
    pass


def make_tables(nc, ctx):
    t = Tables()

    def sb(name, shape, dt):
        return ctx.enter_context(nc.sbuf_tensor(name, shape, dt))

    t.ident = sb("ident", [P, P], F32)
    t.ones = sb("ones", [P, P], F32)
    t.eps = sb("eps", [P, 1], F32)
    t.rowiota = sb("rowiota", [P, P], F32)
    t.partiota = sb("partiota", [P, 1], F32)
    t.same = [sb(f"same{q}", [P, ET, P], BF16) for q in range(2)]
    t.last = [sb(f"last{q}", [P, NB], I32) for q in range(2)]
    t.dis = sb("dis", [P, NB], F32)
    t.rcnt = [sb(f"rcnt{q}", [P, NB], F32) for q in range(2)]
    t.meta = [sb(f"meta{q}", [P, ET, 4], I32) for q in range(2)]
    t.other = [sb(f"other{q}", [P, ET], I32) for q in range(2)]
    t.eid = [sb(f"eid{q}", [P, ET], I32) for q in range(2)]
    t.etab = [sb(f"etab{q}", [P, ET, 4], I32) for q in range(2)]
    t.nlast = [sb(f"nlast{q}", [P, ET], I32) for q in range(2)]
    t.fetch = [sb(f"fetch{q}", [P, ET, 3], I32) for q in range(2)]
    t.dis_other = sb("dis_other", [P, ET], F32)
    t.cut_rows = [sb(f"cut_rows{q}", [ET, 1], I32) for q in range(2)]
    t.cut_dest = [sb(f"cut_dest{q}", [ET, 1], I32) for q in range(2)]
    t.cut_same = [sb(f"cut_same{q}", [ET, ET], F32) for q in range(2)]

    def dram(name, shape, dt=F32):
        return nc.dram_tensor(name, shape, dt).ap()

    t.smeta = [dram(f"smeta{q}", [EP + 1, 4], I32) for q in range(2)]
    t.tab = dram("tab", [NB * P, 4], I32)
    t.seg_in = dram("seg_a", [TROWS, D])
    t.seg_dst = dram("seg_b", [TROWS, D])
    t.seg_src = dram("seg_c", [TROWS, D])
    t.y1 = dram("y1", [NG, P, HC, GR])
    t.y2 = dram("y2", [NG, P, DC, GR])
    t.x1 = dram("x1", [N, D])
    t.r1 = dram("r1", [N, D])
    t.x2 = dram("x2", [N, D])
    return t


def sort_edges(nc, t, src, dst):
    keys = (dst, src)
    with ExitStack() as ctx:
        ctx.enter_context(nc.cleanup_on_exit())
        def sb(name, shape, dt=F32):
            return ctx.enter_context(nc.sbuf_tensor(name, shape, dt))

        ktile = sb("ktile", [ET, 2, P], I32)
        ktile_f = sb("ktile_f", [ET, 2, P])
        kcol = sb("kcol", [P, 2, ET])
        kcol_i = sb("kcol_i", [P, 2, ET], I32)
        hi_i = sb("hi_i", [P, 2, ET], I32)
        lo_i = sb("lo_i", [P, 2, ET], I32)
        hi_f = sb("hi_f", [P, 2, ET])
        lo_f = sb("lo_f", [P, 2, ET])
        eid_f = sb("eid_f", [P, ET])
        pack = sb("pack", [P, 2, ET, 5], I32)
        krow_i = sb("krow_i", [P, 2, EP], I32)
        hrow_i = sb("hrow_i", [NB, 2, EP], I32)
        earlier = sb("earlier", [P, P])
        before = sb("before", [NB, NB])
        hot_hi = sb("hot_hi", [P, 2, ET, NB], BF16)
        hot_lo = sb("hot_lo", [P, 2, ET, P], BF16)
        count = sb("count", [NB, 2, ET + 1, P])
        incl = sb("incl", [NB, 2, P])
        start_of = sb("start_of", [NB, 2, P])
        rowsum = sb("rowsum", [NB, 2])
        lastf = sb("lastf", [NB, 2, P])
        some = sb("some", [NB, 2, P])
        disf = sb("disf", [NB, P])
        tabs = sb("tabs", [NB, P, 4], I32)
        zeros = sb("zeros", [P, D])
        onesrow = sb("onesrow", [NB, P])
        hitT = sb("hitT", [NB, 2, P])
        from_ = sb("from_", [NB, 2, P])
        scratch = sb("scratch", [P, 2, P])
        prior = sb("prior", [P, 2, ET])
        tie = sb("tie", [P, 2, ET])
        rank = sb("rank", [P, 2, ET])
        slot = sb("slot", [P, 4, 5], I32)
        psum = [ctx.enter_context(nc.psum_tensor(f"sort_ps{i}", [P, 512], F32)) for i in range(8)]

        def sem(name):
            return nc.alloc_semaphore(name)

        padded, loaded, pads_done, made = sem("padded"), sem("loaded"), sem("pads_done"), sem("made")
        step, turned, zstored = sem("sort_step"), sem("turned"), sem("zstored")
        with nc.Block() as block:
            @block.sync
            def _(sp):
                sp.wait_ge(padded, 1)
                full = E // P
                for q in range(2):
                    sp.dma_start(ktile[0:full, q, :], keys[q][0:full * P].rearrange("(t p) -> t p", p=P)).then_inc(loaded, 16)
                    sp.dma_start(ktile[full:ET, q, 0:E - full * P], keys[q][full * P:E].rearrange("(t p) -> t p", t=1)).then_inc(loaded, 16)
                    sp.dma_start(krow_i[:, q, 0:E], keys[q].rearrange("(o e) -> o e", o=1).to_broadcast([P, E])).then_inc(loaded, 16)
                sp.wait_ge(made, 1)
                for q, table in enumerate((t.seg_in, t.seg_dst, t.seg_src)):
                    sp.dma_start(table[ZROW:TROWS, :], zeros[0:TROWS - ZROW, :]).then_inc(zstored, 16)
                sp.wait_ge(zstored, 48)

            @block.gpsimd
            def _(pl):
                nc.gpsimd.memset(ktile[:], PADKEY)
                nc.gpsimd.memset(krow_i[:, :, E:EP], PADKEY).then_inc(padded, 1)
                nc.gpsimd.memset(zeros[:], 0.0).then_inc(made, 1)
                nc.gpsimd.memset(t.ident[:], 1.0)
                nc.gpsimd.memset(t.ones[:], 1.0)
                nc.gpsimd.memset(earlier[:], 1.0)
                nc.gpsimd.memset(before[:], 1.0)
                nc.gpsimd.memset(onesrow[:], 1.0)
                nc.gpsimd.memset(t.eps[:], LN_EPS)
                nc.gpsimd.iota(t.rowiota[:], pattern=[[1, P]], base=0, channel_multiplier=0, allow_small_or_imprecise_dtypes=True)
                nc.gpsimd.iota(t.partiota[:], pattern=[[1, 1]], base=0, channel_multiplier=1, allow_small_or_imprecise_dtypes=True)
                nc.gpsimd.iota(eid_f[:], pattern=[[P, ET]], base=0, channel_multiplier=1, allow_small_or_imprecise_dtypes=True).then_inc(made, 1)
                pl.wait_ge(made, 2)
                nc.gpsimd.affine_select(out=t.ident[:], in_=t.ident[:], compare_op=ALU.is_equal, fill=0.0, base=0, pattern=[[-1, P]], channel_multiplier=1)
                nc.gpsimd.affine_select(out=earlier[:], in_=earlier[:], compare_op=ALU.is_gt, fill=0.0, base=0, pattern=[[-1, P]], channel_multiplier=1)
                nc.gpsimd.affine_select(out=before[:], in_=before[:], compare_op=ALU.is_gt, fill=0.0, base=0, pattern=[[1, NB]], channel_multiplier=-1).then_inc(made, 1)

            @block.tensor
            def _(pe):
                pe.wait_ge(made, 3)
                pe.wait_ge(step, 1)
                for q in range(2):
                    mm = nc.tensor.transpose(psum[q][:, 0:ET], ktile_f[:, q, :], t.ident[0:ET, 0:ET])
                mm.then_inc(turned, 1)

            @block.vector
            def _(v):
                n = [0]

                def link(ins):
                    n[0] += 1
                    ins.then_inc(step, 1)
                    v.wait_ge(step, n[0])

                v.wait_ge(padded, 1)
                v.wait_ge(loaded, 96)
                link(nc.vector.tensor_copy(ktile_f[:], ktile[:]))
                v.wait_ge(turned, 1)
                for q in range(2):
                    link(nc.vector.tensor_copy(kcol[:, q, :], psum[q][:, 0:ET]))
                link(nc.vector.tensor_copy(kcol_i[:], kcol[:]))
                link(nc.vector.tensor_scalar(hi_i[:], kcol_i[:], 7, None, ALU.logical_shift_right))
                link(nc.vector.tensor_scalar(lo_i[:], kcol_i[:], P - 1, None, ALU.bitwise_and))
                link(nc.vector.tensor_copy(hi_f[:], hi_i[:]))
                link(nc.vector.tensor_copy(lo_f[:], lo_i[:]))
                v.wait_ge(made, 3)
                for q in range(2):
                    link(nc.vector.tensor_tensor(
                        hot_hi[:, q], t.rowiota[:, 0:NB].rearrange("p (o n) -> p o n", o=1).to_broadcast([P, ET, NB]),
                        hi_f[:, q, :].rearrange("p (t o) -> p t o", o=1).to_broadcast([P, ET, NB]), ALU.is_equal))
                    link(nc.vector.tensor_tensor(
                        hot_lo[:, q], t.rowiota[:, :].rearrange("p (o n) -> p o n", o=1).to_broadcast([P, ET, P]),
                        lo_f[:, q, :].rearrange("p (t o) -> p t o", o=1).to_broadcast([P, ET, P]), ALU.is_equal))
                    link(nc.vector.tensor_scalar(hrow_i[:, q, :], krow_i[0:NB, q, :], 7, None, ALU.logical_shift_right))
                link(nc.vector.memset(pack[:], 0))
                for q in range(2):
                    link(nc.vector.tensor_copy(pack[:, q, :, 1], kcol[:, q, :]))
                    link(nc.vector.scalar_tensor_tensor(pack[:, q, :, 2], kcol[:, 1 - q, :], float(PADKEY), kcol[:, 1 - q, :], ALU.is_lt, ALU.mult))
                    link(nc.vector.scalar_tensor_tensor(pack[:, q, :, 3], eid_f[:], float(E), eid_f[:], ALU.is_lt, ALU.mult))
                link(nc.vector.memset(count[:, :, 0, :], 0.0))

        tile_counted, added = sem("tile_counted"), sem("added")
        with nc.Block() as block:
            @block.tensor
            def _(pe):
                pe.sem_inc(added, 4)
                with pe.Fori(0, ET // 2) as i:
                    for b in range(2):
                        for q in range(2):
                            pe.wait_ge(added, 4 * i + 2 * b + q + 1)
                            nc.tensor.matmul(psum[2 * b + q][0:NB, 0:P], hot_hi[:, q, DS(2 * i + b, 1), :].rearrange("p o n -> p (o n)"),
                                             hot_lo[:, q, DS(2 * i + b, 1), :].rearrange("p o n -> p (o n)"), start=True, stop=True).then_inc(tile_counted, 1)

            @block.vector
            def _(v):
                with v.Fori(0, ET // 2) as i:
                    for b in range(2):
                        for q in range(2):
                            v.wait_ge(tile_counted, 4 * i + 2 * b + q + 1)
                            v.wait_ge(added, 4 * i + 2 * b + q + 3)
                            nc.vector.tensor_tensor(count[:, q, DS(2 * i + b + 1, 1), :], count[:, q, DS(2 * i + b, 1), :],
                                                    psum[2 * b + q][0:NB, 0:P].rearrange("p (o n) -> p o n", o=1), ALU.add).then_inc(added, 1)

        pstep, prowed, pturned, sq, tabbed = sem("pstep"), sem("prowed"), sem("pturned"), sem("sq"), sem("tabbed")
        with nc.Block() as block:
            @block.vector
            def _(v):
                n = [0]

                def link(ins):
                    n[0] += 1
                    ins.then_inc(pstep, 1)
                    v.wait_ge(pstep, n[0])

                total = count[:, :, ET, :]
                for q in range(2):
                    link(nc.vector.tensor_tensor_scan(incl[:, q, :], onesrow[:], total[:, q, :], 0.0, ALU.mult, ALU.add))
                link(nc.vector.tensor_copy(rowsum[:], incl[:, :, P - 1]))
                link(nc.vector.tensor_tensor(start_of[:], incl[:], total, ALU.subtract))
                v.wait_ge(prowed, 1)
                for q in range(2):
                    link(nc.vector.tensor_scalar(start_of[:, q, :], start_of[:, q, :], psum[4][0:NB, q:q + 1], None, ALU.add))
                link(nc.vector.tensor_tensor(lastf[:], start_of[:], total, ALU.add))
                link(nc.vector.tensor_scalar(lastf[:], lastf[:], -1.0 - ZROW, None, ALU.add))
                link(nc.vector.tensor_scalar(some[:], total, 0.0, None, ALU.is_gt))
                link(nc.vector.tensor_tensor(lastf[:], lastf[:], some[:], ALU.mult))
                link(nc.vector.tensor_scalar(lastf[:], lastf[:], float(ZROW), None, ALU.add))
                link(nc.vector.memset(tabs[:], 0))
                for q in range(2):
                    link(nc.vector.tensor_copy(tabs[:, :, q], lastf[:, q, :]))
                v.wait_ge(sq, 1)
                link(nc.vector.reciprocal(disf[:], disf[:]))
                finish_rsqrt(nc, link, disf[:], some[:, 0, :], total[:, 0, :], 1.0)
                link(nc.vector.tensor_copy(tabs[:, :, 2].bitcast(F32), disf[:]))
                v.wait_ge(pturned, 1)
                for q in range(2):
                    link(nc.vector.tensor_copy(t.last[q][:], psum[q][:, 0:NB]))
                    link(nc.vector.tensor_scalar(t.rcnt[q][:], psum[2 + q][:, 0:NB], 1.0, None, ALU.max))
                    link(nc.vector.reciprocal(t.rcnt[q][:], t.rcnt[q][:]))
                link(nc.vector.tensor_copy(t.dis[:], psum[5][:, 0:NB]))

            @block.scalar
            def _(a):
                a.wait_ge(added, 2 * ET + 4)
                a.wait_ge(made, 3)
                nc.scalar.activation(disf[:], count[:, 0, ET, :], ACT.Sqrt, bias=t.ones[0:NB, 0:1]).then_inc(sq, 1)

            @block.tensor
            def _(pe):
                pe.wait_ge(pstep, 3)
                nc.tensor.matmul(psum[4][0:NB, 0:2], before[:], rowsum[:], start=True, stop=True).then_inc(prowed, 1)
                pe.wait_ge(pstep, 20)
                for q in range(2):
                    nc.tensor.transpose(psum[q][:, 0:NB], lastf[:, q, :], t.ident[0:NB, 0:NB])
                    nc.tensor.transpose(psum[2 + q][:, 0:NB], count[:, q, ET, :], t.ident[0:NB, 0:NB])
                nc.tensor.transpose(psum[5][:, 0:NB], disf[:], t.ident[0:NB, 0:NB]).then_inc(pturned, 1)

            @block.sync
            def _(sp):
                sp.wait_ge(pstep, 20)
                sp.dma_start(t.tab.rearrange("(a b) c -> a (b c)", b=P), tabs[:].rearrange("a b c -> a (b c)")).then_inc(tabbed, 16)
                sp.wait_ge(tabbed, 16)

        hit, based, picked, tied = sem("hit"), sem("based"), sem("picked"), sem("tied")
        dotted, rstep = sem("dotted"), sem("rstep")
        with nc.Block() as block:
            @block.vector
            def _(v):
                v.sem_inc(rstep, 2)
                with v.Fori(0, ET) as i:
                    for q in range(2):
                        v.wait_ge(picked, 2 * i + q + 1)
                        nc.vector.tensor_scalar(hitT[:, q, :], hrow_i[:, q, DS(i * P, P)], t.partiota[0:NB, :], None, ALU.is_equal).then_inc(hit, 1)
                        nc.vector.tensor_tensor(from_[:, q, :], count[:, q, DS(i, 1), :].rearrange("p o n -> p (o n)"), start_of[:, q, :], ALU.add).then_inc(based, 1)
                    for q in range(2):
                        v.wait_ge(rstep, 2 * i + q + 1)
                        nc.vector.tensor_scalar(scratch[:, q, :], krow_i[:, q, DS(i * P, P)], kcol[:, q, DS(i, 1)], None, ALU.is_equal).then_inc(tied, 1)
                    for q in range(2):
                        v.wait_ge(tied, 2 * i + q + 1)
                        nc.vector.scalar_tensor_tensor(scratch[:, q, :], scratch[:, q, :], 1.0, earlier[:], ALU.mult, ALU.mult,
                                                       accum_out=tie[:, q, DS(i, 1)]).then_inc(dotted, 1)
                    for q in range(2):
                        v.wait_ge(dotted, 2 * i + q + 1)
                        v.wait_ge(picked, 2 * i + q + 3)
                        nc.vector.scalar_tensor_tensor(scratch[:, q, :], psum[q][:, 0:P], 1.0, hot_lo[:, q, DS(i, 1), :].rearrange("p o n -> p (o n)"),
                                                       ALU.mult, ALU.mult, accum_out=prior[:, q, DS(i, 1)]).then_inc(rstep, 1)
                v.wait_ge(rstep, 2 * ET + 2)
                nc.vector.tensor_tensor(rank[:], prior[:], tie[:], ALU.add).then_inc(rstep, 1)
                v.wait_ge(rstep, 2 * ET + 3)
                nc.vector.tensor_copy(pack[:, :, :, 0], rank[:]).then_inc(rstep, 1)

            @block.tensor
            def _(pe):
                pe.sem_inc(picked, 2)
                with pe.Fori(0, ET) as i:
                    for q in range(2):
                        pe.wait_ge(hit, 2 * i + q + 1)
                        pe.wait_ge(based, 2 * i + q + 1)
                        pe.wait_ge(rstep, 2 * i + q + 1)
                        nc.tensor.matmul(psum[q][:, 0:P], hitT[:, q, :], from_[:, q, :], start=True, stop=True).then_inc(picked, 1)

        filled, placed, sent = sem("filled"), [sem(f"placed{s}") for s in range(4)], sem("sent")
        fenced = sem("fenced")
        with nc.Block() as block:
            @block.gpsimd
            def _(pl):
                def scatter(i):
                    for b in range(2):
                        for q in range(2):
                            s = 2 * b + q
                            wait_uses(pl, placed[s], 16 * i)
                            nc.gpsimd.tensor_copy(slot[:, s, :], pack[:, q, DS(2 * i + b, 1), :].rearrange("p o c -> p (o c)")).then_inc(filled, 1)
                            pl.wait_ge(filled, 4 * i + s + 1)
                            pl.sem_inc(sent, 1)
                            nc.gpsimd.indirect_dma_start(out=t.smeta[q], out_offset=bass.IndirectOffsetOnAxis(ap=slot[:, s, 0:1], axis=0),
                                                         in_=slot[:, s, 1:5], in_offset=None).then_inc(placed[s], 16)

                scatter(0)
                with pl.Fori(1, ET // 2) as i:
                    scatter(i)
                for s in range(4):
                    pl.wait_ge(placed[s], 16 * (ET // 2))

            @block.sync
            def _(sp):
                for q in range(2):
                    sp.dma_start(t.smeta[q][EP:EP + 1, :], zeros[0:1, 0:4].bitcast(I32)).then_inc(fenced, 16)
                sp.wait_ge(fenced, 32)


def index_edges(nc, t):
    with ExitStack() as ctx:
        ctx.enter_context(nc.cleanup_on_exit())
        def sb(name, shape, dt=F32):
            return ctx.enter_context(nc.sbuf_tensor(name, shape, dt))

        def sem(name):
            return nc.alloc_semaphore(name)

        keyf = sb("keyf", [P, 2, ET])
        diag = sb("diag", [P, 4, P])
        slot = sb("islot", [P, 4], I32)
        got = sb("igot", [P, 4, 4], I32)
        end_i = sb("end_i", [ET, 2, 4], I32)
        next_i = sb("next_i", [ET, 2, 4], I32)
        cut_tab = sb("cut_tab", [ET, 2, 4], I32)
        end_f = sb("end_f", [ET, 2])
        next_f = sb("next_f", [ET, 2])
        runs_on = sb("runs_on", [ET, 2])
        final = sb("final", [ET, 2])
        rowf = sb("rowf", [ET, 2])
        limit = sb("limit", [ET, 1])
        spare = sb("spare", [ET, 1])
        destf = sb("destf", [ET, 2])
        diag_end = sb("diag_end", [ET, 2, ET])
        psum = [ctx.enter_context(nc.psum_tensor(f"index_ps{i}", [P, 512], F32)) for i in range(6)]

        back, ends, cut_got, made = sem("back"), sem("ends"), sem("cut_got"), sem("imade")
        step, ended = sem("istep"), sem("iended")
        with nc.Block() as block:
            @block.sync
            def _(sp):
                for q in range(2):
                    sp.dma_start(t.meta[q][:], t.smeta[q][0:EP, :].rearrange("(t p) c -> p t c", p=P)).then_inc(back, 16)
                    sp.dma_start(end_i[:, q, :], t.smeta[q][0:EP, :].rearrange("(t p) c -> p t c", p=P)[P - 1]).then_inc(ends, 16)
                    sp.dma_start(next_i[:, q, :], t.smeta[q][1:EP + 1, :].rearrange("(t p) c -> p t c", p=P)[P - 1]).then_inc(ends, 16)

            @block.gpsimd
            def _(pl):
                nc.gpsimd.iota(limit[:], pattern=[[1, 1]], base=2 * P, channel_multiplier=P, allow_small_or_imprecise_dtypes=True)
                nc.gpsimd.iota(spare[:], pattern=[[1, 1]], base=SPARE, channel_multiplier=1, allow_small_or_imprecise_dtypes=True).then_inc(made, 1)
                pl.wait_ge(ends, 64)
                for q in range(2):
                    nc.gpsimd.indirect_dma_start(out=cut_tab[:, q, :], out_offset=None, in_=t.tab,
                                                 in_offset=bass.IndirectOffsetOnAxis(ap=end_i[:, q, 0:1], axis=0)).then_inc(cut_got, 16)
                pl.wait_ge(cut_got, 32)

            @block.vector
            def _(v):
                n = [0]

                def link(ins):
                    n[0] += 1
                    ins.then_inc(step, 1)
                    v.wait_ge(step, n[0])

                v.wait_ge(back, 32)
                for q in range(2):
                    link(nc.vector.tensor_copy(keyf[:, q, :], t.meta[q][:, :, 0]))
                    link(nc.vector.tensor_copy(t.other[q][:], t.meta[q][:, :, 1]))
                    link(nc.vector.tensor_copy(t.eid[q][:], t.meta[q][:, :, 2]))
                v.wait_ge(ends, 64)
                link(nc.vector.tensor_copy(end_f[:], end_i[:, :, 0]))
                link(nc.vector.tensor_copy(next_f[:], next_i[:, :, 0]))
                link(nc.vector.tensor_tensor(runs_on[:], end_f[:], next_f[:], ALU.is_equal))
                for q in range(2):
                    link(nc.vector.tensor_scalar(diag_end[:, q, :], t.ident[0:ET, 0:ET], end_f[:, q:q + 1], None, ALU.mult))
                v.wait_ge(ended, 1)
                for q in range(2):
                    link(nc.vector.tensor_scalar(t.cut_same[q][:], psum[q][0:ET, 0:ET], end_f[:, q:q + 1], runs_on[:, q:q + 1], ALU.is_equal, ALU.mult))
                v.wait_ge(cut_got, 32)
                v.wait_ge(made, 1)
                for q in range(2):
                    link(nc.vector.tensor_copy(t.cut_rows[q][:], cut_tab[:, q, q:q + 1]))
                    link(nc.vector.tensor_copy(rowf[:, q:q + 1], cut_tab[:, q, q:q + 1]))
                    link(nc.vector.tensor_scalar(final[:, q:q + 1], rowf[:, q:q + 1], limit[:], runs_on[:, q:q + 1], ALU.is_lt, ALU.mult))
                    link(nc.vector.tensor_tensor(destf[:, q:q + 1], rowf[:, q:q + 1], spare[:], ALU.subtract))
                    link(nc.vector.tensor_tensor(destf[:, q:q + 1], destf[:, q:q + 1], final[:, q:q + 1], ALU.mult))
                    link(nc.vector.tensor_tensor(destf[:, q:q + 1], destf[:, q:q + 1], spare[:], ALU.add))
                    link(nc.vector.tensor_copy(t.cut_dest[q][:], destf[:, q:q + 1]))

            @block.tensor
            def _(pe):
                pe.wait_ge(step, 11)
                for q in range(2):
                    mm = nc.tensor.matmul(psum[q][0:ET, 0:ET], t.ones[0:ET, 0:ET], diag_end[:, q, :], start=True, stop=True)
                mm.then_inc(ended, 1)

        diagd, spread, same_made = sem("diagd"), sem("spread"), sem("same_made")
        filled, fetched, kept, sent = sem("ifilled"), [sem(f"fetched{s}") for s in range(4)], sem("kept"), sem("isent")
        with nc.Block() as block:
            @block.vector
            def _(v):
                v.sem_inc(same_made, 4)
                with v.Fori(0, ET // 2) as i:
                    for b in range(2):
                        for q in range(2):
                            s = 2 * b + q
                            v.wait_ge(spread, 4 * i + s + 1)
                            nc.vector.tensor_scalar(diag[:, s, :], t.ident[:], keyf[:, q, DS(2 * i + b, 1)], None, ALU.mult).then_inc(diagd, 1)
                    for b in range(2):
                        for q in range(2):
                            s = 2 * b + q
                            v.wait_ge(spread, 4 * i + s + 5)
                            nc.vector.tensor_scalar(t.same[q][:, DS(2 * i + b, 1), :].rearrange("p o n -> p (o n)"), psum[s][:, 0:P],
                                                    keyf[:, q, DS(2 * i + b, 1)], None, ALU.is_equal).then_inc(same_made, 1)
                    for b in range(2):
                        for q in range(2):
                            s = 2 * b + q
                            v.wait_ge(fetched[s], 16 * (i + 1))
                            nc.vector.tensor_copy(t.etab[q][:, DS(2 * i + b, 1), :].rearrange("p o c -> p (o c)"), got[:, s, :]).then_inc(kept, 1)

            @block.tensor
            def _(pe):
                pe.sem_inc(spread, 4)
                with pe.Fori(0, ET // 2) as i:
                    for s in range(4):
                        pe.wait_ge(diagd, 4 * i + s + 1)
                        pe.wait_ge(same_made, 4 * i + s + 1)
                        nc.tensor.matmul(psum[s][:, 0:P], t.ones[:], diag[:, s, :], start=True, stop=True).then_inc(spread, 1)

            @block.gpsimd
            def _(pl):
                pl.sem_inc(kept, 4)
                with pl.Fori(0, ET // 2) as i:
                    for b in range(2):
                        for q in range(2):
                            s = 2 * b + q
                            pl.wait_ge(kept, 4 * i + s + 1)
                            nc.gpsimd.tensor_copy(slot[:, s:s + 1], t.other[q][:, DS(2 * i + b, 1)]).then_inc(filled, 1)
                            pl.wait_ge(filled, 4 * i + s + 1)
                            pl.sem_inc(sent, 1)
                            nc.gpsimd.indirect_dma_start(out=got[:, s, :], out_offset=None, in_=t.tab,
                                                         in_offset=bass.IndirectOffsetOnAxis(ap=slot[:, s:s + 1], axis=0)).then_inc(fetched[s], 16)

        with nc.Block() as block:
            @block.vector
            def _(v):
                for q in range(2):
                    nc.vector.tensor_copy(t.nlast[q][:], t.etab[q][:, :, 0])
                    for n, what in enumerate((t.other[q][:], t.etab[q][:, :, 0], t.eid[q][:])):
                        nc.vector.tensor_copy(t.fetch[q][:, :, n], what)
                nc.vector.tensor_copy(t.dis_other[:], t.etab[0][:, :, 2].bitcast(F32))


def tile_done(g, k):
    return 4 * g + k + 9


def tile_before(g, k):
    return 4 * g + k + 5


def tiles_two_before(g):
    return 4 * g + 4


def group_done(g):
    return g + 3


def group_two_before(g):
    return g + 1


TILE_CREDIT, GROUP_CREDIT = 8, 2


def finish_rsqrt(nc, link, y, half, var, eps):
    link(nc.vector.tensor_tensor(half, y, y, ALU.mult))
    link(nc.vector.scalar_tensor_tensor(half, var, eps, half, ALU.add, ALU.mult))
    link(nc.vector.tensor_scalar(half, half, -0.5, 1.5, ALU.mult, ALU.add))
    link(nc.vector.tensor_tensor(y, y, half, ALU.mult))


def make_norm(nc, ctx, name):
    norm = Tables()

    def sb(what, shape):
        return ctx.enter_context(nc.sbuf_tensor(f"{name}_{what}", shape, F32))

    norm.stats, norm.mv = sb("stats", [P, 2, GT, 6]), sb("mv", [P, 2, GT, 2])
    norm.root, norm.half = sb("root", [P, 2, GT]), sb("half", [P, 2, GT])
    norm.scale, norm.shift = sb("scale", [P, 2, GT]), sb("shift", [P, 2, GT])
    norm.measured, norm.pooling, norm.pooled, norm.rooted, norm.step, norm.ready = (
        nc.alloc_semaphore(f"{name}_{s}") for s in ("measured", "pooling", "pooled", "rooted", "step", "ready"))
    return norm


def norm_credit_vector(v, norm):
    v.sem_inc(norm.measured, TILE_CREDIT)
    v.sem_inc(norm.pooled, TILE_CREDIT)
    v.sem_inc(norm.ready, GROUP_CREDIT)


def norm_credit_scalar(a, norm):
    a.sem_inc(norm.rooted, GROUP_CREDIT)


def norm_statistics(nc, v, norm, x, g, par, tiles):
    for k in range(tiles):
        nc.vector.bn_stats(norm.stats[:, par, k, :], x[:, k, :]).then_inc(norm.measured, 1)
    v.wait_ge(norm.measured, tile_done(g, tiles - 1))
    v.sem_inc(norm.pooling, 1)
    for k in range(tiles):
        nc.vector.bn_aggr(norm.mv[:, par, k, :], norm.stats[:, par, k, :]).then_inc(norm.pooled, 1)


def norm_root(nc, a, norm, t, g, par, tiles):
    a.wait_ge(norm.pooled, tile_done(g, tiles - 1))
    nc.scalar.activation(norm.root[:, par, 0:tiles], norm.mv[:, par, 0:tiles, 1], ACT.Sqrt, bias=t.eps[:]).then_inc(norm.rooted, 1)


def norm_coefficients(nc, v, norm, g, par, tiles, times=None):
    y, half = norm.scale[:, par, 0:tiles], norm.half[:, par, 0:tiles]
    v.wait_ge(norm.rooted, group_done(g))
    steps = 6 if times is not None else 5
    n = [0]

    def link(ins):
        n[0] += 1
        ins.then_inc(norm.step, 1)
        v.wait_ge(norm.step, g * steps + n[0])

    link(nc.vector.reciprocal(y, norm.root[:, par, 0:tiles]))
    finish_rsqrt(nc, link, y, half, norm.mv[:, par, 0:tiles, 1], LN_EPS)
    if times is not None:
        link(nc.vector.tensor_tensor(y, y, times, ALU.mult))
    nc.vector.scalar_tensor_tensor(norm.shift[:, par, 0:tiles], norm.mv[:, par, 0:tiles, 0], -1.0, y, ALU.mult, ALU.mult).then_inc(norm.ready, 1)


def complete_segments(nc, t, q, tables, name):
    with ExitStack() as ctx:
        ctx.enter_context(nc.cleanup_on_exit())
        def sb(what, shape):
            return ctx.enter_context(nc.sbuf_tensor(f"{name}_{what}", shape, F32))

        def sem(what):
            return nc.alloc_semaphore(f"{name}_{what}")

        ends, finals = sb("ends", [ET, D]), sb("finals", [ET, D])
        psum = ctx.enter_context(nc.psum_tensor(f"{name}_ps", [ET, D], F32))
        got, fetched, added, completed, written = sem("got"), sem("fetched"), sem("added"), sem("completed"), sem("written")
        with nc.Block() as block:
            @block.sync
            def _(sp):
                sp.dma_start(ends[:], tables[0:EP, :].rearrange("(t p) d -> p t d", p=P)[P - 1]).then_inc(got, 16)

            @block.gpsimd
            def _(pl):
                nc.gpsimd.indirect_dma_start(out=finals[:], out_offset=None, in_=tables,
                                             in_offset=bass.IndirectOffsetOnAxis(ap=t.cut_rows[q][:, 0:1], axis=0)).then_inc(fetched, 16)
                pl.wait_ge(completed, 1)
                nc.gpsimd.indirect_dma_start(out=tables, out_offset=bass.IndirectOffsetOnAxis(ap=t.cut_dest[q][:, 0:1], axis=0),
                                             in_=finals[:], in_offset=None).then_inc(written, 16)
                pl.wait_ge(written, 16)

            @block.tensor
            def _(pe):
                pe.wait_ge(got, 16)
                nc.tensor.matmul(psum[:], t.cut_same[q][:], ends[:], start=True, stop=True).then_inc(added, 1)

            @block.vector
            def _(v):
                v.wait_ge(added, 1)
                v.wait_ge(fetched, 16)
                nc.vector.tensor_tensor(finals[:], finals[:], psum[:], ALU.add).then_inc(completed, 1)


def sum_segments(nc, t, rows, table, name, normed, times=None):
    q = 0
    with ExitStack() as ctx:
        ctx.enter_context(nc.cleanup_on_exit())
        def sb(what, shape, dt=F32):
            return ctx.enter_context(nc.sbuf_tensor(f"{name}_{what}", shape, dt))

        def sem(what):
            return nc.alloc_semaphore(f"{name}_{what}")

        index = sb("index", [P, 2, GT], I32)
        x = sb("x", [P, 2, GT, D])
        z = sb("z", [P, 2, GT, D]) if normed else x
        high, low = sb("high", [P, 2, GT, D], F32R), sb("low", [P, 2, GT, D], F32R)
        same = sb("same", [P, 2, GT, P], F32R)
        out = sb("out", [P, 2, GT, D])
        psum = [ctx.enter_context(nc.psum_tensor(f"{name}_ps{i}", [P, D], F32)) for i in range(8)]
        norm = make_norm(nc, ctx, name + "n") if normed else None
        indexed, sent = sem("indexed"), sem("sent")
        gathered, stored = [sem(f"gathered{p}") for p in range(2)], [sem(f"stored{p}") for p in range(2)]
        relued, halved, split, widened, summed, copied = (sem(s) for s in ("relued", "halved", "split", "widened", "summed", "copied"))
        used = relued if normed else split

        with nc.Block() as block:
            @block.gpsimd
            def _(pl):
                def fetch(g, par, i):
                    pl.wait_ge(used, tiles_two_before(g))
                    nc.gpsimd.tensor_copy(index[:, par, :], t.other[q][:, DS(g * GT, GT)]).then_inc(indexed, 1)
                    pl.wait_ge(indexed, g + 1)
                    pl.sem_inc(sent, 1)
                    for k in range(GT):
                        nc.gpsimd.indirect_dma_start(out=x[:, par, k, :], out_offset=None, in_=rows,
                                                     in_offset=bass.IndirectOffsetOnAxis(ap=index[:, par, k:k + 1], axis=0)).then_inc(gathered[par], 16)

                edge_groups(pl, fetch, lambda g, par, i, nxt: nxt and fetch(*nxt))

            @block.vector
            def _(v):
                v.sem_inc(halved, TILE_CREDIT)
                v.sem_inc(split, TILE_CREDIT)
                if normed:
                    norm_credit_vector(v, norm)

                def message(g, par, i):
                    v.wait_ge(gathered[par], 64 * (i + 1))
                    if normed:
                        norm_statistics(nc, v, norm, x[:, par], g, par, GT)
                        norm_coefficients(nc, v, norm, g, par, GT, times[:, DS(g * GT, GT)] if times is not None else None)
                    v.wait_ge(summed, tiles_two_before(g))
                    for k in range(GT):
                        if normed:
                            v.wait_ge(relued, tile_done(g, k))
                        nc.vector.tensor_copy(high[:, par, k, :], z[:, par, k, :]).then_inc(halved, 1)
                    for k in range(GT):
                        v.wait_ge(halved, tile_done(g, k))
                        nc.vector.tensor_tensor(low[:, par, k, :], z[:, par, k, :], high[:, par, k, :].bitcast(F32), ALU.subtract).then_inc(split, 1)

                edge_groups(v, message, lambda g, par, i, nxt: nxt and message(*nxt))

            @block.scalar
            def _(a):
                a.sem_inc(copied, TILE_CREDIT)
                a.sem_inc(widened, GROUP_CREDIT)
                if normed:
                    norm_credit_scalar(a, norm)
                    a.sem_inc(relued, TILE_CREDIT)

                def prepare(g, par, i):
                    a.wait_ge(summed, tiles_two_before(g))
                    nc.scalar.copy(same[:, par], t.same[q][:, DS(g * GT, GT), :]).then_inc(widened, 1)
                    if normed:
                        norm_root(nc, a, norm, t, g, par, GT)
                        a.wait_ge(norm.ready, group_done(g))
                        a.wait_ge(split, tiles_two_before(g))
                        for k in range(GT):
                            nc.scalar.activation(z[:, par, k, :], x[:, par, k, :], ACT.Relu, bias=norm.shift[:, par, k:k + 1],
                                                 scale=norm.scale[:, par, k:k + 1]).then_inc(relued, 1)

                def body(g, par, i, nxt):
                    if nxt:
                        prepare(*nxt)
                    wait_uses(a, stored[par], 16 * i)
                    for k in range(GT):
                        a.wait_ge(summed, tile_done(g, k))
                        nc.scalar.copy(out[:, par, k, :], psum[4 * par + k][:]).then_inc(copied, 1)

                edge_groups(a, prepare, body)

            @block.tensor
            def _(pe):
                pe.sem_inc(summed, TILE_CREDIT)

                def body(g, par, i, nxt):
                    pe.wait_ge(widened, group_done(g))
                    pe.wait_ge(copied, tiles_two_before(g))
                    for k in range(GT):
                        pe.wait_ge(split, tile_done(g, k))
                        nc.tensor.matmul(psum[4 * par + k][:], same[:, par, k, :], low[:, par, k, :], start=True, stop=False)
                        nc.tensor.matmul(psum[4 * par + k][:], same[:, par, k, :], high[:, par, k, :], start=False, stop=True).then_inc(summed, 1)

                edge_groups(pe, nothing, body)

            @block.sync
            def _(sp):
                def store(g, par, i, nxt):
                    sp.wait_ge(copied, tile_done(g, GT - 1))
                    sp.dma_start(table[DS(g * GR, GR), :].rearrange("(k p) d -> p k d", p=P), out[:, par]).then_inc(stored[par], 16)

                edge_groups(sp, nothing, store)
                for par in range(2):
                    sp.wait_ge(stored[par], 16 * (EG // 2))
    complete_segments(nc, t, q, table, name + "c")


def load_split(nc, parts, name):
    width = max(src.shape[1] * src.shape[2] for src, _, _ in parts)
    with ExitStack() as ctx:
        ctx.enter_context(nc.cleanup_on_exit())
        raw = ctx.enter_context(nc.sbuf_tensor(f"{name}_raw", [P, len(parts), width], F32))
        loaded = nc.alloc_semaphore(f"{name}_loaded")
        halved = nc.alloc_semaphore(f"{name}_halved")
        views = [raw[:, n, 0:s.shape[1] * s.shape[2]].rearrange("p (c n) -> p c n", c=s.shape[1]) for n, (s, _, _) in enumerate(parts)]
        with nc.Block() as block:
            @block.sync
            def _(sp):
                for (src, _, _), view in zip(parts, views):
                    sp.dma_start(view, src).then_inc(loaded, 16)

            @block.vector
            def _(v):
                v.wait_ge(loaded, 16 * len(parts))
                for n, ((_, high, low), view) in enumerate(zip(parts, views)):
                    nc.vector.tensor_copy(high, view).then_inc(halved, 1)
                    v.wait_ge(halved, n + 1)
                    nc.vector.tensor_tensor(low, view, high.bitcast(F32), ALU.subtract)


def column_loads(eng, dst, vectors, sem):
    for n, vec in enumerate(vectors):
        eng.dma_start(dst[:, n, :], vec.rearrange("(c p) -> p c", p=P), allow_slow_non_contiguous=True).then_inc(sem, 16)


def gin_up(nc, t, x, eps, w1, b1, stats):
    with ExitStack() as ctx:
        ctx.enter_context(nc.cleanup_on_exit())
        def sb(what, shape, dt=F32):
            return ctx.enter_context(nc.sbuf_tensor(f"up_{what}", shape, dt))

        def sem(what):
            return nc.alloc_semaphore(f"up_{what}")

        wh, wl = sb("wh", [P, DC, H], F32R), sb("wl", [P, DC, H], F32R)
        load_split(nc, [(w1.rearrange("(c p) n -> p c n", p=P), wh[:], wl[:])], "upw")
        bias, own = sb("bias", [P, 1, HC]), sb("own", [P, 1])
        xin, agg, h = sb("x", [P, 2, GT, D]), sb("agg", [P, 2, GT, D]), sb("h", [P, 2, GT, D])
        ah, al = sb("ah", [P, 2, DC, GR], F32R), sb("al", [P, 2, DC, GR], F32R)
        y = sb("y", [P, HC, GR])
        index = sb("index", [P, 2, GT], I32)
        turn_ps = [ctx.enter_context(nc.psum_tensor(f"up_tps{i}", [P, DC, P], F32)) for i in range(4)]
        y_ps = [ctx.enter_context(nc.psum_tensor(f"up_yps{i}", [P, GR], F32)) for i in range(4)]
        norm = make_norm(nc, ctx, "upn")
        consts, own_ready, indexed, sent = sem("consts"), sem("own_ready"), sem("indexed"), sem("sent")
        loaded, gathered = [sem(f"loaded{p}") for p in range(2)], [sem(f"gathered{p}") for p in range(2)]
        stored = [sem(f"stored{p}") for p in range(2)]
        relued, combined, turned, halved, split = (sem(s) for s in ("relued", "combined", "turned", "halved", "split"))
        produced, biased, measured = sem("produced"), sem("biased"), sem("measured")
        HALF = HC // 2

        with nc.Block() as block:
            @block.sync
            def _(sp):
                column_loads(sp, bias[:], [b1], consts)
                sp.dma_start(own[:], eps.to_broadcast([P, 1])).then_inc(consts, 16)

                def load(g, par, i, tail):
                    sp.wait_ge(relued, tiles_two_before(g))
                    load_group(sp, xin[:, par], x, g, tail, loaded[par])

                node_groups(sp, load, lambda g, par, i, tail, nxt: nxt and load(*nxt))

            @block.gpsimd
            def _(pl):
                def fetch(g, par, i, tail):
                    pl.wait_ge(turned, tiles_two_before(g))
                    tiles = tiles_of(tail)
                    nc.gpsimd.tensor_copy(index[:, par, 0:tiles], t.last[0][:, DS(g * GT, tiles)]).then_inc(indexed, 1)
                    pl.wait_ge(indexed, g + 1)
                    pl.sem_inc(sent, 1)
                    for k in range(tiles):
                        nc.gpsimd.indirect_dma_start(out=agg[:, par, k, :], out_offset=None, in_=t.seg_in,
                                                     in_offset=bass.IndirectOffsetOnAxis(ap=index[:, par, k:k + 1], axis=0)).then_inc(gathered[par], 16)

                node_groups(pl, fetch, lambda g, par, i, tail, nxt: nxt and fetch(*nxt))

            @block.vector
            def _(v):
                v.sem_inc(combined, TILE_CREDIT)
                v.sem_inc(split, TILE_CREDIT)
                v.sem_inc(measured, HC)
                norm_credit_vector(v, norm)
                v.wait_ge(consts, 32)
                nc.vector.tensor_scalar(own[:], own[:], 1.0, None, ALU.add).then_inc(own_ready, 1)

                def combine(g, par, i, tail):
                    tiles = tiles_of(tail)
                    v.wait_ge(loaded[par], loads_done(i, tail))
                    norm_statistics(nc, v, norm, xin[:, par], g, par, tiles)
                    norm_coefficients(nc, v, norm, g, par, tiles)
                    v.wait_ge(gathered[par], 64 * i + 16 * tiles)
                    v.wait_ge(own_ready, 1)
                    for k in range(tiles):
                        v.wait_ge(relued, tile_done(g, k))
                        nc.vector.scalar_tensor_tensor(agg[:, par, k, :], h[:, par, k, :], own[:], agg[:, par, k, :], ALU.mult, ALU.add).then_inc(combined, 1)

                def lows(g, par, tail):
                    for k in range(tiles_of(tail)):
                        v.wait_ge(halved, tile_done(g, k))
                        cols = slice(k * P, (k + 1) * P)
                        nc.vector.tensor_tensor(al[:, par, :, cols], turn_ps[k][:], ah[:, par, :, cols].bitcast(F32), ALU.subtract).then_inc(split, 1)

                def measure_y(g, tail, chunks):
                    for m in chunks:
                        v.wait_ge(biased, HC * g + m + 5)
                        nc.vector.bn_stats(stats[:, m, DS(g, 1), :].rearrange("p o s -> p (o s)"), y[:, m, 0:(TAIL if tail else GR)]).then_inc(measured, 1)

                def start(g, par, i, tail):
                    combine(g, par, i, tail)
                    lows(g, par, tail)

                def body(g, par, i, tail, nxt):
                    if nxt:
                        combine(*nxt)
                    measure_y(g, tail, range(HALF))
                    if nxt:
                        lows(nxt[0], nxt[1], nxt[3])
                    measure_y(g, tail, range(HALF, HC))

                node_groups(v, start, body)

            @block.scalar
            def _(a):
                norm_credit_scalar(a, norm)
                a.sem_inc(relued, TILE_CREDIT)
                a.sem_inc(halved, TILE_CREDIT)
                a.sem_inc(biased, 4)
                a.wait_ge(consts, 32)

                def apply(g, par, i, tail):
                    norm_root(nc, a, norm, t, g, par, tiles_of(tail))
                    a.wait_ge(norm.ready, group_done(g))
                    a.wait_ge(combined, tiles_two_before(g))
                    for k in range(tiles_of(tail)):
                        nc.scalar.activation(h[:, par, k, :], xin[:, par, k, :], ACT.Relu, bias=norm.shift[:, par, k:k + 1],
                                             scale=norm.scale[:, par, k:k + 1]).then_inc(relued, 1)

                def highs(g, par, tail):
                    a.wait_ge(produced, HC * g + 4)
                    for k in range(tiles_of(tail)):
                        a.wait_ge(turned, tile_done(g, k))
                        nc.scalar.copy(ah[:, par, :, k * P:(k + 1) * P], turn_ps[k][:]).then_inc(halved, 1)

                def finish(g, i, tail, half):
                    cols = TAIL if tail else GR
                    wait_uses(a, stored[half], 16 * g)
                    for m in range(half * HALF, (half + 1) * HALF):
                        a.wait_ge(produced, HC * g + m + HC + 5)
                        a.wait_ge(measured, HC * g + m + 1)
                        nc.scalar.activation(y[:, m, 0:cols], y_ps[m % 4][:, 0:cols], ACT.Identity, bias=bias[:, 0, m:m + 1]).then_inc(biased, 1)
                    a.wait_ge(biased, HC * g + (half + 1) * HALF + 4)
                    a.dma_start(t.y1[DS(g, 1), :, half * HALF:(half + 1) * HALF, 0:cols].rearrange("o p c n -> p (o c) n"),
                                y[:, half * HALF:(half + 1) * HALF, 0:cols]).then_inc(stored[half], 16)

                def start(g, par, i, tail):
                    apply(g, par, i, tail)
                    highs(g, par, tail)

                def body(g, par, i, tail, nxt):
                    if nxt:
                        apply(*nxt)
                    finish(g, i, tail, 0)
                    if nxt:
                        highs(nxt[0], nxt[1], nxt[3])
                    finish(g, i, tail, 1)

                node_groups(a, start, body)
                for half in range(2):
                    a.wait_ge(stored[half], 16 * NG)

            @block.tensor
            def _(pe):
                pe.sem_inc(turned, TILE_CREDIT)
                pe.sem_inc(produced, HC + 4)

                def turn(g, par, i, tail):
                    for k in range(tiles_of(tail)):
                        pe.wait_ge(combined, tile_done(g, k))
                        pe.wait_ge(split, tile_before(g, k))
                        for c in range(DC):
                            mm = nc.tensor.transpose(turn_ps[k][:, c, :], agg[:, par, k, c * P:(c + 1) * P], t.ident[:])
                        mm.then_inc(turned, 1)

                def product(g, par, tail, chunks):
                    cols = TAIL if tail else GR
                    for m in chunks:
                        pe.wait_ge(biased, HC * g + m + 1)
                        for c in range(DC):
                            mm = product3(nc, y_ps[m % 4][:, 0:cols], wh[:, c, m * P:(m + 1) * P], wl[:, c, m * P:(m + 1) * P],
                                          ah[:, par, c, 0:cols], al[:, par, c, 0:cols], c == 0, c == DC - 1)
                        mm.then_inc(produced, 1)

                def body(g, par, i, tail, nxt):
                    pe.wait_ge(split, tile_done(g, tiles_of(tail) - 1))
                    product(g, par, tail, range(HALF))
                    if nxt:
                        turn(*nxt)
                    product(g, par, tail, range(HALF, HC))

                node_groups(pe, turn, body)


def batch_norm_coefficients(nc, t, stats, gamma, beta, coef, chunks, name):
    with ExitStack() as ctx:
        ctx.enter_context(nc.cleanup_on_exit())
        def sb(what, shape):
            return ctx.enter_context(nc.sbuf_tensor(f"{name}_{what}", shape, F32))

        def sem(what):
            return nc.alloc_semaphore(f"{name}_{what}")

        gb, mv = sb("gb", [P, 2, chunks]), sb("mv", [P, chunks, 2])
        root, half = sb("root", [P, chunks]), sb("half", [P, chunks])
        loaded, step, rooted = sem("loaded"), sem("step"), sem("rooted")
        with nc.Block() as block:
            @block.sync
            def _(sp):
                column_loads(sp, gb[:], [gamma, beta], loaded)

            @block.scalar
            def _(a):
                a.wait_ge(step, chunks)
                nc.scalar.activation(root[:], mv[:, :, 1], ACT.Sqrt, bias=t.eps[:]).then_inc(rooted, 1)

            @block.vector
            def _(v):
                n = [0]

                def link(ins):
                    n[0] += 1
                    ins.then_inc(step, 1)
                    v.wait_ge(step, n[0])

                for m in range(chunks):
                    link(nc.vector.bn_aggr(mv[:, m, :], stats[:, m].rearrange("p g s -> p (g s)")))
                v.wait_ge(rooted, 1)
                v.wait_ge(loaded, 32)
                link(nc.vector.reciprocal(root[:], root[:]))
                finish_rsqrt(nc, link, root[:], half[:], mv[:, :, 1], LN_EPS)
                link(nc.vector.tensor_tensor(coef[:, 0, :], gb[:, 0, :], root[:], ALU.mult))
                link(nc.vector.tensor_tensor(half[:], mv[:, :, 0], coef[:, 0, :], ALU.mult))
                link(nc.vector.tensor_tensor(coef[:, 1, :], gb[:, 1, :], half[:], ALU.subtract))


def gin_down(nc, t, w2, b2, coef, stats):
    with ExitStack() as ctx:
        ctx.enter_context(nc.cleanup_on_exit())
        def sb(what, shape, dt=F32):
            return ctx.enter_context(nc.sbuf_tensor(f"down_{what}", shape, dt))

        def sem(what):
            return nc.alloc_semaphore(f"down_{what}")

        wh, wl = sb("wh", [P, HC, D], F32R), sb("wl", [P, HC, D], F32R)
        load_split(nc, [(w2.rearrange("(c p) n -> p c n", p=P), wh[:], wl[:])], "downw")
        bias = sb("bias", [P, 1, DC])
        z = sb("z", [P, 2, HC, GR])
        zh, zl = sb("zh", [P, HC, GR], F32R), sb("zl", [P, HC, GR], F32R)
        y = sb("y", [P, 2, DC, GR])
        psum = [ctx.enter_context(nc.psum_tensor(f"down_ps{i}", [P, GR], F32)) for i in range(8)]
        consts = sem("consts")
        loaded, stored = [sem(f"loaded{p}") for p in range(2)], [sem(f"stored{p}") for p in range(2)]
        relued, halved, split, used = sem("relued"), sem("halved"), sem("split"), sem("used")
        produced, biased, measured = sem("produced"), sem("biased"), sem("measured")

        with nc.Block() as block:
            @block.sync
            def _(sp):
                column_loads(sp, bias[:], [b2], consts)

                def load(g, par, i, tail):
                    cols = TAIL if tail else GR
                    sp.wait_ge(split, HC * g + HC)
                    sp.dma_start(z[:, par, :, 0:cols], t.y1[DS(g, 1), :, :, 0:cols].rearrange("o p c n -> p (o c) n")).then_inc(loaded[par], 16)

                node_groups(sp, load, lambda g, par, i, tail, nxt: nxt and load(*nxt))

            @block.scalar
            def _(a):
                a.sem_inc(relued, HC)
                a.sem_inc(biased, TILE_CREDIT)
                a.wait_ge(consts, 16)

                def apply(g, par, i, tail):
                    cols = TAIL if tail else GR
                    a.wait_ge(loaded[par], 16 * (i + 1))
                    for m in range(HC):
                        nc.scalar.activation(z[:, par, m, 0:cols], z[:, par, m, 0:cols], ACT.Relu, bias=coef[:, 1, m:m + 1],
                                             scale=coef[:, 0, m:m + 1]).then_inc(relued, 1)

                def body(g, par, i, tail, nxt):
                    cols = TAIL if tail else GR
                    if nxt:
                        apply(*nxt)
                    wait_uses(a, stored[par], 16 * i)
                    a.wait_ge(measured, tiles_two_before(g))
                    for m in range(DC):
                        a.wait_ge(produced, tile_done(g, m))
                        nc.scalar.activation(y[:, par, m, 0:cols], psum[4 * par + m][:, 0:cols], ACT.Identity, bias=bias[:, 0, m:m + 1]).then_inc(biased, 1)
                    a.wait_ge(biased, tile_done(g, DC - 1))
                    a.dma_start(t.y2[DS(g, 1), :, :, 0:cols].rearrange("o p c n -> p (o c) n"), y[:, par, :, 0:cols]).then_inc(stored[par], 16)

                node_groups(a, apply, body)
                for par in range(2):
                    a.wait_ge(stored[par], 16 * (NG // 2))

            @block.vector
            def _(v):
                v.sem_inc(halved, HC)
                v.sem_inc(split, 2 * HC)
                v.sem_inc(measured, TILE_CREDIT)

                def halve(g, par, i, tail):
                    cols = TAIL if tail else GR
                    for m in range(HC):
                        v.wait_ge(relued, HC * g + m + HC + 1)
                        if m < HC - 1:
                            v.wait_ge(used, (HC - 1) * g + m + 1)
                        else:
                            v.wait_ge(produced, tile_before(g, DC - 1))
                        nc.vector.tensor_copy(zh[:, m, 0:cols], z[:, par, m, 0:cols]).then_inc(halved, 1)
                        if m > 0:
                            lower(g, par, m - 1, cols)
                    lower(g, par, HC - 1, cols)

                def lower(g, par, m, cols):
                    v.wait_ge(halved, HC * g + m + HC + 1)
                    nc.vector.tensor_tensor(zl[:, m, 0:cols], z[:, par, m, 0:cols], zh[:, m, 0:cols].bitcast(F32), ALU.subtract).then_inc(split, 1)

                def body(g, par, i, tail, nxt):
                    if nxt:
                        halve(*nxt)
                    for m in range(DC):
                        v.wait_ge(biased, tile_done(g, m))
                        nc.vector.bn_stats(stats[:, m, DS(g, 1), :].rearrange("p o s -> p (o s)"), y[:, par, m, 0:(TAIL if tail else GR)]).then_inc(measured, 1)

                node_groups(v, halve, body)

            @block.tensor
            def _(pe):
                pe.sem_inc(used, HC - 1)
                pe.sem_inc(produced, TILE_CREDIT)

                def body(g, par, i, tail, nxt):
                    cols = TAIL if tail else GR
                    pe.wait_ge(biased, tiles_two_before(g))
                    for c in range(HC):
                        pe.wait_ge(split, HC * g + c + 2 * HC + 1)
                        for m in range(DC):
                            mm = product3(nc, psum[4 * par + m][:, 0:cols], wh[:, c, m * P:(m + 1) * P], wl[:, c, m * P:(m + 1) * P],
                                          zh[:, c, 0:cols], zl[:, c, 0:cols], c == 0, c == HC - 1)
                            if c == HC - 1:
                                mm.then_inc(produced, 1)
                            elif m == DC - 1:
                                mm.then_inc(used, 1)

                node_groups(pe, nothing, body)


def gin_out(nc, t, x, coef):
    with ExitStack() as ctx:
        ctx.enter_context(nc.cleanup_on_exit())
        def sb(what, shape, dt=F32):
            return ctx.enter_context(nc.sbuf_tensor(f"out_{what}", shape, dt))

        def sem(what):
            return nc.alloc_semaphore(f"out_{what}")

        xin, h, u = sb("x", [P, 2, GT, D]), sb("h", [P, 2, GT, D]), sb("u", [P, 2, DC, GR])
        out = sb("out", [P, 2, GT, D])
        psum = [ctx.enter_context(nc.psum_tensor(f"out_ps{i}", [P, DC, P], F32)) for i in range(8)]
        norm = make_norm(nc, ctx, "outn")
        loaded, stored = [sem(f"loaded{p}") for p in range(2)], [sem(f"stored{p}") for p in range(2)]
        u_loaded = [sem(f"u_loaded{p}") for p in range(2)]
        activated, relued, turned, added, finished = (sem(s) for s in ("activated", "relued", "turned", "added", "finished"))

        with nc.Block() as block:
            @block.sync
            def _(sp):
                def load(g, par, i, tail):
                    cols = TAIL if tail else GR
                    sp.wait_ge(finished, tiles_two_before(g))
                    load_group(sp, xin[:, par], x, g, tail, loaded[par])
                    sp.wait_ge(turned, tiles_two_before(g))
                    sp.dma_start(u[:, par, :, 0:cols], t.y2[DS(g, 1), :, :, 0:cols].rearrange("o p c n -> p (o c) n")).then_inc(u_loaded[par], 16)

                node_groups(sp, load, lambda g, par, i, tail, nxt: nxt and load(*nxt))

            @block.scalar
            def _(a):
                norm_credit_scalar(a, norm)
                a.sem_inc(activated, TILE_CREDIT)
                a.sem_inc(relued, TILE_CREDIT)

                def apply(g, par, i, tail):
                    cols = TAIL if tail else GR
                    a.wait_ge(u_loaded[par], 16 * (i + 1))
                    for c in range(DC):
                        nc.scalar.activation(u[:, par, c, 0:cols], u[:, par, c, 0:cols], ACT.Relu, bias=coef[:, 1, c:c + 1],
                                             scale=coef[:, 0, c:c + 1]).then_inc(activated, 1)
                    norm_root(nc, a, norm, t, g, par, tiles_of(tail))
                    a.wait_ge(norm.ready, group_done(g))
                    a.wait_ge(added, tiles_two_before(g))
                    for k in range(tiles_of(tail)):
                        nc.scalar.activation(h[:, par, k, :], xin[:, par, k, :], ACT.Relu, bias=norm.shift[:, par, k:k + 1],
                                             scale=norm.scale[:, par, k:k + 1]).then_inc(relued, 1)

                def body(g, par, i, tail, nxt):
                    if nxt:
                        apply(*nxt)
                    a.wait_ge(finished, tile_done(g, tiles_of(tail) - 1))
                    store_group(a, t.x1, out[:, par], g, tail, stored[par])

                node_groups(a, apply, body)
                a.wait_ge(stored[0], 16 * (NG // 2))
                a.wait_ge(stored[1], 16 * (NG // 2 + 1))

            @block.tensor
            def _(pe):
                pe.sem_inc(turned, TILE_CREDIT)

                def body(g, par, i, tail, nxt):
                    pe.wait_ge(activated, tile_done(g, DC - 1))
                    pe.wait_ge(added, tiles_two_before(g))
                    for k in range(tiles_of(tail)):
                        for c in range(DC):
                            mm = nc.tensor.transpose(psum[4 * par + k][:, c, :], u[:, par, c, k * P:(k + 1) * P], t.ident[:])
                        mm.then_inc(turned, 1)

                node_groups(pe, nothing, body)

            @block.vector
            def _(v):
                norm_credit_vector(v, norm)
                v.sem_inc(added, TILE_CREDIT)
                v.sem_inc(finished, TILE_CREDIT)

                def measure(g, par, i, tail):
                    v.wait_ge(loaded[par], loads_done(i, tail))
                    norm_statistics(nc, v, norm, xin[:, par], g, par, tiles_of(tail))
                    norm_coefficients(nc, v, norm, g, par, tiles_of(tail))

                def body(g, par, i, tail, nxt):
                    if nxt:
                        measure(*nxt)
                    tiles = tiles_of(tail)
                    wait_uses(v, stored[par], 16 * i)
                    for k in range(tiles):
                        v.wait_ge(turned, tile_done(g, k))
                        v.wait_ge(relued, tile_done(g, k))
                        nc.vector.tensor_tensor(h[:, par, k, :], h[:, par, k, :], psum[4 * par + k][:].rearrange("p c n -> p (c n)"), ALU.add).then_inc(added, 1)
                    for k in range(tiles):
                        v.wait_ge(added, tile_done(g, k))
                        nc.vector.tensor_tensor(out[:, par, k, :], xin[:, par, k, :], h[:, par, k, :], ALU.add).then_inc(finished, 1)

                node_groups(v, measure, body)


def row_broadcast(eng, dst, vec, sem):
    eng.dma_start(dst, vec.rearrange("(o d) -> o d", o=1).to_broadcast([P, vec.shape[0]])).then_inc(sem, 16)


def gcn(nc, t, layer, rows, w, b, out_rows, residual=None):
    normed = layer == 0
    name = f"gcn{layer}"
    with ExitStack() as ctx:
        ctx.enter_context(nc.cleanup_on_exit())
        def sb(what, shape, dt=F32):
            return ctx.enter_context(nc.sbuf_tensor(f"{name}_{what}", shape, dt))

        def sem(what):
            return nc.alloc_semaphore(f"{name}_{what}")

        wh, wl = sb("wh", [P, DC, D], F32R), sb("wl", [P, DC, D], F32R)
        load_split(nc, [(w.rearrange("(c p) n -> p c n", p=P), wh[:], wl[:])], name + "w")
        bias = sb("bias", [P, D])
        xin, agg = sb("x", [P, 2, GT, D]), sb("agg", [P, 2, GT, D])
        s = sb("s", [P, 2, GT, D]) if normed else xin
        res = sb("res", [P, 2, GT, D]) if residual is not None else None
        ah, al = sb("ah", [P, GT, DC, P], F32R), sb("al", [P, GT, DC, P], F32R)
        tmp, out = sb("tmp", [P, GT, D]), sb("out", [P, 2, GT, D])
        index = sb("index", [P, 2, GT], I32)
        turn_ps = [ctx.enter_context(nc.psum_tensor(f"{name}_tps{i}", [P, DC, P], F32)) for i in range(4)]
        row_ps = [ctx.enter_context(nc.psum_tensor(f"{name}_rps{i}", [P, D], F32)) for i in range(4)]
        norm = make_norm(nc, ctx, name + "n") if normed else None
        consts, indexed, sent = sem("consts"), sem("indexed"), sem("sent")
        loaded, gathered = [sem(f"loaded{p}") for p in range(2)], [sem(f"gathered{p}") for p in range(2)]
        res_loaded, stored = [sem(f"res_loaded{p}") for p in range(2)], [sem(f"stored{p}") for p in range(2)]
        relued, combined, turned, halved, split = (sem(n) for n in ("relued", "combined", "turned", "halved", "split"))
        produced, scaled, finished = sem("produced"), sem("scaled"), sem("finished")
        used = relued if normed else combined

        with nc.Block() as block:
            @block.sync
            def _(sp):
                row_broadcast(sp, bias[:], b, consts)

                def load(g, par, i, tail):
                    sp.wait_ge(used, tiles_two_before(g))
                    load_group(sp, xin[:, par], rows, g, tail, loaded[par])
                    if residual is not None:
                        sp.wait_ge(finished, tiles_two_before(g))
                        load_group(sp, res[:, par], residual, g, tail, res_loaded[par])

                node_groups(sp, load, lambda g, par, i, tail, nxt: nxt and load(*nxt))

            @block.gpsimd
            def _(pl):
                def fetch(g, par, i, tail):
                    tiles = tiles_of(tail)
                    pl.wait_ge(turned, tiles_two_before(g))
                    nc.gpsimd.tensor_copy(index[:, par, 0:tiles], t.last[0][:, DS(g * GT, tiles)]).then_inc(indexed, 1)
                    pl.wait_ge(indexed, g + 1)
                    pl.sem_inc(sent, 1)
                    for k in range(tiles):
                        nc.gpsimd.indirect_dma_start(out=agg[:, par, k, :], out_offset=None, in_=t.seg_in,
                                                     in_offset=bass.IndirectOffsetOnAxis(ap=index[:, par, k:k + 1], axis=0)).then_inc(gathered[par], 16)

                node_groups(pl, fetch, lambda g, par, i, tail, nxt: nxt and fetch(*nxt))

            @block.vector
            def _(v):
                v.sem_inc(combined, TILE_CREDIT)
                v.sem_inc(split, TILE_CREDIT)
                v.sem_inc(scaled, TILE_CREDIT)
                if normed:
                    norm_credit_vector(v, norm)
                else:
                    v.sem_inc(finished, TILE_CREDIT)
                v.wait_ge(consts, 16)

                def combine(g, par, i, tail):
                    tiles = tiles_of(tail)
                    v.wait_ge(loaded[par], loads_done(i, tail))
                    if normed:
                        norm_statistics(nc, v, norm, xin[:, par], g, par, tiles)
                        norm_coefficients(nc, v, norm, g, par, tiles, t.dis[:, DS(g * GT, tiles)])
                    v.wait_ge(gathered[par], 64 * i + 16 * tiles)
                    for k in range(tiles):
                        if normed:
                            v.wait_ge(relued, tile_done(g, k))
                        nc.vector.tensor_tensor(agg[:, par, k, :], agg[:, par, k, :], s[:, par, k, :], ALU.add).then_inc(combined, 1)

                def lower(g, k):
                    v.wait_ge(halved, tile_done(g, k))
                    nc.vector.tensor_tensor(al[:, k], turn_ps[k][:], ah[:, k].bitcast(F32), ALU.subtract).then_inc(split, 1)

                def start(g, par, i, tail):
                    combine(g, par, i, tail)
                    for k in range(GT):
                        lower(g, k)

                def body(g, par, i, tail, nxt):
                    if nxt:
                        combine(*nxt)
                    if not normed:
                        wait_uses(v, stored[par], 16 * i)
                        v.wait_ge(res_loaded[par], loads_done(i, tail))
                    for k in range(GT):
                        if k < tiles_of(tail):
                            v.wait_ge(produced, tile_done(g, k))
                            if normed:
                                v.wait_ge(finished, tile_before(g, k))
                            nc.vector.scalar_tensor_tensor(tmp[:, k, :], row_ps[k][:], t.dis[:, DS(g * GT + k, 1)], bias[:], ALU.mult, ALU.add).then_inc(scaled, 1)
                        if nxt and k < tiles_of(nxt[3]):
                            lower(nxt[0], k)
                        if k < tiles_of(tail) and not normed:
                            v.wait_ge(scaled, tile_done(g, k))
                            nc.vector.tensor_tensor(out[:, par, k, :], tmp[:, k, :], res[:, par, k, :], ALU.add).then_inc(finished, 1)

                node_groups(v, start, body)

            @block.scalar
            def _(a):
                a.sem_inc(halved, TILE_CREDIT)
                if normed:
                    a.sem_inc(relued, TILE_CREDIT)
                    a.sem_inc(finished, TILE_CREDIT)
                    norm_credit_scalar(a, norm)

                def apply(g, par, i, tail):
                    if normed:
                        norm_root(nc, a, norm, t, g, par, tiles_of(tail))
                        a.wait_ge(norm.ready, group_done(g))
                        a.wait_ge(combined, tiles_two_before(g))
                        for k in range(tiles_of(tail)):
                            nc.scalar.activation(s[:, par, k, :], xin[:, par, k, :], ACT.Relu, bias=norm.shift[:, par, k:k + 1],
                                                 scale=norm.scale[:, par, k:k + 1]).then_inc(relued, 1)

                def higher(g, k):
                    a.wait_ge(turned, tile_done(g, k))
                    a.wait_ge(produced, tile_before(g, k))
                    nc.scalar.copy(ah[:, k], turn_ps[k][:]).then_inc(halved, 1)

                def start(g, par, i, tail):
                    apply(g, par, i, tail)
                    for k in range(GT):
                        higher(g, k)

                def body(g, par, i, tail, nxt):
                    if nxt:
                        apply(*nxt)
                    if normed:
                        wait_uses(a, stored[par], 16 * i)
                    for k in range(GT):
                        if nxt and k < tiles_of(nxt[3]):
                            higher(nxt[0], k)
                        if normed and k < tiles_of(tail):
                            a.wait_ge(scaled, tile_done(g, k))
                            nc.scalar.activation(out[:, par, k, :], tmp[:, k, :], ACT.Relu, scale=t.dis[:, DS(g * GT + k, 1)]).then_inc(finished, 1)
                    a.wait_ge(finished, tile_done(g, tiles_of(tail) - 1))
                    store_group(a, out_rows, out[:, par], g, tail, stored[par])

                node_groups(a, start, body)
                a.wait_ge(stored[0], 16 * (NG // 2))
                a.wait_ge(stored[1], 16 * (NG // 2 + 1))

            @block.tensor
            def _(pe):
                pe.sem_inc(turned, TILE_CREDIT)
                pe.sem_inc(produced, TILE_CREDIT)

                def turn(g, par, k):
                    pe.wait_ge(combined, tile_done(g, k))
                    pe.wait_ge(split, tile_before(g, k))
                    for c in range(DC):
                        mm = nc.tensor.transpose(turn_ps[k][:, c, :], agg[:, par, k, c * P:(c + 1) * P], t.ident[:])
                    mm.then_inc(turned, 1)

                def start(g, par, i, tail):
                    for k in range(GT):
                        turn(g, par, k)

                def body(g, par, i, tail, nxt):
                    for k in range(GT):
                        if k < tiles_of(tail):
                            pe.wait_ge(split, tile_done(g, k))
                            pe.wait_ge(scaled, tile_before(g, k))
                            for c in range(DC):
                                mm = product3(nc, row_ps[k][:], ah[:, k, c, :], al[:, k, c, :], wh[:, c, :], wl[:, c, :], c == 0, c == DC - 1)
                            mm.then_inc(produced, 1)
                        if nxt and k < tiles_of(nxt[3]):
                            turn(nxt[0], nxt[1], k)

                node_groups(pe, start, body)


BT = ET // 2
BG = BT // GT


def path_products(nc, t, rows, edge_attr, paths, coeffs):
    with ExitStack() as ctx:
        ctx.enter_context(nc.cleanup_on_exit())

        def sb(what, shape, dt=F32):
            return ctx.enter_context(nc.sbuf_tensor(f"path_{what}", shape, dt))

        def sem(what):
            return nc.alloc_semaphore(f"path_{what}")

        h, attr, o = sb("h", [P, BT, D]), sb("attr", [P, BT, D]), sb("o", [P, BT, D])
        term = sb("term", [P, 4, BT, EXT])
        high, low = sb("high", [P, GT, D], F32R), sb("low", [P, GT, D], F32R)
        same = sb("same", [P, GT, P], F32R)
        out = sb("out", [P, GT, D])
        coef, ids, code = sb("coef", [P, PATHS]), sb("ids", [1, PATHS, 3], I32), sb("code", [1, PATHS], I32)
        code_f = sb("code_f", [1, 2, PATHS])
        psum = [ctx.enter_context(nc.psum_tensor(f"path_ps{i}", [P, D], F32)) for i in range(4)]
        norm = make_norm(nc, ctx, "pathn")
        consts, coded, coded_step = sem("consts"), sem("coded"), sem("coded_step")
        gathered, stored = [sem(f"gathered{b}") for b in range(BG)], sem("stored")
        relued, cleared, multiplied, accumulated = sem("relued"), sem("cleared"), sem("multiplied"), sem("accumulated")
        halved, split, widened, summed, copied = (sem(s) for s in ("halved", "split", "widened", "summed", "copied"))
        ALL = 2 * BG

        with nc.Block() as block:
            @block.sync
            def _(sp):
                sp.dma_start(coef[:], coeffs.rearrange("(o d) -> o d", o=1).to_broadcast([P, PATHS])).then_inc(consts, 16)
                sp.dma_start(ids[:].rearrange("o a b -> o (a b)"), paths.rearrange("(o a) b -> o (a b)", o=1)).then_inc(consts, 16)
                for g in range(ALL):
                    sp.wait_ge(copied, GT * (g + 1))
                    sp.dma_start(t.seg_in[g * GR:(g + 1) * GR, :].rearrange("(k p) d -> p k d", p=P), out[:]).then_inc(stored, 16)
                sp.wait_ge(stored, 16 * ALL)

            @block.gpsimd
            def _(pl):
                for batch in range(2):
                    if batch:
                        pl.wait_ge(accumulated, PATHS + 4)
                    for b in range(BG):
                        for k in range(b * GT, (b + 1) * GT):
                            col = batch * BT + k
                            nc.gpsimd.indirect_dma_start(out=h[:, k, :], out_offset=None, in_=rows,
                                                         in_offset=bass.IndirectOffsetOnAxis(ap=t.other[0][:, col:col + 1], axis=0)).then_inc(gathered[b], 16)
                            nc.gpsimd.indirect_dma_start(out=attr[:, k, :], out_offset=None, in_=edge_attr,
                                                         in_offset=bass.IndirectOffsetOnAxis(ap=t.eid[0][:, col:col + 1], axis=0)).then_inc(gathered[b], 16)
                    if batch:
                        pl.wait_ge(split, BT)
                    nc.gpsimd.memset(o[:], 0.0).then_inc(cleared, 1)

            @block.vector
            def _(v):
                norm_credit_vector(v, norm)
                v.sem_inc(accumulated, 4)
                v.wait_ge(consts, 32)
                nc.vector.tensor_scalar(code_f[:, 0], ids[:, :, 2], float(SEG), None, ALU.mult).then_inc(coded_step, 1)
                v.wait_ge(coded_step, 1)
                nc.vector.tensor_tensor(code_f[:, 1], code_f[:, 0], ids[:, :, 1], ALU.add).then_inc(coded_step, 1)
                v.wait_ge(coded_step, 2)
                nc.vector.tensor_scalar(code_f[:, 0], code_f[:, 1], float(SEG), None, ALU.mult).then_inc(coded_step, 1)
                v.wait_ge(coded_step, 3)
                nc.vector.tensor_tensor(code[:], code_f[:, 0], ids[:, :, 0], ALU.add).then_inc(coded_step, 1)
                v.wait_ge(coded_step, 4)
                hv, av, ov = (x[:].rearrange("p t (s k) -> p t s k", k=EXT) for x in (h, attr, o))
                for batch in range(2):
                    for b in range(BG):
                        g = batch * BG + b
                        v.wait_ge(gathered[b], 2 * GT * 16 * (batch + 1))
                        norm_statistics(nc, v, norm, h[:, b * GT:(b + 1) * GT], g, g % 2, GT)
                        norm_coefficients(nc, v, norm, g, g % 2, GT)
                    v.wait_ge(relued, BT * (batch + 1))
                    v.wait_ge(cleared, batch + 1)
                    with v.Fori(0, PATHS // 4) as i:
                        third = []
                        for j in range(4):
                            word = v.value_load(code[0:1, DS(4 * i + j, 1)], min_val=0, max_val=SEG ** 3 - 1)
                            first, second = word % SEG, (word // SEG) % SEG
                            third.append(word // SEG ** 2)
                            v.wait_ge(accumulated, PATHS * batch + 4 * i + 4)
                            nc.vector.scalar_tensor_tensor(term[:, j], hv[:, :, DS(first, 1), :].rearrange("p t o k -> p t (o k)"), coef[:, DS(4 * i + j, 1)],
                                                           av[:, :, DS(second, 1), :].rearrange("p t o k -> p t (o k)"), ALU.mult, ALU.mult).then_inc(multiplied, 1)
                        for j in range(4):
                            v.wait_ge(multiplied, PATHS * batch + 4 * i + j + 1)
                            v.wait_ge(accumulated, PATHS * batch + 4 * i + j + 4)
                            there = ov[:, :, DS(third[j], 1), :].rearrange("p t o k -> p t (o k)")
                            nc.vector.tensor_tensor(there, there, term[:, j], ALU.add).then_inc(accumulated, 1)
                    for b in range(BG):
                        g = batch * BG + b
                        for k in range(GT):
                            n = GT * g + k + 1
                            v.wait_ge(halved, n)
                            nc.vector.tensor_tensor(low[:, k, :], o[:, b * GT + k, :], high[:, k, :].bitcast(F32), ALU.subtract).then_inc(split, 1)

            @block.scalar
            def _(a):
                norm_credit_scalar(a, norm)
                for batch in range(2):
                    for b in range(BG):
                        g = batch * BG + b
                        norm_root(nc, a, norm, t, g, g % 2, GT)
                        a.wait_ge(norm.ready, group_done(g))
                        for k in range(GT):
                            n = b * GT + k
                            nc.scalar.activation(h[:, n, :], h[:, n, :], ACT.Relu, bias=norm.shift[:, g % 2, k:k + 1],
                                                 scale=norm.scale[:, g % 2, k:k + 1]).then_inc(relued, 1)
                    a.wait_ge(accumulated, PATHS * (batch + 1) + 4)
                    for b in range(BG):
                        g = batch * BG + b
                        if g:
                            a.wait_ge(summed, GT * g)
                        nc.scalar.copy(same[:], t.same[0][:, g * GT:(g + 1) * GT, :]).then_inc(widened, 1)
                        for k in range(GT):
                            nc.scalar.copy(high[:, k, :], o[:, b * GT + k, :]).then_inc(halved, 1)
                        if g:
                            wait_uses(a, stored, 16 * g)
                        for k in range(GT):
                            a.wait_ge(summed, GT * g + k + 1)
                            nc.scalar.copy(out[:, k, :], psum[k][:]).then_inc(copied, 1)

            @block.tensor
            def _(pe):
                for g in range(ALL):
                    pe.wait_ge(widened, g + 1)
                    for k in range(GT):
                        n = GT * g + k + 1
                        pe.wait_ge(split, n)
                        if g:
                            pe.wait_ge(copied, n - GT)
                        nc.tensor.matmul(psum[k][:], same[:, k, :], low[:, k, :], start=True, stop=False)
                        nc.tensor.matmul(psum[k][:], same[:, k, :], high[:, k, :], start=False, stop=True).then_inc(summed, 1)
    complete_segments(nc, t, 0, t.seg_in, "pathc")


def fold_weights(nc, t, wo_w, wi_w, ws_w, mlp_w, wo_b, wi_b, ws_b, mlp_b, folded, const_row):
    with ExitStack() as ctx:
        ctx.enter_context(nc.cleanup_on_exit())

        def sb(what, shape, dt=F32):
            return ctx.enter_context(nc.sbuf_tensor(f"fold_{what}", shape, dt))

        def sem(what):
            return nc.alloc_semaphore(f"fold_{what}")

        mlp, mlp_t = sb("mlp", [P, DC, 2 * D]), sb("mlp_t", [P, 2 * DC, D])
        w = sb("w", [P, 3, DC, D])
        bcol, bsum, wide = sb("bcol", [P, 3, DC]), sb("bsum", [P, 2, DC]), sb("wide", [P, 2 * DC, P])
        brow = sb("brow", [P, D])
        psum = [ctx.enter_context(nc.psum_tensor(f"fold_ps{i}", [P, D], F32)) for i in range(8)]
        loaded, turned, copied, produced, halved, split = (sem(s) for s in ("loaded", "turned", "copied", "produced", "halved", "split"))
        step, constant = sem("step"), sem("constant")
        order = [(n, c) for n in range(3) for c in range(DC)]

        with nc.Block() as block:
            @block.sync
            def _(sp):
                sp.dma_start(mlp[:], mlp_w.rearrange("(c p) n -> p c n", p=P)).then_inc(loaded, 16)
                for n, x in enumerate((ws_w, wo_w, wi_w)):
                    sp.dma_start(w[:, n], x.rearrange("(c p) n -> p c n", p=P)).then_inc(loaded, 16)
                column_loads(sp, bcol[:], [ws_b, wo_b, wi_b], loaded)
                row_broadcast(sp, brow[:], mlp_b, loaded)

            @block.tensor
            def _(pe):
                pe.wait_ge(loaded, 128)
                for j in range(2 * DC):
                    for m in range(DC):
                        mm = nc.tensor.transpose(psum[j][:, m * P:(m + 1) * P], mlp[:, m, j * P:(j + 1) * P], t.ident[:])
                    mm.then_inc(turned, 1)
                pe.wait_ge(copied, 2 * DC)
                for i, (n, c) in enumerate(order):
                    if i >= 4:
                        pe.wait_ge(split, i - 3)
                    for j in range(DC):
                        mm = nc.tensor.matmul(psum[i % 4][:], w[:, n, j, c * P:(c + 1) * P], mlp_t[:, (DC if n else 0) + j, :], start=j == 0, stop=j == DC - 1)
                    mm.then_inc(produced, 1)
                pe.wait_ge(step, 3)
                for j in range(2 * DC):
                    mm = nc.tensor.matmul(psum[7][:], wide[:, j, :], mlp_t[:, j, :], start=j == 0, stop=j == 2 * DC - 1)
                mm.then_inc(constant, 1)

            @block.scalar
            def _(a):
                for j in range(2 * DC):
                    a.wait_ge(turned, j + 1)
                    nc.scalar.copy(mlp_t[:, j, :], psum[j][:]).then_inc(copied, 1)
                for i, (n, c) in enumerate(order):
                    a.wait_ge(produced, i + 1)
                    nc.scalar.copy(folded[n][0][:, c, :], psum[i % 4][:]).then_inc(halved, 1)

            @block.vector
            def _(v):
                v.wait_ge(loaded, 128)
                nc.vector.tensor_copy(bsum[:, 0], bcol[:, 0])
                nc.vector.tensor_tensor(bsum[:, 1], bcol[:, 1], bcol[:, 2], ALU.add).then_inc(step, 1)
                v.wait_ge(step, 1)
                nc.vector.tensor_copy(wide[:], bsum[:].rearrange("p a (c o) -> p (a c) o", o=1).to_broadcast([P, 2 * DC, P])).then_inc(step, 2)
                for i, (n, c) in enumerate(order):
                    v.wait_ge(halved, i + 1)
                    nc.vector.tensor_tensor(folded[n][1][:, c, :], psum[i % 4][:], folded[n][0][:, c, :].bitcast(F32), ALU.subtract).then_inc(split, 1)
                v.wait_ge(constant, 1)
                nc.vector.tensor_tensor(const_row[:], psum[7][:], brow[:], ALU.add)


def sum_messages(nc, t, q, rows, edge_attr, weight, table, name):
    with ExitStack() as ctx:
        ctx.enter_context(nc.cleanup_on_exit())

        def sb(what, shape, dt=F32):
            return ctx.enter_context(nc.sbuf_tensor(f"{name}_{what}", shape, dt))

        def sem(what):
            return nc.alloc_semaphore(f"{name}_{what}")

        index = sb("index", [P, 2, GT, 3], I32)
        x, seg, attr = sb("x", [P, 2, GT, D]), sb("seg", [P, GT, D]), sb("attr", [P, 2, GT, D])
        high, low = sb("high", [P, GT, D], F32R), sb("low", [P, GT, D], F32R)
        same = sb("same", [P, 2, GT, P], F32R)
        ah, al = sb("ah", [P, GT, DC, P], F32R), sb("al", [P, GT, DC, P], F32R)
        out = sb("out", [P, 2, GT, D])
        turn_ps = [ctx.enter_context(nc.psum_tensor(f"{name}_tps{i}", [P, DC, P], F32)) for i in range(4)]
        row_ps = [ctx.enter_context(nc.psum_tensor(f"{name}_rps{i}", [P, D], F32)) for i in range(4)]
        norm = make_norm(nc, ctx, name + "n")
        wh, wl = weight
        indexed, sent = sem("indexed"), sem("sent")
        gathered, stored = [sem(f"gathered{p}") for p in range(2)], [sem(f"stored{p}") for p in range(2)]
        seg_got = sem("seg_got")
        joined, relued, formed, halved, split = (sem(s) for s in ("joined", "relued", "formed", "halved", "split"))
        widened, summed, t_halved, t_split, produced, copied = (sem(s) for s in ("widened", "summed", "t_halved", "t_split", "produced", "copied"))

        with nc.Block() as block:
            @block.gpsimd
            def _(pl):
                def fetch(g, par, i):
                    pl.wait_ge(split, tiles_two_before(g))
                    nc.gpsimd.tensor_copy(index[:, par], t.fetch[q][:, DS(g * GT, GT), :]).then_inc(indexed, 1)
                    pl.wait_ge(joined, tile_before(g, GT - 1))
                    pl.wait_ge(indexed, g + 1)
                    pl.sem_inc(sent, 1)
                    for k in range(GT):
                        for n, (dst, table_, done) in enumerate(((x[:, par, k, :], rows, gathered[par]), (seg[:, k, :], t.seg_in, seg_got),
                                                                 (attr[:, par, k, :], edge_attr, gathered[par]))):
                            nc.gpsimd.indirect_dma_start(out=dst, out_offset=None, in_=table_,
                                                         in_offset=bass.IndirectOffsetOnAxis(ap=index[:, par, k, n:n + 1], axis=0)).then_inc(done, 16)

                edge_groups(pl, fetch, lambda g, par, i, nxt: nxt and fetch(*nxt))

            @block.vector
            def _(v):
                norm_credit_vector(v, norm)
                for s in (joined, formed, split, t_split):
                    v.sem_inc(s, TILE_CREDIT)

                def message(g, par, i):
                    v.wait_ge(gathered[par], 128 * (i + 1))
                    v.wait_ge(seg_got, 64 * (g + 1))
                    for k in range(GT):
                        nc.vector.tensor_tensor(x[:, par, k, :], x[:, par, k, :], seg[:, k, :], ALU.add).then_inc(joined, 1)
                    v.wait_ge(joined, tile_done(g, GT - 1))
                    norm_statistics(nc, v, norm, x[:, par], g, par, GT)
                    norm_coefficients(nc, v, norm, g, par, GT)
                    for k in range(GT):
                        v.wait_ge(relued, tile_done(g, k))
                        nc.vector.tensor_tensor(x[:, par, k, :], x[:, par, k, :], attr[:, par, k, :], ALU.subtract).then_inc(formed, 1)
                    for k in range(GT):
                        v.wait_ge(halved, tile_done(g, k))
                        nc.vector.tensor_tensor(low[:, k, :], x[:, par, k, :], high[:, k, :].bitcast(F32), ALU.subtract).then_inc(split, 1)

                def lower(g):
                    for k in range(GT):
                        v.wait_ge(t_halved, tile_done(g, k))
                        nc.vector.tensor_tensor(al[:, k], turn_ps[k][:], ah[:, k].bitcast(F32), ALU.subtract).then_inc(t_split, 1)

                def start(g, par, i):
                    message(g, par, i)
                    lower(g)

                def body(g, par, i, nxt):
                    if nxt:
                        message(*nxt)
                        lower(nxt[0])

                edge_groups(v, start, body)

            @block.scalar
            def _(a):
                norm_credit_scalar(a, norm)
                for s in (relued, halved, t_halved, copied):
                    a.sem_inc(s, TILE_CREDIT)
                a.sem_inc(widened, GROUP_CREDIT)

                def prepare(g, par, i):
                    a.wait_ge(summed, tiles_two_before(g))
                    nc.scalar.copy(same[:, par], t.same[q][:, DS(g * GT, GT), :]).then_inc(widened, 1)
                    norm_root(nc, a, norm, t, g, par, GT)
                    a.wait_ge(norm.ready, group_done(g))
                    for k in range(GT):
                        nc.scalar.activation(x[:, par, k, :], x[:, par, k, :], ACT.Relu, bias=norm.shift[:, par, k:k + 1],
                                             scale=norm.scale[:, par, k:k + 1]).then_inc(relued, 1)
                    for k in range(GT):
                        a.wait_ge(formed, tile_done(g, k))
                        a.wait_ge(summed, tile_before(g, k))
                        nc.scalar.copy(high[:, k, :], x[:, par, k, :]).then_inc(halved, 1)

                def higher(g):
                    for k in range(GT):
                        a.wait_ge(summed, tile_done(g, k))
                        a.wait_ge(produced, tile_before(g, k))
                        nc.scalar.copy(ah[:, k], turn_ps[k][:]).then_inc(t_halved, 1)

                def start(g, par, i):
                    prepare(g, par, i)
                    higher(g)

                def body(g, par, i, nxt):
                    if nxt:
                        prepare(*nxt)
                    wait_uses(a, stored[par], 16 * i)
                    for k in range(GT):
                        a.wait_ge(produced, tile_done(g, k))
                        nc.scalar.copy(out[:, par, k, :], row_ps[k][:]).then_inc(copied, 1)
                    if nxt:
                        higher(nxt[0])

                edge_groups(a, start, body)

            @block.tensor
            def _(pe):
                pe.sem_inc(summed, TILE_CREDIT)
                pe.sem_inc(produced, TILE_CREDIT)

                def total(g, par, i):
                    pe.wait_ge(widened, group_done(g))
                    for k in range(GT):
                        pe.wait_ge(split, tile_done(g, k))
                        pe.wait_ge(t_split, tile_before(g, k))
                        for c in range(DC):
                            nc.tensor.matmul(turn_ps[k][:, c, :], low[:, k, c * P:(c + 1) * P], same[:, par, k, :], start=True, stop=False)
                            mm = nc.tensor.matmul(turn_ps[k][:, c, :], high[:, k, c * P:(c + 1) * P], same[:, par, k, :], start=False, stop=True)
                        mm.then_inc(summed, 1)

                def body(g, par, i, nxt):
                    for k in range(GT):
                        pe.wait_ge(t_split, tile_done(g, k))
                        pe.wait_ge(copied, tile_before(g, k))
                        for c in range(DC):
                            mm = product3(nc, row_ps[k][:], ah[:, k, c, :], al[:, k, c, :], wh[:, c, :], wl[:, c, :], c == 0, c == DC - 1)
                        mm.then_inc(produced, 1)
                    if nxt:
                        total(*nxt)

                edge_groups(pe, total, body)

            @block.sync
            def _(sp):
                def store(g, par, i, nxt):
                    sp.wait_ge(copied, tile_done(g, GT - 1))
                    sp.dma_start(table[DS(g * GR, GR), :].rearrange("(k p) d -> p k d", p=P), out[:, par]).then_inc(stored[par], 16)

                edge_groups(sp, nothing, store)
                for par in range(2):
                    sp.wait_ge(stored[par], 16 * (EG // 2))
    complete_segments(nc, t, q, table, name + "c")


def last_layer(nc, t, rows, weight, const_row, slope, out_rows):
    name = "last"
    with ExitStack() as ctx:
        ctx.enter_context(nc.cleanup_on_exit())

        def sb(what, shape, dt=F32):
            return ctx.enter_context(nc.sbuf_tensor(f"{name}_{what}", shape, dt))

        def sem(what):
            return nc.alloc_semaphore(f"{name}_{what}")

        wh, wl = weight
        x, seg, h = sb("x", [P, 2, GT, D]), sb("seg", [P, GT, D]), sb("h", [P, GT, D])
        side = [sb(f"side{q}", [P, 2, GT, D]) for q in range(2)]
        ah, al = sb("ah", [P, GT, DC, P], F32R), sb("al", [P, GT, DC, P], F32R)
        out = sb("out", [P, GT, D])
        slope_col = sb("slope", [P, 1])
        index = sb("index", [P, 2, 2, GT], I32)
        turn_ps = [ctx.enter_context(nc.psum_tensor(f"{name}_tps{i}", [P, DC, P], F32)) for i in range(4)]
        row_ps = [ctx.enter_context(nc.psum_tensor(f"{name}_rps{i}", [P, D], F32)) for i in range(4)]
        norm = make_norm(nc, ctx, name + "n")
        consts, indexed, sent = sem("consts"), sem("indexed"), sem("sent")
        loaded, gathered, seg_got = [sem(f"loaded{p}") for p in range(2)], [sem(f"gathered{p}") for p in range(2)], sem("seg_got")
        stored = sem("stored")
        joined, relued, turned, halved, split = (sem(n) for n in ("joined", "relued", "turned", "halved", "split"))
        produced, added1, added2, z_ready, positive, negative, bent, finished = (
            sem(n) for n in ("produced", "added1", "added2", "z_ready", "positive", "negative", "bent", "finished"))

        with nc.Block() as block:
            @block.sync
            def _(sp):
                sp.dma_start(slope_col[:], slope.rearrange("(o d) -> o d", o=1).to_broadcast([P, 1])).then_inc(consts, 16)

                def load(g, par, i, tail):
                    sp.wait_ge(finished, tiles_two_before(g))
                    load_group(sp, x[:, par], rows, g, tail, loaded[par])

                node_groups(sp, load, lambda g, par, i, tail, nxt: nxt and load(*nxt))

            @block.gpsimd
            def _(pl):
                def fetch(g, par, i, tail):
                    tiles = tiles_of(tail)
                    pl.wait_ge(finished, tiles_two_before(g))
                    for q in range(2):
                        nc.gpsimd.tensor_copy(index[:, par, q, 0:tiles], t.last[q][:, DS(g * GT, tiles)]).then_inc(indexed, 1)
                    pl.wait_ge(joined, tile_before(g, GT - 1))
                    pl.wait_ge(indexed, 2 * g + 2)
                    pl.sem_inc(sent, 1)
                    for k in range(tiles):
                        nc.gpsimd.indirect_dma_start(out=seg[:, k, :], out_offset=None, in_=t.seg_in,
                                                     in_offset=bass.IndirectOffsetOnAxis(ap=index[:, par, 0, k:k + 1], axis=0)).then_inc(seg_got, 16)
                    for k in range(tiles):
                        for q, table in enumerate((t.seg_dst, t.seg_src)):
                            nc.gpsimd.indirect_dma_start(out=side[q][:, par, k, :], out_offset=None, in_=table,
                                                         in_offset=bass.IndirectOffsetOnAxis(ap=index[:, par, q, k:k + 1], axis=0)).then_inc(gathered[par], 16)

                node_groups(pl, fetch, lambda g, par, i, tail, nxt: nxt and fetch(*nxt))

            @block.vector
            def _(v):
                norm_credit_vector(v, norm)
                for s in (joined, split, added1, added2, z_ready, bent, finished):
                    v.sem_inc(s, TILE_CREDIT)
                v.wait_ge(consts, 16)

                def join(g, par, i, tail):
                    tiles = tiles_of(tail)
                    v.wait_ge(loaded[par], loads_done(i, tail))
                    v.wait_ge(seg_got, 64 * g + 16 * tiles)
                    for k in range(tiles):
                        nc.vector.tensor_tensor(x[:, par, k, :], x[:, par, k, :], seg[:, k, :], ALU.add).then_inc(joined, 1)
                    v.wait_ge(joined, tile_done(g, tiles - 1))
                    norm_statistics(nc, v, norm, x[:, par], g, par, tiles)
                    norm_coefficients(nc, v, norm, g, par, tiles)

                def lower(g, k):
                    v.wait_ge(halved, tile_done(g, k))
                    nc.vector.tensor_tensor(al[:, k], turn_ps[k][:], ah[:, k].bitcast(F32), ALU.subtract).then_inc(split, 1)

                def start(g, par, i, tail):
                    join(g, par, i, tail)
                    for k in range(GT):
                        lower(g, k)

                def finish(g, par, k):
                    v.wait_ge(negative, tile_done(g, k))
                    s0, s1 = side[0][:, par, k, :], side[1][:, par, k, :]
                    nc.vector.scalar_tensor_tensor(s0, s0, slope_col[:], s1, ALU.mult, ALU.subtract).then_inc(bent, 1)
                    v.wait_ge(bent, tile_done(g, k))
                    nc.vector.tensor_tensor(out[:, k, :], x[:, par, k, :], s0, ALU.subtract).then_inc(finished, 1)

                def body(g, par, i, tail, nxt):
                    if nxt:
                        join(*nxt)
                    v.wait_ge(gathered[par], 128 * i + 32 * tiles_of(tail))
                    wait_uses(v, stored, 16 * g)
                    for k in range(GT):
                        if k < tiles_of(tail):
                            v.wait_ge(produced, tile_done(g, k))
                            s0, s1 = side[0][:, par, k, :], side[1][:, par, k, :]
                            nc.vector.scalar_tensor_tensor(s0, s0, t.rcnt[0][:, DS(g * GT + k, 1)], row_ps[k][:], ALU.mult, ALU.add).then_inc(added1, 1)
                            v.wait_ge(added1, tile_done(g, k))
                            nc.vector.scalar_tensor_tensor(s0, s1, t.rcnt[1][:, DS(g * GT + k, 1)], s0, ALU.mult, ALU.add).then_inc(added2, 1)
                            v.wait_ge(added2, tile_done(g, k))
                            nc.vector.tensor_tensor(s0, s0, const_row[:], ALU.add).then_inc(z_ready, 1)
                        if nxt and k < tiles_of(nxt[3]):
                            lower(nxt[0], k)
                        if 0 < k <= tiles_of(tail):
                            finish(g, par, k - 1)
                    if not tail:
                        finish(g, par, GT - 1)

                node_groups(v, start, body)

            @block.scalar
            def _(a):
                norm_credit_scalar(a, norm)
                for s in (relued, halved, positive, negative):
                    a.sem_inc(s, TILE_CREDIT)

                def apply(g, par, i, tail):
                    norm_root(nc, a, norm, t, g, par, tiles_of(tail))
                    a.wait_ge(norm.ready, group_done(g))
                    for k in range(tiles_of(tail)):
                        a.wait_ge(turned, tile_before(g, k))
                        nc.scalar.activation(h[:, k, :], x[:, par, k, :], ACT.Relu, bias=norm.shift[:, par, k:k + 1],
                                             scale=norm.scale[:, par, k:k + 1]).then_inc(relued, 1)

                def higher(g, k):
                    a.wait_ge(turned, tile_done(g, k))
                    a.wait_ge(produced, tile_before(g, k))
                    nc.scalar.copy(ah[:, k], turn_ps[k][:]).then_inc(halved, 1)

                def start(g, par, i, tail):
                    apply(g, par, i, tail)
                    for k in range(GT):
                        higher(g, k)

                def body(g, par, i, tail, nxt):
                    if nxt:
                        apply(*nxt)
                    for k in range(GT):
                        if nxt and k < tiles_of(nxt[3]):
                            higher(nxt[0], k)
                        if k < tiles_of(tail):
                            a.wait_ge(z_ready, tile_done(g, k))
                            nc.scalar.activation(side[1][:, par, k, :], side[0][:, par, k, :], ACT.Relu).then_inc(positive, 1)
                            a.wait_ge(positive, tile_done(g, k))
                            nc.scalar.activation(side[0][:, par, k, :], side[0][:, par, k, :], ACT.Relu, scale=-1.0).then_inc(negative, 1)
                    a.wait_ge(finished, tile_done(g, tiles_of(tail) - 1))
                    store_group(a, out_rows, out[:], g, tail, stored)

                node_groups(a, start, body)
                a.wait_ge(stored, 16 * (NG + 1))

            @block.tensor
            def _(pe):
                pe.sem_inc(turned, TILE_CREDIT)
                pe.sem_inc(produced, TILE_CREDIT)

                def turn(g, k):
                    pe.wait_ge(relued, tile_done(g, k))
                    pe.wait_ge(split, tile_before(g, k))
                    for c in range(DC):
                        mm = nc.tensor.transpose(turn_ps[k][:, c, :], h[:, k, c * P:(c + 1) * P], t.ident[:])
                    mm.then_inc(turned, 1)

                def start(g, par, i, tail):
                    for k in range(GT):
                        turn(g, k)

                def body(g, par, i, tail, nxt):
                    for k in range(GT):
                        if k < tiles_of(tail):
                            pe.wait_ge(split, tile_done(g, k))
                            pe.wait_ge(added1, tile_before(g, k))
                            for c in range(DC):
                                mm = product3(nc, row_ps[k][:], ah[:, k, c, :], al[:, k, c, :], wh[:, c, :], wl[:, c, :], c == 0, c == DC - 1)
                            mm.then_inc(produced, 1)
                        if nxt and k < tiles_of(nxt[3]):
                            turn(nxt[0], k)

                node_groups(pe, start, body)


def gnn_program(nc, x, src, dst, edge_attr, l0_eps, l0_w1, l0_b1, l0_g1, l0_be1, l0_w2, l0_b2, l0_g2, l0_be2,
                l1_w1, l1_b1, l1_w2, l1_b2, coeffs, paths, wo_w, wo_b, wi_w, wi_b, ws_w, ws_b, mlp_w, mlp_b, slope, out):
    with ExitStack() as ctx:
        t = make_tables(nc, ctx)
        sort_edges(nc, t, src, dst)
        index_edges(nc, t)
        sum_segments(nc, t, x, t.seg_in, "ginseg", True)
        with ExitStack() as layer:
            stats1 = layer.enter_context(nc.sbuf_tensor("stats1", [P, HC, NG, 6], F32))
            stats2 = layer.enter_context(nc.sbuf_tensor("stats2", [P, DC, NG, 6], F32))
            coef1 = layer.enter_context(nc.sbuf_tensor("coef1", [P, 2, HC], F32))
            coef2 = layer.enter_context(nc.sbuf_tensor("coef2", [P, 2, DC], F32))
            gin_up(nc, t, x, l0_eps, l0_w1, l0_b1, stats1)
            batch_norm_coefficients(nc, t, stats1, l0_g1, l0_be1, coef1, HC, "bn1")
            gin_down(nc, t, l0_w2, l0_b2, coef1, stats2)
            batch_norm_coefficients(nc, t, stats2, l0_g2, l0_be2, coef2, DC, "bn2")
            gin_out(nc, t, x, coef2)
        sum_segments(nc, t, t.x1, t.seg_in, "gcnseg0", True, t.dis_other)
        gcn(nc, t, 0, t.x1, l1_w1, l1_b1, t.r1)
        sum_segments(nc, t, t.r1, t.seg_in, "gcnseg1", False)
        gcn(nc, t, 1, t.r1, l1_w2, l1_b2, t.x2, t.x1)
        path_products(nc, t, t.x2, edge_attr, paths, coeffs)
        folded = [[ctx.enter_context(nc.sbuf_tensor(f"folded{n}{half}", [P, DC, D], F32R)) for half in "hl"] for n in "soi"]
        const_row = ctx.enter_context(nc.sbuf_tensor("const_row", [P, D], F32))
        fold_weights(nc, t, wo_w, wi_w, ws_w, mlp_w, wo_b, wi_b, ws_b, mlp_b, folded, const_row)
        sum_messages(nc, t, 0, t.x2, edge_attr, folded[1], t.seg_dst, "outmsg")
        sum_messages(nc, t, 1, t.x2, edge_attr, folded[2], t.seg_src, "inmsg")
        last_layer(nc, t, t.x2, folded[0], const_row, slope, out)


NAMES = ["x", "src", "dst", "edge_attr_512", "L0_gnn_eps", "L0_gnn_W1", "L0_gnn_b1", "L0_gnn_g1", "L0_gnn_be1", "L0_gnn_W2",
         "L0_gnn_b2", "L0_gnn_g2", "L0_gnn_be2", "L1_gnn_W1", "L1_gnn_b1", "L1_gnn_W2", "L1_gnn_b2", "L2_gnn_path_coeffs",
         "L2_gnn_path_indices", "L3_gnn_WO_w", "L3_gnn_WO_b", "L3_gnn_WI_w", "L3_gnn_WI_b", "L3_gnn_WS_w", "L3_gnn_WS_b",
         "L3_gnn_mlp_w", "L3_gnn_mlp_b", "L3_gnn_prelu_a"]


def kernel(**inputs):
    import concourse.bacc as bacc
    from concourse.bass_utils import run_bass_kernel_spmd

    nc = bacc.Bacc("TRN2", target_bir_lowering=False, num_devices=1)
    arrays, args = {}, []
    for name in NAMES:
        a = np.ascontiguousarray(inputs[name])
        a = a.reshape(1) if a.ndim == 0 else a
        arrays[f"in_{name}"] = a
        args.append(nc.dram_tensor(f"in_{name}", a.shape, mybir.dt.from_np(a.dtype), kind="ExternalInput").ap())
    out = nc.dram_tensor("out", (N, D), F32, kind="ExternalOutput").ap()
    gnn_program(nc, *args, out)
    result = run_bass_kernel_spmd(nc, [arrays], core_ids=[0])
    return result.results[0]["out"]
```

```python
from contextlib import ExitStack

import numpy as np
import concourse.bass as bass
import concourse.mybir as mybir

F32 = mybir.dt.float32
F32R = mybir.dt.float32r
BF16 = mybir.dt.bfloat16
I32 = mybir.dt.int32
ALU = mybir.AluOpType
ACT = mybir.ActivationFunctionType
DS = bass.ds

P = 128
N = 10000
E = 5000
D = 512
H = 1024
DC = D // P
HC = H // P
GT = 4
GR = GT * P
NG = -(-N // GR)
TAIL = N - (NG - 1) * GR
TAIL_T = -(-TAIL // P)
TURNS = NG // 4
ET = -(-E // P)
EP = ET * P
EG = ET // GT
NB = 80
PADKEY = (NB - 1) * P
ZROW = EP
SPARE = EP + 1
TROWS = EP + 1 + ET
SEG, EXT, PATHS = 16, 32, 64
LN_EPS = 1e-5


def tiles_of(g_is_tail):
    return TAIL_T if g_is_tail else GT


def load_group(eng, dst, dram, g, tail, sem, width=D):
    if not tail:
        eng.dma_start(dst, dram[DS(g * GR, GR), 0:width].rearrange("(k p) d -> p k d", p=P)).then_inc(sem, 16)
        return
    full = TAIL // P
    eng.dma_start(dst[:, 0:full], dram[g * GR:g * GR + full * P, 0:width].rearrange("(k p) d -> p k d", p=P)).then_inc(sem, 16)
    eng.dma_start(dst[0:TAIL - full * P, full], dram[g * GR + full * P:N, 0:width]).then_inc(sem, 16)


def store_group(eng, dram, src, g, tail, sem):
    if not tail:
        eng.dma_start(dram[DS(g * GR, GR), :].rearrange("(k p) d -> p k d", p=P), src).then_inc(sem, 16)
        return
    full = TAIL // P
    eng.dma_start(dram[g * GR:g * GR + full * P, :].rearrange("(k p) d -> p k d", p=P), src[:, 0:full]).then_inc(sem, 16)
    eng.dma_start(dram[g * GR + full * P:N, :], src[0:TAIL - full * P, full]).then_inc(sem, 16)


def loads_done(i, tail):
    return 16 * (i + 1) + (16 if tail else 0)


def node_groups(eng, start, body):
    def turn_of_four(turn, first_of_next):
        four = [(4 * turn + j, j % 2, 2 * turn + j // 2, j, turn, False) for j in range(4)]
        for group, nxt in zip(four, four[1:] + [first_of_next]):
            body(*group, nxt)

    def first(turn):
        return (4 * turn, 0, 2 * turn, 0, turn, False)

    start(*first(0))
    turn_of_four(0, first(1))
    with eng.Fori(1, TURNS - 1) as turn:
        turn_of_four(turn, first(turn + 1))
    last = TURNS - 1
    rest = [(4 * last + j, j % 2, 2 * last + j // 2, j, last, j == 3) for j in range(4)]
    for group, nxt in zip(rest, rest[1:] + [None]):
        body(*group, nxt)


def each_node_group(eng, step):
    node_groups(eng, nothing, lambda g, par, i, slot, lap, tail, nxt: step(g, par, i, slot, lap, tail))


def edge_groups(eng, start, body):
    start(0, 0, 0)
    body(0, 0, 0, (1, 1, 0))
    body(1, 1, 0, (2, 0, 1))
    with eng.Fori(1, EG // 2 - 1) as i:
        body(2 * i, 0, i, (2 * i + 1, 1, i))
        body(2 * i + 1, 1, i, (2 * i + 2, 0, i + 1))
    last = EG // 2 - 1
    body(EG - 2, 0, last, (EG - 1, 1, last))
    body(EG - 1, 1, last, None)


def wait_uses(eng, sem, value):
    if not isinstance(value, int) or value > 0:
        eng.wait_ge(sem, value)


def nothing(*_):
    return None


def product3(nc, out, wh, wl, ah, al, first, last):
    nc.tensor.matmul(out, wl, ah, start=first, stop=False)
    nc.tensor.matmul(out, wh, al, start=False, stop=False)
    return nc.tensor.matmul(out, wh, ah, start=False, stop=last)


class Tables:
    pass


def make_tables(nc, ctx):
    t = Tables()

    def sb(name, shape, dt):
        return ctx.enter_context(nc.sbuf_tensor(name, shape, dt))

    t.ident = sb("ident", [P, P], F32)
    t.ones = sb("ones", [P, P], F32)
    t.eps = sb("eps", [P, 1], F32)
    t.rowiota = sb("rowiota", [P, P], F32)
    t.partiota = sb("partiota", [P, 1], F32)
    t.same = [sb(f"same{q}", [P, ET, P], BF16) for q in range(2)]
    t.last = [sb(f"last{q}", [P, NB], I32) for q in range(2)]
    t.dis = sb("dis", [P, NB], F32)
    t.rcnt = [sb(f"rcnt{q}", [P, NB], F32) for q in range(2)]
    t.meta = [sb(f"meta{q}", [P, ET, 4], I32) for q in range(2)]
    t.other = [sb(f"other{q}", [P, ET], I32) for q in range(2)]
    t.eid = [sb(f"eid{q}", [P, ET], I32) for q in range(2)]
    t.etab = [sb(f"etab{q}", [P, ET, 4], I32) for q in range(2)]
    t.nlast = [sb(f"nlast{q}", [P, ET], I32) for q in range(2)]
    t.fetch = [sb(f"fetch{q}", [P, ET, 3], I32) for q in range(2)]
    t.dis_other = sb("dis_other", [P, ET], F32)
    t.cut_rows = [sb(f"cut_rows{q}", [ET, 1], I32) for q in range(2)]
    t.cut_dest = [sb(f"cut_dest{q}", [ET, 1], I32) for q in range(2)]
    t.cut_same = [sb(f"cut_same{q}", [ET, ET], F32) for q in range(2)]

    def dram(name, shape, dt=F32):
        return nc.dram_tensor(name, shape, dt).ap()

    t.smeta = [dram(f"smeta{q}", [EP + 1, 4], I32) for q in range(2)]
    t.tab = dram("tab", [NB * P, 4], I32)
    t.seg_in = dram("seg_a", [TROWS, D])
    t.seg_dst = dram("seg_b", [TROWS, D])
    t.seg_src = dram("seg_c", [TROWS, D])
    t.y1 = dram("y1", [NG, P, HC, GR])
    t.y2 = dram("y2", [NG, P, DC, GR])
    t.x1 = dram("x1", [N, D])
    t.r1 = dram("r1", [N, D])
    t.x2 = dram("x2", [N, D])
    return t


def sort_edges(nc, t, src, dst):
    keys = (dst, src)
    with ExitStack() as ctx:
        ctx.enter_context(nc.cleanup_on_exit())
        def sb(name, shape, dt=F32):
            return ctx.enter_context(nc.sbuf_tensor(name, shape, dt))

        ktile = sb("ktile", [ET, 2, P], I32)
        ktile_f = sb("ktile_f", [ET, 2, P])
        kcol = sb("kcol", [P, 2, ET])
        kcol_i = sb("kcol_i", [P, 2, ET], I32)
        hi_i = sb("hi_i", [P, 2, ET], I32)
        lo_i = sb("lo_i", [P, 2, ET], I32)
        hi_f = sb("hi_f", [P, 2, ET])
        lo_f = sb("lo_f", [P, 2, ET])
        eid_f = sb("eid_f", [P, ET])
        pack = sb("pack", [P, 2, ET, 5], I32)
        krow_i = sb("krow_i", [P, 2, EP], I32)
        hrow_i = sb("hrow_i", [NB, 2, EP], I32)
        earlier = sb("earlier", [P, P])
        before = sb("before", [NB, NB])
        hot_hi = sb("hot_hi", [P, 2, ET, NB], BF16)
        hot_lo = sb("hot_lo", [P, 2, ET, P], BF16)
        count = sb("count", [NB, 2, ET + 1, P])
        incl = sb("incl", [NB, 2, P])
        start_of = sb("start_of", [NB, 2, P])
        rowsum = sb("rowsum", [NB, 2])
        lastf = sb("lastf", [NB, 2, P])
        some = sb("some", [NB, 2, P])
        disf = sb("disf", [NB, P])
        tabs = sb("tabs", [NB, P, 4], I32)
        zeros = sb("zeros", [P, D])
        onesrow = sb("onesrow", [NB, P])
        hitT = sb("hitT", [NB, 2, P])
        from_ = sb("from_", [NB, 2, P])
        scratch = sb("scratch", [P, 2, P])
        prior = sb("prior", [P, 2, ET])
        tie = sb("tie", [P, 2, ET])
        rank = sb("rank", [P, 2, ET])
        slot = sb("slot", [P, 4, 5], I32)
        psum = [ctx.enter_context(nc.psum_tensor(f"sort_ps{i}", [P, 512], F32)) for i in range(8)]

        def sem(name):
            return nc.alloc_semaphore(name)

        padded, loaded, pads_done, made = sem("padded"), sem("loaded"), sem("pads_done"), sem("made")
        step, turned, zstored = sem("sort_step"), sem("turned"), sem("zstored")
        with nc.Block() as block:
            @block.sync
            def _(sp):
                sp.wait_ge(padded, 1)
                full = E // P
                for q in range(2):
                    sp.dma_start(ktile[0:full, q, :], keys[q][0:full * P].rearrange("(t p) -> t p", p=P)).then_inc(loaded, 16)
                    sp.dma_start(ktile[full:ET, q, 0:E - full * P], keys[q][full * P:E].rearrange("(t p) -> t p", t=1)).then_inc(loaded, 16)
                    sp.dma_start(krow_i[:, q, 0:E], keys[q].rearrange("(o e) -> o e", o=1).to_broadcast([P, E])).then_inc(loaded, 16)
                sp.wait_ge(made, 1)
                for q, table in enumerate((t.seg_in, t.seg_dst, t.seg_src)):
                    sp.dma_start(table[ZROW:TROWS, :], zeros[0:TROWS - ZROW, :]).then_inc(zstored, 16)
                sp.wait_ge(zstored, 48)

            @block.gpsimd
            def _(pl):
                nc.gpsimd.memset(ktile[:], PADKEY)
                nc.gpsimd.memset(krow_i[:, :, E:EP], PADKEY).then_inc(padded, 1)
                nc.gpsimd.memset(zeros[:], 0.0).then_inc(made, 1)
                nc.gpsimd.memset(t.ident[:], 1.0)
                nc.gpsimd.memset(t.ones[:], 1.0)
                nc.gpsimd.memset(earlier[:], 1.0)
                nc.gpsimd.memset(before[:], 1.0)
                nc.gpsimd.memset(onesrow[:], 1.0)
                nc.gpsimd.memset(t.eps[:], LN_EPS)
                nc.gpsimd.iota(t.rowiota[:], pattern=[[1, P]], base=0, channel_multiplier=0, allow_small_or_imprecise_dtypes=True)
                nc.gpsimd.iota(t.partiota[:], pattern=[[1, 1]], base=0, channel_multiplier=1, allow_small_or_imprecise_dtypes=True)
                nc.gpsimd.iota(eid_f[:], pattern=[[P, ET]], base=0, channel_multiplier=1, allow_small_or_imprecise_dtypes=True).then_inc(made, 1)
                pl.wait_ge(made, 2)
                nc.gpsimd.affine_select(out=t.ident[:], in_=t.ident[:], compare_op=ALU.is_equal, fill=0.0, base=0, pattern=[[-1, P]], channel_multiplier=1)
                nc.gpsimd.affine_select(out=earlier[:], in_=earlier[:], compare_op=ALU.is_gt, fill=0.0, base=0, pattern=[[-1, P]], channel_multiplier=1)
                nc.gpsimd.affine_select(out=before[:], in_=before[:], compare_op=ALU.is_gt, fill=0.0, base=0, pattern=[[1, NB]], channel_multiplier=-1).then_inc(made, 1)

            @block.tensor
            def _(pe):
                pe.wait_ge(made, 3)
                pe.wait_ge(step, 1)
                for q in range(2):
                    mm = nc.tensor.transpose(psum[q][:, 0:ET], ktile_f[:, q, :], t.ident[0:ET, 0:ET])
                mm.then_inc(turned, 1)

            @block.vector
            def _(v):
                n = [0]

                def link(ins):
                    n[0] += 1
                    ins.then_inc(step, 1)
                    v.wait_ge(step, n[0])

                v.wait_ge(padded, 1)
                v.wait_ge(loaded, 96)
                link(nc.vector.tensor_copy(ktile_f[:], ktile[:]))
                v.wait_ge(turned, 1)
                for q in range(2):
                    link(nc.vector.tensor_copy(kcol[:, q, :], psum[q][:, 0:ET]))
                link(nc.vector.tensor_copy(kcol_i[:], kcol[:]))
                link(nc.vector.tensor_scalar(hi_i[:], kcol_i[:], 7, None, ALU.logical_shift_right))
                link(nc.vector.tensor_scalar(lo_i[:], kcol_i[:], P - 1, None, ALU.bitwise_and))
                link(nc.vector.tensor_copy(hi_f[:], hi_i[:]))
                link(nc.vector.tensor_copy(lo_f[:], lo_i[:]))
                v.wait_ge(made, 3)
                for q in range(2):
                    link(nc.vector.tensor_tensor(
                        hot_hi[:, q], t.rowiota[:, 0:NB].rearrange("p (o n) -> p o n", o=1).to_broadcast([P, ET, NB]),
                        hi_f[:, q, :].rearrange("p (t o) -> p t o", o=1).to_broadcast([P, ET, NB]), ALU.is_equal))
                    link(nc.vector.tensor_tensor(
                        hot_lo[:, q], t.rowiota[:, :].rearrange("p (o n) -> p o n", o=1).to_broadcast([P, ET, P]),
                        lo_f[:, q, :].rearrange("p (t o) -> p t o", o=1).to_broadcast([P, ET, P]), ALU.is_equal))
                    link(nc.vector.tensor_scalar(hrow_i[:, q, :], krow_i[0:NB, q, :], 7, None, ALU.logical_shift_right))
                link(nc.vector.memset(pack[:], 0))
                for q in range(2):
                    link(nc.vector.tensor_copy(pack[:, q, :, 1], kcol[:, q, :]))
                    link(nc.vector.scalar_tensor_tensor(pack[:, q, :, 2], kcol[:, 1 - q, :], float(PADKEY), kcol[:, 1 - q, :], ALU.is_lt, ALU.mult))
                    link(nc.vector.scalar_tensor_tensor(pack[:, q, :, 3], eid_f[:], float(E), eid_f[:], ALU.is_lt, ALU.mult))
                link(nc.vector.memset(count[:, :, 0, :], 0.0))

        tile_counted, added = sem("tile_counted"), sem("added")
        with nc.Block() as block:
            @block.tensor
            def _(pe):
                pe.sem_inc(added, 4)
                with pe.Fori(0, ET // 2) as i:
                    for b in range(2):
                        for q in range(2):
                            pe.wait_ge(added, 4 * i + 2 * b + q + 1)
                            nc.tensor.matmul(psum[2 * b + q][0:NB, 0:P], hot_hi[:, q, DS(2 * i + b, 1), :].rearrange("p o n -> p (o n)"),
                                             hot_lo[:, q, DS(2 * i + b, 1), :].rearrange("p o n -> p (o n)"), start=True, stop=True).then_inc(tile_counted, 1)

            @block.vector
            def _(v):
                with v.Fori(0, ET // 2) as i:
                    for b in range(2):
                        for q in range(2):
                            v.wait_ge(tile_counted, 4 * i + 2 * b + q + 1)
                            v.wait_ge(added, 4 * i + 2 * b + q + 3)
                            nc.vector.tensor_tensor(count[:, q, DS(2 * i + b + 1, 1), :], count[:, q, DS(2 * i + b, 1), :],
                                                    psum[2 * b + q][0:NB, 0:P].rearrange("p (o n) -> p o n", o=1), ALU.add).then_inc(added, 1)

        pstep, prowed, pturned, sq, tabbed = sem("pstep"), sem("prowed"), sem("pturned"), sem("sq"), sem("tabbed")
        with nc.Block() as block:
            @block.vector
            def _(v):
                n = [0]

                def link(ins):
                    n[0] += 1
                    ins.then_inc(pstep, 1)
                    v.wait_ge(pstep, n[0])

                total = count[:, :, ET, :]
                for q in range(2):
                    link(nc.vector.tensor_tensor_scan(incl[:, q, :], onesrow[:], total[:, q, :], 0.0, ALU.mult, ALU.add))
                link(nc.vector.tensor_copy(rowsum[:], incl[:, :, P - 1]))
                link(nc.vector.tensor_tensor(start_of[:], incl[:], total, ALU.subtract))
                v.wait_ge(prowed, 1)
                for q in range(2):
                    link(nc.vector.tensor_scalar(start_of[:, q, :], start_of[:, q, :], psum[4][0:NB, q:q + 1], None, ALU.add))
                link(nc.vector.tensor_tensor(lastf[:], start_of[:], total, ALU.add))
                link(nc.vector.tensor_scalar(lastf[:], lastf[:], -1.0 - ZROW, None, ALU.add))
                link(nc.vector.tensor_scalar(some[:], total, 0.0, None, ALU.is_gt))
                link(nc.vector.tensor_tensor(lastf[:], lastf[:], some[:], ALU.mult))
                link(nc.vector.tensor_scalar(lastf[:], lastf[:], float(ZROW), None, ALU.add))
                link(nc.vector.memset(tabs[:], 0))
                for q in range(2):
                    link(nc.vector.tensor_copy(tabs[:, :, q], lastf[:, q, :]))
                v.wait_ge(sq, 1)
                link(nc.vector.reciprocal(disf[:], disf[:]))
                finish_rsqrt(nc, link, disf[:], some[:, 0, :], total[:, 0, :], 1.0)
                link(nc.vector.tensor_copy(tabs[:, :, 2].bitcast(F32), disf[:]))
                v.wait_ge(pturned, 1)
                for q in range(2):
                    link(nc.vector.tensor_copy(t.last[q][:], psum[q][:, 0:NB]))
                    link(nc.vector.tensor_scalar(t.rcnt[q][:], psum[2 + q][:, 0:NB], 1.0, None, ALU.max))
                    link(nc.vector.reciprocal(t.rcnt[q][:], t.rcnt[q][:]))
                link(nc.vector.tensor_copy(t.dis[:], psum[5][:, 0:NB]))

            @block.scalar
            def _(a):
                a.wait_ge(added, 2 * ET + 4)
                a.wait_ge(made, 3)
                nc.scalar.activation(disf[:], count[:, 0, ET, :], ACT.Sqrt, bias=t.ones[0:NB, 0:1]).then_inc(sq, 1)

            @block.tensor
            def _(pe):
                pe.wait_ge(pstep, 3)
                nc.tensor.matmul(psum[4][0:NB, 0:2], before[:], rowsum[:], start=True, stop=True).then_inc(prowed, 1)
                pe.wait_ge(pstep, 20)
                for q in range(2):
                    nc.tensor.transpose(psum[q][:, 0:NB], lastf[:, q, :], t.ident[0:NB, 0:NB])
                    nc.tensor.transpose(psum[2 + q][:, 0:NB], count[:, q, ET, :], t.ident[0:NB, 0:NB])
                nc.tensor.transpose(psum[5][:, 0:NB], disf[:], t.ident[0:NB, 0:NB]).then_inc(pturned, 1)

            @block.sync
            def _(sp):
                sp.wait_ge(pstep, 20)
                sp.dma_start(t.tab.rearrange("(a b) c -> a (b c)", b=P), tabs[:].rearrange("a b c -> a (b c)")).then_inc(tabbed, 16)
                sp.wait_ge(tabbed, 16)

        hit, based, picked, tied = sem("hit"), sem("based"), sem("picked"), sem("tied")
        dotted, rstep = sem("dotted"), sem("rstep")
        with nc.Block() as block:
            @block.vector
            def _(v):
                v.sem_inc(rstep, 2)
                with v.Fori(0, ET) as i:
                    for q in range(2):
                        v.wait_ge(picked, 2 * i + q + 1)
                        nc.vector.tensor_scalar(hitT[:, q, :], hrow_i[:, q, DS(i * P, P)], t.partiota[0:NB, :], None, ALU.is_equal).then_inc(hit, 1)
                        nc.vector.tensor_tensor(from_[:, q, :], count[:, q, DS(i, 1), :].rearrange("p o n -> p (o n)"), start_of[:, q, :], ALU.add).then_inc(based, 1)
                    for q in range(2):
                        v.wait_ge(rstep, 2 * i + q + 1)
                        nc.vector.tensor_scalar(scratch[:, q, :], krow_i[:, q, DS(i * P, P)], kcol[:, q, DS(i, 1)], None, ALU.is_equal).then_inc(tied, 1)
                    for q in range(2):
                        v.wait_ge(tied, 2 * i + q + 1)
                        nc.vector.scalar_tensor_tensor(scratch[:, q, :], scratch[:, q, :], 1.0, earlier[:], ALU.mult, ALU.mult,
                                                       accum_out=tie[:, q, DS(i, 1)]).then_inc(dotted, 1)
                    for q in range(2):
                        v.wait_ge(dotted, 2 * i + q + 1)
                        v.wait_ge(picked, 2 * i + q + 3)
                        nc.vector.scalar_tensor_tensor(scratch[:, q, :], psum[q][:, 0:P], 1.0, hot_lo[:, q, DS(i, 1), :].rearrange("p o n -> p (o n)"),
                                                       ALU.mult, ALU.mult, accum_out=prior[:, q, DS(i, 1)]).then_inc(rstep, 1)
                v.wait_ge(rstep, 2 * ET + 2)
                nc.vector.tensor_tensor(rank[:], prior[:], tie[:], ALU.add).then_inc(rstep, 1)
                v.wait_ge(rstep, 2 * ET + 3)
                nc.vector.tensor_copy(pack[:, :, :, 0], rank[:]).then_inc(rstep, 1)

            @block.tensor
            def _(pe):
                pe.sem_inc(picked, 2)
                with pe.Fori(0, ET) as i:
                    for q in range(2):
                        pe.wait_ge(hit, 2 * i + q + 1)
                        pe.wait_ge(based, 2 * i + q + 1)
                        pe.wait_ge(rstep, 2 * i + q + 1)
                        nc.tensor.matmul(psum[q][:, 0:P], hitT[:, q, :], from_[:, q, :], start=True, stop=True).then_inc(picked, 1)

        filled, placed, sent = sem("filled"), [sem(f"placed{s}") for s in range(4)], sem("sent")
        fenced = sem("fenced")
        with nc.Block() as block:
            @block.gpsimd
            def _(pl):
                def scatter(i):
                    for b in range(2):
                        for q in range(2):
                            s = 2 * b + q
                            wait_uses(pl, placed[s], 16 * i)
                            nc.gpsimd.tensor_copy(slot[:, s, :], pack[:, q, DS(2 * i + b, 1), :].rearrange("p o c -> p (o c)")).then_inc(filled, 1)
                            pl.wait_ge(filled, 4 * i + s + 1)
                            pl.sem_inc(sent, 1)
                            nc.gpsimd.indirect_dma_start(out=t.smeta[q], out_offset=bass.IndirectOffsetOnAxis(ap=slot[:, s, 0:1], axis=0),
                                                         in_=slot[:, s, 1:5], in_offset=None).then_inc(placed[s], 16)

                scatter(0)
                with pl.Fori(1, ET // 2) as i:
                    scatter(i)
                for s in range(4):
                    pl.wait_ge(placed[s], 16 * (ET // 2))

            @block.sync
            def _(sp):
                for q in range(2):
                    sp.dma_start(t.smeta[q][EP:EP + 1, :], zeros[0:1, 0:4].bitcast(I32)).then_inc(fenced, 16)
                sp.wait_ge(fenced, 32)


def index_edges(nc, t):
    with ExitStack() as ctx:
        ctx.enter_context(nc.cleanup_on_exit())
        def sb(name, shape, dt=F32):
            return ctx.enter_context(nc.sbuf_tensor(name, shape, dt))

        def sem(name):
            return nc.alloc_semaphore(name)

        keyf = sb("keyf", [P, 2, ET])
        diag = sb("diag", [P, 4, P])
        slot = sb("islot", [P, 4], I32)
        got = sb("igot", [P, 4, 4], I32)
        end_i = sb("end_i", [ET, 2, 4], I32)
        next_i = sb("next_i", [ET, 2, 4], I32)
        cut_tab = sb("cut_tab", [ET, 2, 4], I32)
        end_f = sb("end_f", [ET, 2])
        next_f = sb("next_f", [ET, 2])
        runs_on = sb("runs_on", [ET, 2])
        final = sb("final", [ET, 2])
        rowf = sb("rowf", [ET, 2])
        limit = sb("limit", [ET, 1])
        spare = sb("spare", [ET, 1])
        destf = sb("destf", [ET, 2])
        diag_end = sb("diag_end", [ET, 2, ET])
        psum = [ctx.enter_context(nc.psum_tensor(f"index_ps{i}", [P, 512], F32)) for i in range(6)]

        back, ends, cut_got, made = sem("back"), sem("ends"), sem("cut_got"), sem("imade")
        step, ended = sem("istep"), sem("iended")
        with nc.Block() as block:
            @block.sync
            def _(sp):
                for q in range(2):
                    sp.dma_start(t.meta[q][:], t.smeta[q][0:EP, :].rearrange("(t p) c -> p t c", p=P)).then_inc(back, 16)
                    sp.dma_start(end_i[:, q, :], t.smeta[q][0:EP, :].rearrange("(t p) c -> p t c", p=P)[P - 1]).then_inc(ends, 16)
                    sp.dma_start(next_i[:, q, :], t.smeta[q][1:EP + 1, :].rearrange("(t p) c -> p t c", p=P)[P - 1]).then_inc(ends, 16)

            @block.gpsimd
            def _(pl):
                nc.gpsimd.iota(limit[:], pattern=[[1, 1]], base=2 * P, channel_multiplier=P, allow_small_or_imprecise_dtypes=True)
                nc.gpsimd.iota(spare[:], pattern=[[1, 1]], base=SPARE, channel_multiplier=1, allow_small_or_imprecise_dtypes=True).then_inc(made, 1)
                pl.wait_ge(ends, 64)
                for q in range(2):
                    nc.gpsimd.indirect_dma_start(out=cut_tab[:, q, :], out_offset=None, in_=t.tab,
                                                 in_offset=bass.IndirectOffsetOnAxis(ap=end_i[:, q, 0:1], axis=0)).then_inc(cut_got, 16)
                pl.wait_ge(cut_got, 32)

            @block.vector
            def _(v):
                n = [0]

                def link(ins):
                    n[0] += 1
                    ins.then_inc(step, 1)
                    v.wait_ge(step, n[0])

                v.wait_ge(back, 32)
                for q in range(2):
                    link(nc.vector.tensor_copy(keyf[:, q, :], t.meta[q][:, :, 0]))
                    link(nc.vector.tensor_copy(t.other[q][:], t.meta[q][:, :, 1]))
                    link(nc.vector.tensor_copy(t.eid[q][:], t.meta[q][:, :, 2]))
                v.wait_ge(ends, 64)
                link(nc.vector.tensor_copy(end_f[:], end_i[:, :, 0]))
                link(nc.vector.tensor_copy(next_f[:], next_i[:, :, 0]))
                link(nc.vector.tensor_tensor(runs_on[:], end_f[:], next_f[:], ALU.is_equal))
                for q in range(2):
                    link(nc.vector.tensor_scalar(diag_end[:, q, :], t.ident[0:ET, 0:ET], end_f[:, q:q + 1], None, ALU.mult))
                v.wait_ge(ended, 1)
                for q in range(2):
                    link(nc.vector.tensor_scalar(t.cut_same[q][:], psum[q][0:ET, 0:ET], end_f[:, q:q + 1], runs_on[:, q:q + 1], ALU.is_equal, ALU.mult))
                v.wait_ge(cut_got, 32)
                v.wait_ge(made, 1)
                for q in range(2):
                    link(nc.vector.tensor_copy(t.cut_rows[q][:], cut_tab[:, q, q:q + 1]))
                    link(nc.vector.tensor_copy(rowf[:, q:q + 1], cut_tab[:, q, q:q + 1]))
                    link(nc.vector.tensor_scalar(final[:, q:q + 1], rowf[:, q:q + 1], limit[:], runs_on[:, q:q + 1], ALU.is_lt, ALU.mult))
                    link(nc.vector.tensor_tensor(destf[:, q:q + 1], rowf[:, q:q + 1], spare[:], ALU.subtract))
                    link(nc.vector.tensor_tensor(destf[:, q:q + 1], destf[:, q:q + 1], final[:, q:q + 1], ALU.mult))
                    link(nc.vector.tensor_tensor(destf[:, q:q + 1], destf[:, q:q + 1], spare[:], ALU.add))
                    link(nc.vector.tensor_copy(t.cut_dest[q][:], destf[:, q:q + 1]))

            @block.tensor
            def _(pe):
                pe.wait_ge(step, 11)
                for q in range(2):
                    mm = nc.tensor.matmul(psum[q][0:ET, 0:ET], t.ones[0:ET, 0:ET], diag_end[:, q, :], start=True, stop=True)
                mm.then_inc(ended, 1)

        diagd, spread, same_made = sem("diagd"), sem("spread"), sem("same_made")
        filled, fetched, kept, sent = sem("ifilled"), [sem(f"fetched{s}") for s in range(4)], sem("kept"), sem("isent")
        with nc.Block() as block:
            @block.vector
            def _(v):
                v.sem_inc(same_made, 4)
                with v.Fori(0, ET // 2) as i:
                    for b in range(2):
                        for q in range(2):
                            s = 2 * b + q
                            v.wait_ge(spread, 4 * i + s + 1)
                            nc.vector.tensor_scalar(diag[:, s, :], t.ident[:], keyf[:, q, DS(2 * i + b, 1)], None, ALU.mult).then_inc(diagd, 1)
                    for b in range(2):
                        for q in range(2):
                            s = 2 * b + q
                            v.wait_ge(spread, 4 * i + s + 5)
                            nc.vector.tensor_scalar(t.same[q][:, DS(2 * i + b, 1), :].rearrange("p o n -> p (o n)"), psum[s][:, 0:P],
                                                    keyf[:, q, DS(2 * i + b, 1)], None, ALU.is_equal).then_inc(same_made, 1)
                    for b in range(2):
                        for q in range(2):
                            s = 2 * b + q
                            v.wait_ge(fetched[s], 16 * (i + 1))
                            nc.vector.tensor_copy(t.etab[q][:, DS(2 * i + b, 1), :].rearrange("p o c -> p (o c)"), got[:, s, :]).then_inc(kept, 1)

            @block.tensor
            def _(pe):
                pe.sem_inc(spread, 4)
                with pe.Fori(0, ET // 2) as i:
                    for s in range(4):
                        pe.wait_ge(diagd, 4 * i + s + 1)
                        pe.wait_ge(same_made, 4 * i + s + 1)
                        nc.tensor.matmul(psum[s][:, 0:P], t.ones[:], diag[:, s, :], start=True, stop=True).then_inc(spread, 1)

            @block.gpsimd
            def _(pl):
                pl.sem_inc(kept, 4)
                with pl.Fori(0, ET // 2) as i:
                    for b in range(2):
                        for q in range(2):
                            s = 2 * b + q
                            pl.wait_ge(kept, 4 * i + s + 1)
                            nc.gpsimd.tensor_copy(slot[:, s:s + 1], t.other[q][:, DS(2 * i + b, 1)]).then_inc(filled, 1)
                            pl.wait_ge(filled, 4 * i + s + 1)
                            pl.sem_inc(sent, 1)
                            nc.gpsimd.indirect_dma_start(out=got[:, s, :], out_offset=None, in_=t.tab,
                                                         in_offset=bass.IndirectOffsetOnAxis(ap=slot[:, s:s + 1], axis=0)).then_inc(fetched[s], 16)

        with nc.Block() as block:
            @block.vector
            def _(v):
                for q in range(2):
                    nc.vector.tensor_copy(t.nlast[q][:], t.etab[q][:, :, 0])
                    for n, what in enumerate((t.other[q][:], t.etab[q][:, :, 0], t.eid[q][:])):
                        nc.vector.tensor_copy(t.fetch[q][:, :, n], what)
                nc.vector.tensor_copy(t.dis_other[:], t.etab[0][:, :, 2].bitcast(F32))


def tile_done(g, k):
    return 4 * g + k + 9


def tile_before(g, k):
    return 4 * g + k + 5


def tiles_two_before(g):
    return 4 * g + 4


def tiles_four_before(g):
    return 4 * g - 4


def group_done(g):
    return g + 3


def group_two_before(g):
    return g + 1


TILE_CREDIT, GROUP_CREDIT = 8, 2


def finish_rsqrt(nc, link, y, half, var, eps):
    link(nc.vector.tensor_tensor(half, y, y, ALU.mult))
    link(nc.vector.scalar_tensor_tensor(half, var, eps, half, ALU.add, ALU.mult))
    link(nc.vector.tensor_scalar(half, half, -0.5, 1.5, ALU.mult, ALU.add))
    link(nc.vector.tensor_tensor(y, y, half, ALU.mult))


def make_norm(nc, ctx, name):
    norm = Tables()

    def sb(what, shape):
        return ctx.enter_context(nc.sbuf_tensor(f"{name}_{what}", shape, F32))

    norm.stats, norm.mv = sb("stats", [P, 2, GT, 6]), sb("mv", [P, 2, GT, 2])
    norm.root, norm.half = sb("root", [P, 2, GT]), sb("half", [P, 2, GT])
    norm.scale, norm.shift = sb("scale", [P, 2, GT]), sb("shift", [P, 2, GT])
    norm.measured, norm.pooling, norm.pooled, norm.rooted, norm.step, norm.ready = (
        nc.alloc_semaphore(f"{name}_{s}") for s in ("measured", "pooling", "pooled", "rooted", "step", "ready"))
    return norm


def norm_credit_vector(v, norm):
    v.sem_inc(norm.measured, TILE_CREDIT)
    v.sem_inc(norm.pooled, TILE_CREDIT)
    v.sem_inc(norm.ready, GROUP_CREDIT)


def norm_credit_scalar(a, norm):
    a.sem_inc(norm.rooted, GROUP_CREDIT)


def norm_statistics(nc, v, norm, x, g, par, tiles):
    for k in range(tiles):
        nc.vector.bn_stats(norm.stats[:, par, k, :], x[:, k, :]).then_inc(norm.measured, 1)
    v.wait_ge(norm.measured, tile_done(g, tiles - 1))
    v.sem_inc(norm.pooling, 1)
    for k in range(tiles):
        nc.vector.bn_aggr(norm.mv[:, par, k, :], norm.stats[:, par, k, :]).then_inc(norm.pooled, 1)


def norm_root(nc, a, norm, t, g, par, tiles):
    a.wait_ge(norm.pooled, tile_done(g, tiles - 1))
    nc.scalar.activation(norm.root[:, par, 0:tiles], norm.mv[:, par, 0:tiles, 1], ACT.Sqrt, bias=t.eps[:]).then_inc(norm.rooted, 1)


def norm_coefficients(nc, v, norm, g, par, tiles, times=None):
    y, half = norm.scale[:, par, 0:tiles], norm.half[:, par, 0:tiles]
    v.wait_ge(norm.rooted, group_done(g))
    steps = 6 if times is not None else 5
    n = [0]

    def link(ins):
        n[0] += 1
        ins.then_inc(norm.step, 1)
        v.wait_ge(norm.step, g * steps + n[0])

    link(nc.vector.reciprocal(y, norm.root[:, par, 0:tiles]))
    finish_rsqrt(nc, link, y, half, norm.mv[:, par, 0:tiles, 1], LN_EPS)
    if times is not None:
        link(nc.vector.tensor_tensor(y, y, times, ALU.mult))
    nc.vector.scalar_tensor_tensor(norm.shift[:, par, 0:tiles], norm.mv[:, par, 0:tiles, 0], -1.0, y, ALU.mult, ALU.mult).then_inc(norm.ready, 1)


def complete_segments(nc, t, q, tables, name):
    with ExitStack() as ctx:
        ctx.enter_context(nc.cleanup_on_exit())
        def sb(what, shape):
            return ctx.enter_context(nc.sbuf_tensor(f"{name}_{what}", shape, F32))

        def sem(what):
            return nc.alloc_semaphore(f"{name}_{what}")

        ends, finals = sb("ends", [ET, D]), sb("finals", [ET, D])
        psum = ctx.enter_context(nc.psum_tensor(f"{name}_ps", [ET, D], F32))
        got, fetched, added, completed, written = sem("got"), sem("fetched"), sem("added"), sem("completed"), sem("written")
        with nc.Block() as block:
            @block.sync
            def _(sp):
                sp.dma_start(ends[:], tables[0:EP, :].rearrange("(t p) d -> p t d", p=P)[P - 1]).then_inc(got, 16)

            @block.gpsimd
            def _(pl):
                nc.gpsimd.indirect_dma_start(out=finals[:], out_offset=None, in_=tables,
                                             in_offset=bass.IndirectOffsetOnAxis(ap=t.cut_rows[q][:, 0:1], axis=0)).then_inc(fetched, 16)
                pl.wait_ge(completed, 1)
                nc.gpsimd.indirect_dma_start(out=tables, out_offset=bass.IndirectOffsetOnAxis(ap=t.cut_dest[q][:, 0:1], axis=0),
                                             in_=finals[:], in_offset=None).then_inc(written, 16)
                pl.wait_ge(written, 16)

            @block.tensor
            def _(pe):
                pe.wait_ge(got, 16)
                nc.tensor.matmul(psum[:], t.cut_same[q][:], ends[:], start=True, stop=True).then_inc(added, 1)

            @block.vector
            def _(v):
                v.wait_ge(added, 1)
                v.wait_ge(fetched, 16)
                nc.vector.tensor_tensor(finals[:], finals[:], psum[:], ALU.add).then_inc(completed, 1)


def sum_segments(nc, t, rows, table, name, normed, times=None):
    q = 0
    with ExitStack() as ctx:
        ctx.enter_context(nc.cleanup_on_exit())
        def sb(what, shape, dt=F32):
            return ctx.enter_context(nc.sbuf_tensor(f"{name}_{what}", shape, dt))

        def sem(what):
            return nc.alloc_semaphore(f"{name}_{what}")

        index = sb("index", [P, 2, GT], I32)
        x = sb("x", [P, 2, GT, D])
        z = sb("z", [P, 2, GT, D]) if normed else x
        high, low = sb("high", [P, 2, GT, D], F32R), sb("low", [P, 2, GT, D], F32R)
        same = sb("same", [P, 2, GT, P], F32R)
        out = sb("out", [P, 2, GT, D])
        psum = [ctx.enter_context(nc.psum_tensor(f"{name}_ps{i}", [P, D], F32)) for i in range(8)]
        norm = make_norm(nc, ctx, name + "n") if normed else None
        indexed, sent = sem("indexed"), sem("sent")
        gathered, stored = [sem(f"gathered{p}") for p in range(2)], [sem(f"stored{p}") for p in range(2)]
        relued, halved, split, widened, summed, copied = (sem(s) for s in ("relued", "halved", "split", "widened", "summed", "copied"))
        used = relued if normed else split

        with nc.Block() as block:
            @block.gpsimd
            def _(pl):
                def fetch(g, par, i):
                    pl.wait_ge(used, tiles_two_before(g))
                    nc.gpsimd.tensor_copy(index[:, par, :], t.other[q][:, DS(g * GT, GT)]).then_inc(indexed, 1)
                    pl.wait_ge(indexed, g + 1)
                    pl.sem_inc(sent, 1)
                    for k in range(GT):
                        nc.gpsimd.indirect_dma_start(out=x[:, par, k, :], out_offset=None, in_=rows,
                                                     in_offset=bass.IndirectOffsetOnAxis(ap=index[:, par, k:k + 1], axis=0)).then_inc(gathered[par], 16)

                edge_groups(pl, fetch, lambda g, par, i, nxt: nxt and fetch(*nxt))

            @block.vector
            def _(v):
                v.sem_inc(halved, TILE_CREDIT)
                v.sem_inc(split, TILE_CREDIT)
                if normed:
                    norm_credit_vector(v, norm)

                def coefficients(g, par, i):
                    if normed:
                        v.wait_ge(gathered[par], 64 * (i + 1))
                        norm_statistics(nc, v, norm, x[:, par], g, par, GT)
                        norm_coefficients(nc, v, norm, g, par, GT, times[:, DS(g * GT, GT)] if times is not None else None)

                def body(g, par, i, nxt):
                    if not normed:
                        v.wait_ge(gathered[par], 64 * (i + 1))
                    elif nxt:
                        coefficients(*nxt)
                    v.wait_ge(summed, tiles_two_before(g))
                    for k in range(GT):
                        if normed:
                            v.wait_ge(relued, tile_done(g, k))
                        nc.vector.tensor_copy(high[:, par, k, :], z[:, par, k, :]).then_inc(halved, 1)
                    for k in range(GT):
                        v.wait_ge(halved, tile_done(g, k))
                        nc.vector.tensor_tensor(low[:, par, k, :], z[:, par, k, :], high[:, par, k, :].bitcast(F32), ALU.subtract).then_inc(split, 1)

                edge_groups(v, coefficients, body)

            @block.scalar
            def _(a):
                a.sem_inc(copied, TILE_CREDIT)
                a.sem_inc(widened, GROUP_CREDIT)
                if normed:
                    norm_credit_scalar(a, norm)
                    a.sem_inc(relued, TILE_CREDIT)

                def prepare(g, par, i):
                    a.wait_ge(summed, tiles_two_before(g))
                    nc.scalar.copy(same[:, par], t.same[q][:, DS(g * GT, GT), :]).then_inc(widened, 1)
                    if normed:
                        norm_root(nc, a, norm, t, g, par, GT)
                        a.wait_ge(norm.ready, group_done(g))
                        a.wait_ge(split, tiles_two_before(g))
                        for k in range(GT):
                            nc.scalar.activation(z[:, par, k, :], x[:, par, k, :], ACT.Relu, bias=norm.shift[:, par, k:k + 1],
                                                 scale=norm.scale[:, par, k:k + 1]).then_inc(relued, 1)

                def body(g, par, i, nxt):
                    if nxt:
                        prepare(*nxt)
                    wait_uses(a, stored[par], 16 * i)
                    for k in range(GT):
                        a.wait_ge(summed, tile_done(g, k))
                        nc.scalar.copy(out[:, par, k, :], psum[4 * par + k][:]).then_inc(copied, 1)

                edge_groups(a, prepare, body)

            @block.tensor
            def _(pe):
                pe.sem_inc(summed, TILE_CREDIT)

                def body(g, par, i, nxt):
                    pe.wait_ge(widened, group_done(g))
                    pe.wait_ge(copied, tiles_two_before(g))
                    for k in range(GT):
                        pe.wait_ge(split, tile_done(g, k))
                        nc.tensor.matmul(psum[4 * par + k][:], same[:, par, k, :], low[:, par, k, :], start=True, stop=False)
                        nc.tensor.matmul(psum[4 * par + k][:], same[:, par, k, :], high[:, par, k, :], start=False, stop=True).then_inc(summed, 1)

                edge_groups(pe, nothing, body)

            @block.sync
            def _(sp):
                def store(g, par, i, nxt):
                    sp.wait_ge(copied, tile_done(g, GT - 1))
                    sp.dma_start(table[DS(g * GR, GR), :].rearrange("(k p) d -> p k d", p=P), out[:, par]).then_inc(stored[par], 16)

                edge_groups(sp, nothing, store)
                for par in range(2):
                    sp.wait_ge(stored[par], 16 * (EG // 2))
    complete_segments(nc, t, q, table, name + "c")


def load_split(nc, parts, name):
    width = max(src.shape[1] * src.shape[2] for src, _, _ in parts)
    with ExitStack() as ctx:
        ctx.enter_context(nc.cleanup_on_exit())
        raw = ctx.enter_context(nc.sbuf_tensor(f"{name}_raw", [P, len(parts), width], F32))
        loaded = nc.alloc_semaphore(f"{name}_loaded")
        halved = nc.alloc_semaphore(f"{name}_halved")
        views = [raw[:, n, 0:s.shape[1] * s.shape[2]].rearrange("p (c n) -> p c n", c=s.shape[1]) for n, (s, _, _) in enumerate(parts)]
        with nc.Block() as block:
            @block.sync
            def _(sp):
                for (src, _, _), view in zip(parts, views):
                    sp.dma_start(view, src).then_inc(loaded, 16)

            @block.vector
            def _(v):
                v.wait_ge(loaded, 16 * len(parts))
                for n, ((_, high, low), view) in enumerate(zip(parts, views)):
                    nc.vector.tensor_copy(high, view).then_inc(halved, 1)
                    v.wait_ge(halved, n + 1)
                    nc.vector.tensor_tensor(low, view, high.bitcast(F32), ALU.subtract)


def column_loads(eng, dst, vectors, sem):
    for n, vec in enumerate(vectors):
        eng.dma_start(dst[:, n, :], vec.rearrange("(c p) -> p c", p=P), allow_slow_non_contiguous=True).then_inc(sem, 16)


def gin_up(nc, t, x, eps, w1, b1, stats):
    with ExitStack() as ctx:
        ctx.enter_context(nc.cleanup_on_exit())
        def sb(what, shape, dt=F32):
            return ctx.enter_context(nc.sbuf_tensor(f"up_{what}", shape, dt))

        def sem(what):
            return nc.alloc_semaphore(f"up_{what}")

        wh, wl = sb("wh", [P, DC, H], F32R), sb("wl", [P, DC, H], F32R)
        load_split(nc, [(w1.rearrange("(c p) n -> p c n", p=P), wh[:], wl[:])], "upw")
        bias, own = sb("bias", [P, 1, HC]), sb("own", [P, 1])
        xin, agg, h = sb("x", [P, 2, GT, D]), sb("agg", [P, 2, GT, D]), sb("h", [P, 2, GT, D])
        ah, al = sb("ah", [P, 2, DC, GR], F32R), sb("al", [P, 2, DC, GR], F32R)
        y = sb("y", [P, HC, GR])
        index = sb("index", [P, 2, GT], I32)
        turn_ps = [ctx.enter_context(nc.psum_tensor(f"up_tps{i}", [P, DC, P], F32)) for i in range(4)]
        y_ps = [ctx.enter_context(nc.psum_tensor(f"up_yps{i}", [P, GR], F32)) for i in range(4)]
        norm = make_norm(nc, ctx, "upn")
        consts, own_ready, indexed, sent = sem("consts"), sem("own_ready"), sem("indexed"), sem("sent")
        loaded, gathered = [sem(f"loaded{p}") for p in range(2)], [sem(f"gathered{p}") for p in range(2)]
        stored = [sem(f"stored{p}") for p in range(2)]
        relued, combined, turned, halved, split = (sem(s) for s in ("relued", "combined", "turned", "halved", "split"))
        produced, biased, measured = sem("produced"), sem("biased"), sem("measured")
        HALF = HC // 2

        with nc.Block() as block:
            @block.sync
            def _(sp):
                column_loads(sp, bias[:], [b1], consts)
                sp.dma_start(own[:], eps.to_broadcast([P, 1])).then_inc(consts, 16)

                def load(g, par, i, slot, lap, tail):
                    sp.wait_ge(relued, tiles_two_before(g))
                    load_group(sp, xin[:, par], x, g, tail, loaded[par])

                each_node_group(sp, load)

            @block.gpsimd
            def _(pl):
                def fetch(g, par, i, slot, lap, tail):
                    pl.wait_ge(turned, tiles_two_before(g))
                    tiles = tiles_of(tail)
                    nc.gpsimd.tensor_copy(index[:, par, 0:tiles], t.last[0][:, DS(g * GT, tiles)]).then_inc(indexed, 1)
                    pl.wait_ge(indexed, g + 1)
                    pl.sem_inc(sent, 1)
                    for k in range(tiles):
                        nc.gpsimd.indirect_dma_start(out=agg[:, par, k, :], out_offset=None, in_=t.seg_in,
                                                     in_offset=bass.IndirectOffsetOnAxis(ap=index[:, par, k:k + 1], axis=0)).then_inc(gathered[par], 16)

                each_node_group(pl, fetch)

            @block.vector
            def _(v):
                v.sem_inc(combined, TILE_CREDIT)
                v.sem_inc(split, TILE_CREDIT)
                v.sem_inc(measured, HC)
                norm_credit_vector(v, norm)
                v.wait_ge(consts, 32)
                nc.vector.tensor_scalar(own[:], own[:], 1.0, None, ALU.add).then_inc(own_ready, 1)

                def combine(g, par, i, slot, lap, tail):
                    tiles = tiles_of(tail)
                    v.wait_ge(loaded[par], loads_done(i, tail))
                    norm_statistics(nc, v, norm, xin[:, par], g, par, tiles)
                    norm_coefficients(nc, v, norm, g, par, tiles)
                    v.wait_ge(gathered[par], 64 * i + 16 * tiles)
                    v.wait_ge(own_ready, 1)
                    for k in range(tiles):
                        v.wait_ge(relued, tile_done(g, k))
                        nc.vector.scalar_tensor_tensor(agg[:, par, k, :], h[:, par, k, :], own[:], agg[:, par, k, :], ALU.mult, ALU.add).then_inc(combined, 1)

                def lows(g, par, tail):
                    for k in range(tiles_of(tail)):
                        v.wait_ge(halved, tile_done(g, k))
                        cols = slice(k * P, (k + 1) * P)
                        nc.vector.tensor_tensor(al[:, par, :, cols], turn_ps[k][:], ah[:, par, :, cols].bitcast(F32), ALU.subtract).then_inc(split, 1)

                def measure_y(g, tail, chunks):
                    for m in chunks:
                        v.wait_ge(biased, HC * g + m + 5)
                        nc.vector.bn_stats(stats[:, m, DS(g, 1), :].rearrange("p o s -> p (o s)"), y[:, m, 0:(TAIL if tail else GR)]).then_inc(measured, 1)

                def start(g, par, i, slot, lap, tail):
                    combine(g, par, i, slot, lap, tail)
                    lows(g, par, tail)

                def body(g, par, i, slot, lap, tail, nxt):
                    if nxt:
                        combine(*nxt)
                    measure_y(g, tail, range(HALF))
                    if nxt:
                        lows(nxt[0], nxt[1], nxt[-1])
                    measure_y(g, tail, range(HALF, HC))

                node_groups(v, start, body)

            @block.scalar
            def _(a):
                norm_credit_scalar(a, norm)
                a.sem_inc(relued, TILE_CREDIT)
                a.sem_inc(halved, TILE_CREDIT)
                a.sem_inc(biased, 4)
                a.wait_ge(consts, 32)

                def apply(g, par, i, slot, lap, tail):
                    norm_root(nc, a, norm, t, g, par, tiles_of(tail))
                    a.wait_ge(norm.ready, group_done(g))
                    a.wait_ge(combined, tiles_two_before(g))
                    for k in range(tiles_of(tail)):
                        nc.scalar.activation(h[:, par, k, :], xin[:, par, k, :], ACT.Relu, bias=norm.shift[:, par, k:k + 1],
                                             scale=norm.scale[:, par, k:k + 1]).then_inc(relued, 1)

                def highs(g, par, tail):
                    a.wait_ge(produced, HC * g + 4)
                    for k in range(tiles_of(tail)):
                        a.wait_ge(turned, tile_done(g, k))
                        nc.scalar.copy(ah[:, par, :, k * P:(k + 1) * P], turn_ps[k][:]).then_inc(halved, 1)

                def finish(g, i, tail, half):
                    cols = TAIL if tail else GR
                    wait_uses(a, stored[half], 16 * g)
                    for m in range(half * HALF, (half + 1) * HALF):
                        a.wait_ge(produced, HC * g + m + HC + 5)
                        a.wait_ge(measured, HC * g + m + 1)
                        nc.scalar.activation(y[:, m, 0:cols], y_ps[m % 4][:, 0:cols], ACT.Identity, bias=bias[:, 0, m:m + 1]).then_inc(biased, 1)
                    a.wait_ge(biased, HC * g + (half + 1) * HALF + 4)
                    a.dma_start(t.y1[DS(g, 1), :, half * HALF:(half + 1) * HALF, 0:cols].rearrange("o p c n -> p (o c) n"),
                                y[:, half * HALF:(half + 1) * HALF, 0:cols]).then_inc(stored[half], 16)

                def start(g, par, i, slot, lap, tail):
                    apply(g, par, i, slot, lap, tail)
                    highs(g, par, tail)

                def body(g, par, i, slot, lap, tail, nxt):
                    if nxt:
                        apply(*nxt)
                    finish(g, i, tail, 0)
                    if nxt:
                        highs(nxt[0], nxt[1], nxt[-1])
                    finish(g, i, tail, 1)

                node_groups(a, start, body)
                for half in range(2):
                    a.wait_ge(stored[half], 16 * NG)

            @block.tensor
            def _(pe):
                pe.sem_inc(turned, TILE_CREDIT)
                pe.sem_inc(produced, HC + 4)

                def turn(g, par, i, slot, lap, tail):
                    for k in range(tiles_of(tail)):
                        pe.wait_ge(combined, tile_done(g, k))
                        pe.wait_ge(split, tile_before(g, k))
                        for c in range(DC):
                            mm = nc.tensor.transpose(turn_ps[k][:, c, :], agg[:, par, k, c * P:(c + 1) * P], t.ident[:])
                        mm.then_inc(turned, 1)

                def product(g, par, tail, chunks):
                    cols = TAIL if tail else GR
                    for m in chunks:
                        pe.wait_ge(biased, HC * g + m + 1)
                        for c in range(DC):
                            mm = product3(nc, y_ps[m % 4][:, 0:cols], wh[:, c, m * P:(m + 1) * P], wl[:, c, m * P:(m + 1) * P],
                                          ah[:, par, c, 0:cols], al[:, par, c, 0:cols], c == 0, c == DC - 1)
                        mm.then_inc(produced, 1)

                def body(g, par, i, slot, lap, tail, nxt):
                    pe.wait_ge(split, tile_done(g, tiles_of(tail) - 1))
                    product(g, par, tail, range(HALF))
                    if nxt:
                        turn(*nxt)
                    product(g, par, tail, range(HALF, HC))

                node_groups(pe, turn, body)


def batch_norm_coefficients(nc, t, stats, gamma, beta, coef, chunks, name):
    with ExitStack() as ctx:
        ctx.enter_context(nc.cleanup_on_exit())
        def sb(what, shape):
            return ctx.enter_context(nc.sbuf_tensor(f"{name}_{what}", shape, F32))

        def sem(what):
            return nc.alloc_semaphore(f"{name}_{what}")

        gb, mv = sb("gb", [P, 2, chunks]), sb("mv", [P, chunks, 2])
        root, half = sb("root", [P, chunks]), sb("half", [P, chunks])
        loaded, step, rooted = sem("loaded"), sem("step"), sem("rooted")
        with nc.Block() as block:
            @block.sync
            def _(sp):
                column_loads(sp, gb[:], [gamma, beta], loaded)

            @block.scalar
            def _(a):
                a.wait_ge(step, chunks)
                nc.scalar.activation(root[:], mv[:, :, 1], ACT.Sqrt, bias=t.eps[:]).then_inc(rooted, 1)

            @block.vector
            def _(v):
                n = [0]

                def link(ins):
                    n[0] += 1
                    ins.then_inc(step, 1)
                    v.wait_ge(step, n[0])

                for m in range(chunks):
                    link(nc.vector.bn_aggr(mv[:, m, :], stats[:, m].rearrange("p g s -> p (g s)")))
                v.wait_ge(rooted, 1)
                v.wait_ge(loaded, 32)
                link(nc.vector.reciprocal(root[:], root[:]))
                finish_rsqrt(nc, link, root[:], half[:], mv[:, :, 1], LN_EPS)
                link(nc.vector.tensor_tensor(coef[:, 0, :], gb[:, 0, :], root[:], ALU.mult))
                link(nc.vector.tensor_tensor(half[:], mv[:, :, 0], coef[:, 0, :], ALU.mult))
                link(nc.vector.tensor_tensor(coef[:, 1, :], gb[:, 1, :], half[:], ALU.subtract))


def gin_down(nc, t, w2, b2, coef, stats):
    with ExitStack() as ctx:
        ctx.enter_context(nc.cleanup_on_exit())
        def sb(what, shape, dt=F32):
            return ctx.enter_context(nc.sbuf_tensor(f"down_{what}", shape, dt))

        def sem(what):
            return nc.alloc_semaphore(f"down_{what}")

        wh, wl = sb("wh", [P, HC, D], F32R), sb("wl", [P, HC, D], F32R)
        load_split(nc, [(w2.rearrange("(c p) n -> p c n", p=P), wh[:], wl[:])], "downw")
        bias = sb("bias", [P, 1, DC])
        z = sb("z", [P, 2, HC, GR])
        zh, zl = sb("zh", [P, HC, GR], F32R), sb("zl", [P, HC, GR], F32R)
        y = sb("y", [P, 2, DC, GR])
        psum = [ctx.enter_context(nc.psum_tensor(f"down_ps{i}", [P, GR], F32)) for i in range(8)]
        consts = sem("consts")
        loaded, stored = [sem(f"loaded{p}") for p in range(2)], [sem(f"stored{p}") for p in range(2)]
        relued, halved, split, used = sem("relued"), sem("halved"), sem("split"), sem("used")
        produced, biased, measured = sem("produced"), sem("biased"), sem("measured")

        with nc.Block() as block:
            @block.sync
            def _(sp):
                column_loads(sp, bias[:], [b2], consts)

                def load(g, par, i, slot, lap, tail):
                    cols = TAIL if tail else GR
                    sp.wait_ge(split, HC * g + HC)
                    sp.dma_start(z[:, par, :, 0:cols], t.y1[DS(g, 1), :, :, 0:cols].rearrange("o p c n -> p (o c) n")).then_inc(loaded[par], 16)

                each_node_group(sp, load)

            @block.scalar
            def _(a):
                a.sem_inc(relued, HC)
                a.sem_inc(biased, TILE_CREDIT)
                a.wait_ge(consts, 16)

                def apply(g, par, i, slot, lap, tail):
                    cols = TAIL if tail else GR
                    a.wait_ge(loaded[par], 16 * (i + 1))
                    for m in range(HC):
                        nc.scalar.activation(z[:, par, m, 0:cols], z[:, par, m, 0:cols], ACT.Relu, bias=coef[:, 1, m:m + 1],
                                             scale=coef[:, 0, m:m + 1]).then_inc(relued, 1)

                def body(g, par, i, slot, lap, tail, nxt):
                    cols = TAIL if tail else GR
                    if nxt:
                        apply(*nxt)
                    wait_uses(a, stored[par], 16 * i)
                    a.wait_ge(measured, tiles_two_before(g))
                    for m in range(DC):
                        a.wait_ge(produced, tile_done(g, m))
                        nc.scalar.activation(y[:, par, m, 0:cols], psum[4 * par + m][:, 0:cols], ACT.Identity, bias=bias[:, 0, m:m + 1]).then_inc(biased, 1)
                    a.wait_ge(biased, tile_done(g, DC - 1))
                    a.dma_start(t.y2[DS(g, 1), :, :, 0:cols].rearrange("o p c n -> p (o c) n"), y[:, par, :, 0:cols]).then_inc(stored[par], 16)

                node_groups(a, apply, body)
                for par in range(2):
                    a.wait_ge(stored[par], 16 * (NG // 2))

            @block.vector
            def _(v):
                v.sem_inc(halved, HC)
                v.sem_inc(split, 2 * HC)
                v.sem_inc(measured, TILE_CREDIT)

                def halve(g, par, i, slot, lap, tail):
                    cols = TAIL if tail else GR
                    for m in range(HC):
                        v.wait_ge(relued, HC * g + m + HC + 1)
                        if m < HC - 1:
                            v.wait_ge(used, (HC - 1) * g + m + 1)
                        else:
                            v.wait_ge(produced, tile_before(g, DC - 1))
                        nc.vector.tensor_copy(zh[:, m, 0:cols], z[:, par, m, 0:cols]).then_inc(halved, 1)
                        if m > 0:
                            lower(g, par, m - 1, cols)
                    lower(g, par, HC - 1, cols)

                def lower(g, par, m, cols):
                    v.wait_ge(halved, HC * g + m + HC + 1)
                    nc.vector.tensor_tensor(zl[:, m, 0:cols], z[:, par, m, 0:cols], zh[:, m, 0:cols].bitcast(F32), ALU.subtract).then_inc(split, 1)

                def body(g, par, i, slot, lap, tail, nxt):
                    if nxt:
                        halve(*nxt)
                    for m in range(DC):
                        v.wait_ge(biased, tile_done(g, m))
                        nc.vector.bn_stats(stats[:, m, DS(g, 1), :].rearrange("p o s -> p (o s)"), y[:, par, m, 0:(TAIL if tail else GR)]).then_inc(measured, 1)

                node_groups(v, halve, body)

            @block.tensor
            def _(pe):
                pe.sem_inc(used, HC - 1)
                pe.sem_inc(produced, TILE_CREDIT)

                def body(g, par, i, slot, lap, tail, nxt):
                    cols = TAIL if tail else GR
                    pe.wait_ge(biased, tiles_two_before(g))
                    for c in range(HC):
                        pe.wait_ge(split, HC * g + c + 2 * HC + 1)
                        for m in range(DC):
                            mm = product3(nc, psum[4 * par + m][:, 0:cols], wh[:, c, m * P:(m + 1) * P], wl[:, c, m * P:(m + 1) * P],
                                          zh[:, c, 0:cols], zl[:, c, 0:cols], c == 0, c == HC - 1)
                            if c == HC - 1:
                                mm.then_inc(produced, 1)
                            elif m == DC - 1:
                                mm.then_inc(used, 1)

                node_groups(pe, nothing, body)


def gin_out(nc, t, x, coef):
    with ExitStack() as ctx:
        ctx.enter_context(nc.cleanup_on_exit())
        def sb(what, shape, dt=F32):
            return ctx.enter_context(nc.sbuf_tensor(f"out_{what}", shape, dt))

        def sem(what):
            return nc.alloc_semaphore(f"out_{what}")

        xin, h, u = sb("x", [P, 4, GT, D]), sb("h", [P, 2, GT, D]), sb("u", [P, 4, DC, GR])
        out = sb("out", [P, 2, GT, D])
        psum = [ctx.enter_context(nc.psum_tensor(f"out_ps{i}", [P, DC, P], F32)) for i in range(8)]
        norm = make_norm(nc, ctx, "outn")
        loaded, stored = [sem(f"loaded{s}") for s in range(4)], [sem(f"stored{p}") for p in range(2)]
        u_loaded = [sem(f"u_loaded{s}") for s in range(4)]
        activated, relued, turned, added, finished = (sem(s) for s in ("activated", "relued", "turned", "added", "finished"))

        with nc.Block() as block:
            @block.sync
            def _(sp):
                def load(g, par, i, slot, lap, tail):
                    cols = TAIL if tail else GR
                    wait_uses(sp, finished, tiles_four_before(g))
                    load_group(sp, xin[:, slot], x, g, tail, loaded[slot])
                    wait_uses(sp, turned, tiles_four_before(g))
                    sp.dma_start(u[:, slot, :, 0:cols], t.y2[DS(g, 1), :, :, 0:cols].rearrange("o p c n -> p (o c) n")).then_inc(u_loaded[slot], 16)

                each_node_group(sp, load)

            @block.scalar
            def _(a):
                norm_credit_scalar(a, norm)
                a.sem_inc(activated, TILE_CREDIT)
                a.sem_inc(relued, TILE_CREDIT)

                def apply(g, par, i, slot, lap, tail):
                    cols = TAIL if tail else GR
                    a.wait_ge(u_loaded[slot], 16 * (lap + 1))
                    for c in range(DC):
                        nc.scalar.activation(u[:, slot, c, 0:cols], u[:, slot, c, 0:cols], ACT.Relu, bias=coef[:, 1, c:c + 1],
                                             scale=coef[:, 0, c:c + 1]).then_inc(activated, 1)
                    norm_root(nc, a, norm, t, g, par, tiles_of(tail))
                    a.wait_ge(norm.ready, group_done(g))
                    a.wait_ge(added, tiles_two_before(g))
                    for k in range(tiles_of(tail)):
                        nc.scalar.activation(h[:, par, k, :], xin[:, slot, k, :], ACT.Relu, bias=norm.shift[:, par, k:k + 1],
                                             scale=norm.scale[:, par, k:k + 1]).then_inc(relued, 1)

                def body(g, par, i, slot, lap, tail, nxt):
                    if nxt:
                        apply(*nxt)
                    a.wait_ge(finished, tile_done(g, tiles_of(tail) - 1))
                    store_group(a, t.x1, out[:, par], g, tail, stored[par])

                node_groups(a, apply, body)
                a.wait_ge(stored[0], 16 * (NG // 2))
                a.wait_ge(stored[1], 16 * (NG // 2 + 1))

            @block.tensor
            def _(pe):
                pe.sem_inc(turned, TILE_CREDIT)

                def body(g, par, i, slot, lap, tail, nxt):
                    pe.wait_ge(activated, tile_done(g, DC - 1))
                    pe.wait_ge(added, tiles_two_before(g))
                    for k in range(tiles_of(tail)):
                        for c in range(DC):
                            mm = nc.tensor.transpose(psum[4 * par + k][:, c, :], u[:, slot, c, k * P:(k + 1) * P], t.ident[:])
                        mm.then_inc(turned, 1)

                node_groups(pe, nothing, body)

            @block.vector
            def _(v):
                norm_credit_vector(v, norm)
                v.sem_inc(added, TILE_CREDIT)
                v.sem_inc(finished, TILE_CREDIT)

                def measure(g, par, i, slot, lap, tail):
                    v.wait_ge(loaded[slot], loads_done(lap, tail))
                    norm_statistics(nc, v, norm, xin[:, slot], g, par, tiles_of(tail))
                    norm_coefficients(nc, v, norm, g, par, tiles_of(tail))

                def body(g, par, i, slot, lap, tail, nxt):
                    if nxt:
                        measure(*nxt)
                    tiles = tiles_of(tail)
                    wait_uses(v, stored[par], 16 * i)
                    for k in range(tiles):
                        v.wait_ge(turned, tile_done(g, k))
                        v.wait_ge(relued, tile_done(g, k))
                        nc.vector.tensor_tensor(h[:, par, k, :], h[:, par, k, :], psum[4 * par + k][:].rearrange("p c n -> p (c n)"), ALU.add).then_inc(added, 1)
                    for k in range(tiles):
                        v.wait_ge(added, tile_done(g, k))
                        nc.vector.tensor_tensor(out[:, par, k, :], xin[:, slot, k, :], h[:, par, k, :], ALU.add).then_inc(finished, 1)

                node_groups(v, measure, body)


def row_broadcast(eng, dst, vec, sem):
    eng.dma_start(dst, vec.rearrange("(o d) -> o d", o=1).to_broadcast([P, vec.shape[0]])).then_inc(sem, 16)


def gcn(nc, t, layer, rows, w, b, out_rows, residual=None):
    normed = layer == 0
    name = f"gcn{layer}"
    with ExitStack() as ctx:
        ctx.enter_context(nc.cleanup_on_exit())
        def sb(what, shape, dt=F32):
            return ctx.enter_context(nc.sbuf_tensor(f"{name}_{what}", shape, dt))

        def sem(what):
            return nc.alloc_semaphore(f"{name}_{what}")

        wh, wl = sb("wh", [P, DC, D], F32R), sb("wl", [P, DC, D], F32R)
        load_split(nc, [(w.rearrange("(c p) n -> p c n", p=P), wh[:], wl[:])], name + "w")
        bias = sb("bias", [P, D])
        xin, agg = sb("x", [P, 4, GT, D]), sb("agg", [P, 2, GT, D])
        s = sb("s", [P, 2, GT, D]) if normed else None
        res = sb("res", [P, 2, GT, D]) if residual is not None else None
        ah, al = sb("ah", [P, 2, GT, DC, P], F32R), sb("al", [P, 2, GT, DC, P], F32R)
        tmp, out = sb("tmp", [P, GT, D]), sb("out", [P, 2, GT, D])
        index = sb("index", [P, 2, GT], I32)
        turn_ps = [ctx.enter_context(nc.psum_tensor(f"{name}_tps{i}", [P, DC, P], F32)) for i in range(4)]
        row_ps = [ctx.enter_context(nc.psum_tensor(f"{name}_rps{i}", [P, D], F32)) for i in range(4)]
        norm = make_norm(nc, ctx, name + "n") if normed else None
        consts, indexed, sent = sem("consts"), sem("indexed"), sem("sent")
        loaded, gathered = [sem(f"loaded{s}") for s in range(4)], [sem(f"gathered{p}") for p in range(2)]
        res_loaded, stored = [sem(f"res_loaded{p}") for p in range(2)], [sem(f"stored{p}") for p in range(2)]
        relued, combined, turned, halved, split = (sem(n) for n in ("relued", "combined", "turned", "halved", "split"))
        produced, scaled, finished = sem("produced"), sem("scaled"), sem("finished")
        used = relued if normed else combined

        with nc.Block() as block:
            @block.sync
            def _(sp):
                row_broadcast(sp, bias[:], b, consts)

                def load(g, par, i, slot, lap, tail):
                    wait_uses(sp, used, tiles_four_before(g))
                    load_group(sp, xin[:, slot], rows, g, tail, loaded[slot])
                    if residual is not None:
                        sp.wait_ge(finished, tiles_two_before(g))
                        load_group(sp, res[:, par], residual, g, tail, res_loaded[par])

                each_node_group(sp, load)

            @block.gpsimd
            def _(pl):
                def fetch(g, par, i, slot, lap, tail):
                    tiles = tiles_of(tail)
                    pl.wait_ge(turned, tiles_two_before(g))
                    nc.gpsimd.tensor_copy(index[:, par, 0:tiles], t.last[0][:, DS(g * GT, tiles)]).then_inc(indexed, 1)
                    pl.wait_ge(indexed, g + 1)
                    pl.sem_inc(sent, 1)
                    for k in range(tiles):
                        nc.gpsimd.indirect_dma_start(out=agg[:, par, k, :], out_offset=None, in_=t.seg_in,
                                                     in_offset=bass.IndirectOffsetOnAxis(ap=index[:, par, k:k + 1], axis=0)).then_inc(gathered[par], 16)

                each_node_group(pl, fetch)

            @block.vector
            def _(v):
                v.sem_inc(combined, TILE_CREDIT)
                v.sem_inc(split, TILE_CREDIT)
                v.sem_inc(scaled, TILE_CREDIT)
                if normed:
                    norm_credit_vector(v, norm)
                else:
                    v.sem_inc(finished, TILE_CREDIT)
                v.wait_ge(consts, 16)

                def combine(g, par, i, slot, lap, tail):
                    tiles = tiles_of(tail)
                    v.wait_ge(loaded[slot], loads_done(lap, tail))
                    if normed:
                        norm_statistics(nc, v, norm, xin[:, slot], g, par, tiles)
                        norm_coefficients(nc, v, norm, g, par, tiles, t.dis[:, DS(g * GT, tiles)])
                    v.wait_ge(gathered[par], 64 * i + 16 * tiles)
                    for k in range(tiles):
                        if normed:
                            v.wait_ge(relued, tile_done(g, k))
                        nc.vector.tensor_tensor(agg[:, par, k, :], agg[:, par, k, :], (s[:, par, k, :] if normed else xin[:, slot, k, :]), ALU.add).then_inc(combined, 1)

                def lower(g, par, i, slot, lap, tail):
                    for k in range(tiles_of(tail)):
                        v.wait_ge(halved, tile_done(g, k))
                        nc.vector.tensor_tensor(al[:, par, k], turn_ps[k][:], ah[:, par, k].bitcast(F32), ALU.subtract).then_inc(split, 1)

                def start(g, par, i, slot, lap, tail):
                    combine(g, par, i, slot, lap, tail)
                    lower(g, par, i, slot, lap, tail)

                def body(g, par, i, slot, lap, tail, nxt):
                    if nxt:
                        combine(*nxt)
                    if not normed:
                        wait_uses(v, stored[par], 16 * i)
                        v.wait_ge(res_loaded[par], loads_done(i, tail))
                    for k in range(tiles_of(tail)):
                        v.wait_ge(produced, tile_done(g, k))
                        v.wait_ge(finished, tile_before(g, k))
                        nc.vector.scalar_tensor_tensor(tmp[:, k, :], row_ps[k][:], t.dis[:, DS(g * GT + k, 1)], bias[:], ALU.mult, ALU.add).then_inc(scaled, 1)
                    if nxt:
                        lower(*nxt)
                    if not normed:
                        for k in range(tiles_of(tail)):
                            v.wait_ge(scaled, tile_done(g, k))
                            nc.vector.tensor_tensor(out[:, par, k, :], tmp[:, k, :], res[:, par, k, :], ALU.add).then_inc(finished, 1)

                node_groups(v, start, body)

            @block.scalar
            def _(a):
                a.sem_inc(halved, TILE_CREDIT)
                if normed:
                    a.sem_inc(relued, TILE_CREDIT)
                    a.sem_inc(finished, TILE_CREDIT)
                    norm_credit_scalar(a, norm)

                def apply(g, par, i, slot, lap, tail):
                    if normed:
                        norm_root(nc, a, norm, t, g, par, tiles_of(tail))
                        a.wait_ge(norm.ready, group_done(g))
                        a.wait_ge(combined, tiles_two_before(g))
                        for k in range(tiles_of(tail)):
                            nc.scalar.activation(s[:, par, k, :], xin[:, slot, k, :], ACT.Relu, bias=norm.shift[:, par, k:k + 1],
                                                 scale=norm.scale[:, par, k:k + 1]).then_inc(relued, 1)

                def higher(g, par, i, slot, lap, tail):
                    a.wait_ge(produced, tiles_two_before(g))
                    for k in range(tiles_of(tail)):
                        a.wait_ge(turned, tile_done(g, k))
                        nc.scalar.copy(ah[:, par, k], turn_ps[k][:]).then_inc(halved, 1)

                def start(g, par, i, slot, lap, tail):
                    apply(g, par, i, slot, lap, tail)
                    higher(g, par, i, slot, lap, tail)

                def body(g, par, i, slot, lap, tail, nxt):
                    if nxt:
                        apply(*nxt)
                    if normed:
                        wait_uses(a, stored[par], 16 * i)
                        for k in range(tiles_of(tail)):
                            a.wait_ge(scaled, tile_done(g, k))
                            nc.scalar.activation(out[:, par, k, :], tmp[:, k, :], ACT.Relu, scale=t.dis[:, DS(g * GT + k, 1)]).then_inc(finished, 1)
                    if nxt:
                        higher(*nxt)
                    a.wait_ge(finished, tile_done(g, tiles_of(tail) - 1))
                    store_group(a, out_rows, out[:, par], g, tail, stored[par])

                node_groups(a, start, body)
                a.wait_ge(stored[0], 16 * (NG // 2))
                a.wait_ge(stored[1], 16 * (NG // 2 + 1))

            @block.tensor
            def _(pe):
                pe.sem_inc(turned, TILE_CREDIT)
                pe.sem_inc(produced, TILE_CREDIT)

                def turn(g, par, i, slot, lap, tail):
                    for k in range(tiles_of(tail)):
                        pe.wait_ge(combined, tile_done(g, k))
                        pe.wait_ge(split, tile_before(g, k))
                        for c in range(DC):
                            mm = nc.tensor.transpose(turn_ps[k][:, c, :], agg[:, par, k, c * P:(c + 1) * P], t.ident[:])
                        mm.then_inc(turned, 1)

                def body(g, par, i, slot, lap, tail, nxt):
                    for k in range(tiles_of(tail)):
                        pe.wait_ge(split, tile_done(g, k))
                        pe.wait_ge(scaled, tile_before(g, k))
                        for c in range(DC):
                            mm = product3(nc, row_ps[k][:], ah[:, par, k, c, :], al[:, par, k, c, :], wh[:, c, :], wl[:, c, :], c == 0, c == DC - 1)
                        mm.then_inc(produced, 1)
                    if nxt:
                        turn(*nxt)

                node_groups(pe, turn, body)


BT = ET // 2
TERMS = 8
BG = BT // GT


def path_products(nc, t, rows, edge_attr, paths, coeffs):
    with ExitStack() as ctx:
        ctx.enter_context(nc.cleanup_on_exit())

        def sb(what, shape, dt=F32):
            return ctx.enter_context(nc.sbuf_tensor(f"path_{what}", shape, dt))

        def sem(what):
            return nc.alloc_semaphore(f"path_{what}")

        h, attr, o = sb("h", [P, BT, D]), sb("attr", [P, BT, D]), sb("o", [P, BT, D])
        term = sb("term", [P, TERMS, BT, EXT])
        high, low = sb("high", [P, GT, D], F32R), sb("low", [P, GT, D], F32R)
        same = sb("same", [P, GT, P], F32R)
        out = sb("out", [P, GT, D])
        coef, ids, code = sb("coef", [P, PATHS]), sb("ids", [1, PATHS, 3], I32), sb("code", [1, PATHS // 2], I32)
        code_f = sb("code_f", [1, 2, PATHS])
        psum = [ctx.enter_context(nc.psum_tensor(f"path_ps{i}", [P, D], F32)) for i in range(4)]
        norm = make_norm(nc, ctx, "pathn")
        consts, coded, coded_step = sem("consts"), sem("coded"), sem("coded_step")
        gathered, stored = [sem(f"gathered{b}") for b in range(BG)], sem("stored")
        relued, cleared, multiplied, accumulated = sem("relued"), sem("cleared"), sem("multiplied"), sem("accumulated")
        halved, split, widened, summed, copied = (sem(s) for s in ("halved", "split", "widened", "summed", "copied"))
        ALL = 2 * BG

        with nc.Block() as block:
            @block.sync
            def _(sp):
                sp.dma_start(coef[:], coeffs.rearrange("(o d) -> o d", o=1).to_broadcast([P, PATHS])).then_inc(consts, 16)
                sp.dma_start(ids[:].rearrange("o a b -> o (a b)"), paths.rearrange("(o a) b -> o (a b)", o=1)).then_inc(consts, 16)
                for g in range(ALL):
                    sp.wait_ge(copied, GT * (g + 1))
                    sp.dma_start(t.seg_in[g * GR:(g + 1) * GR, :].rearrange("(k p) d -> p k d", p=P), out[:]).then_inc(stored, 16)
                sp.wait_ge(stored, 16 * ALL)

            @block.gpsimd
            def _(pl):
                for batch in range(2):
                    if batch:
                        pl.wait_ge(accumulated, PATHS + TERMS)
                    for b in range(BG):
                        for k in range(b * GT, (b + 1) * GT):
                            col = batch * BT + k
                            nc.gpsimd.indirect_dma_start(out=h[:, k, :], out_offset=None, in_=rows,
                                                         in_offset=bass.IndirectOffsetOnAxis(ap=t.other[0][:, col:col + 1], axis=0)).then_inc(gathered[b], 16)
                            nc.gpsimd.indirect_dma_start(out=attr[:, k, :], out_offset=None, in_=edge_attr,
                                                         in_offset=bass.IndirectOffsetOnAxis(ap=t.eid[0][:, col:col + 1], axis=0)).then_inc(gathered[b], 16)
                    if batch:
                        pl.wait_ge(split, BT)
                    nc.gpsimd.memset(o[:], 0.0).then_inc(cleared, 1)

            @block.vector
            def _(v):
                norm_credit_vector(v, norm)
                v.sem_inc(accumulated, TERMS)
                v.wait_ge(consts, 32)
                nc.vector.tensor_scalar(code_f[:, 0], ids[:, :, 2], float(SEG), None, ALU.mult).then_inc(coded_step, 1)
                v.wait_ge(coded_step, 1)
                nc.vector.tensor_tensor(code_f[:, 1], code_f[:, 0], ids[:, :, 1], ALU.add).then_inc(coded_step, 1)
                v.wait_ge(coded_step, 2)
                nc.vector.tensor_scalar(code_f[:, 0], code_f[:, 1], float(SEG), None, ALU.mult).then_inc(coded_step, 1)
                v.wait_ge(coded_step, 3)
                nc.vector.tensor_tensor(code_f[:, 1], code_f[:, 0], ids[:, :, 0], ALU.add).then_inc(coded_step, 1)
                v.wait_ge(coded_step, 4)
                pairs = code_f[:, 1].rearrange("o (a two) -> o a two", two=2)
                nc.vector.tensor_scalar(code_f[:, 0, 0:PATHS // 2], pairs[:, :, 1], float(SEG ** 3), None, ALU.mult).then_inc(coded_step, 1)
                v.wait_ge(coded_step, 5)
                nc.vector.tensor_tensor(code[:], code_f[:, 0, 0:PATHS // 2], pairs[:, :, 0], ALU.add).then_inc(coded_step, 1)
                v.wait_ge(coded_step, 6)
                hv, av, ov = (x[:].rearrange("p t (s k) -> p t s k", k=EXT) for x in (h, attr, o))
                for batch in range(2):
                    for b in range(BG):
                        g = batch * BG + b
                        v.wait_ge(gathered[b], 2 * GT * 16 * (batch + 1))
                        norm_statistics(nc, v, norm, h[:, b * GT:(b + 1) * GT], g, g % 2, GT)
                        norm_coefficients(nc, v, norm, g, g % 2, GT)
                    v.wait_ge(relued, BT * (batch + 1))
                    v.wait_ge(cleared, batch + 1)
                    with v.Fori(0, PATHS // TERMS) as i:
                        path = TERMS * i
                        done = PATHS * batch + path
                        third = []

                        def multiply(j):
                            if j % 2 == 0:
                                word.append(v.value_load(code[0:1, DS(i * (TERMS // 2) + j // 2, 1)], min_val=0, max_val=SEG ** 6 - 1))
                            own = word[-1] % SEG ** 3 if j % 2 == 0 else word[-1] // SEG ** 3
                            first, second = own % SEG, (own // SEG) % SEG
                            third.append(own // SEG ** 2)
                            v.wait_ge(accumulated, done + j + 1)
                            nc.vector.scalar_tensor_tensor(term[:, j], hv[:, :, DS(first, 1), :].rearrange("p t o k -> p t (o k)"), coef[:, DS(path + j, 1)],
                                                           av[:, :, DS(second, 1), :].rearrange("p t o k -> p t (o k)"), ALU.mult, ALU.mult).then_inc(multiplied, 1)

                        word = []
                        multiply(0)
                        for j in range(TERMS):
                            if j + 1 < TERMS:
                                multiply(j + 1)
                            v.wait_ge(multiplied, done + j + 1)
                            v.wait_ge(accumulated, done + j + TERMS)
                            there = ov[:, :, DS(third[j], 1), :].rearrange("p t o k -> p t (o k)")
                            nc.vector.tensor_tensor(there, there, term[:, j], ALU.add).then_inc(accumulated, 1)
                    for b in range(BG):
                        g = batch * BG + b
                        for k in range(GT):
                            n = GT * g + k + 1
                            v.wait_ge(halved, n)
                            nc.vector.tensor_tensor(low[:, k, :], o[:, b * GT + k, :], high[:, k, :].bitcast(F32), ALU.subtract).then_inc(split, 1)

            @block.scalar
            def _(a):
                norm_credit_scalar(a, norm)
                for batch in range(2):
                    for b in range(BG):
                        g = batch * BG + b
                        norm_root(nc, a, norm, t, g, g % 2, GT)
                        a.wait_ge(norm.ready, group_done(g))
                        for k in range(GT):
                            n = b * GT + k
                            nc.scalar.activation(h[:, n, :], h[:, n, :], ACT.Relu, bias=norm.shift[:, g % 2, k:k + 1],
                                                 scale=norm.scale[:, g % 2, k:k + 1]).then_inc(relued, 1)
                    a.wait_ge(accumulated, PATHS * (batch + 1) + TERMS)
                    for b in range(BG):
                        g = batch * BG + b
                        if g:
                            a.wait_ge(summed, GT * g)
                        nc.scalar.copy(same[:], t.same[0][:, g * GT:(g + 1) * GT, :]).then_inc(widened, 1)
                        for k in range(GT):
                            nc.scalar.copy(high[:, k, :], o[:, b * GT + k, :]).then_inc(halved, 1)
                        if g:
                            wait_uses(a, stored, 16 * g)
                        for k in range(GT):
                            a.wait_ge(summed, GT * g + k + 1)
                            nc.scalar.copy(out[:, k, :], psum[k][:]).then_inc(copied, 1)

            @block.tensor
            def _(pe):
                for g in range(ALL):
                    pe.wait_ge(widened, g + 1)
                    for k in range(GT):
                        n = GT * g + k + 1
                        pe.wait_ge(split, n)
                        if g:
                            pe.wait_ge(copied, n - GT)
                        nc.tensor.matmul(psum[k][:], same[:, k, :], low[:, k, :], start=True, stop=False)
                        nc.tensor.matmul(psum[k][:], same[:, k, :], high[:, k, :], start=False, stop=True).then_inc(summed, 1)
    complete_segments(nc, t, 0, t.seg_in, "pathc")


def fold_weights(nc, t, wo_w, wi_w, ws_w, mlp_w, wo_b, wi_b, ws_b, mlp_b, folded, const_halves):
    with ExitStack() as ctx:
        ctx.enter_context(nc.cleanup_on_exit())

        def sb(what, shape, dt=F32):
            return ctx.enter_context(nc.sbuf_tensor(f"fold_{what}", shape, dt))

        def sem(what):
            return nc.alloc_semaphore(f"fold_{what}")

        mlp, mlp_t = sb("mlp", [P, DC, 2 * D]), sb("mlp_t", [P, 2 * DC, D])
        w = sb("w", [P, 3, DC, D])
        bcol, bsum, wide = sb("bcol", [P, 3, DC]), sb("bsum", [P, 2, DC]), sb("wide", [P, 2 * DC, P])
        brow = sb("brow", [1, D])
        psum = [ctx.enter_context(nc.psum_tensor(f"fold_ps{i}", [P, D], F32)) for i in range(8)]
        loaded, turned, copied, produced, halved, split = (sem(s) for s in ("loaded", "turned", "copied", "produced", "halved", "split"))
        step, constant, summed = sem("step"), sem("constant"), sem("summed")
        order = [(n, c) for n in range(3) for c in range(DC)]

        with nc.Block() as block:
            @block.sync
            def _(sp):
                sp.dma_start(mlp[:], mlp_w.rearrange("(c p) n -> p c n", p=P)).then_inc(loaded, 16)
                for n, x in enumerate((ws_w, wo_w, wi_w)):
                    sp.dma_start(w[:, n], x.rearrange("(c p) n -> p c n", p=P)).then_inc(loaded, 16)
                column_loads(sp, bcol[:], [ws_b, wo_b, wi_b], loaded)
                sp.dma_start(brow[:], mlp_b.rearrange("(o d) -> o d", o=1)).then_inc(loaded, 16)

            @block.tensor
            def _(pe):
                pe.wait_ge(loaded, 128)
                for j in range(2 * DC):
                    for m in range(DC):
                        mm = nc.tensor.transpose(psum[j][:, m * P:(m + 1) * P], mlp[:, m, j * P:(j + 1) * P], t.ident[:])
                    mm.then_inc(turned, 1)
                pe.wait_ge(copied, 2 * DC)
                for i, (n, c) in enumerate(order):
                    if i >= 4:
                        pe.wait_ge(split, i - 3)
                    for j in range(DC):
                        mm = nc.tensor.matmul(psum[i % 4][:], w[:, n, j, c * P:(c + 1) * P], mlp_t[:, (DC if n else 0) + j, :], start=j == 0, stop=j == DC - 1)
                    mm.then_inc(produced, 1)
                pe.wait_ge(step, 3)
                for j in range(2 * DC):
                    mm = nc.tensor.matmul(psum[7][:], wide[:, j, :], mlp_t[:, j, :], start=j == 0, stop=j == 2 * DC - 1)
                mm.then_inc(constant, 1)

            @block.scalar
            def _(a):
                for j in range(2 * DC):
                    a.wait_ge(turned, j + 1)
                    nc.scalar.copy(mlp_t[:, j, :], psum[j][:]).then_inc(copied, 1)
                for i, (n, c) in enumerate(order):
                    a.wait_ge(produced, i + 1)
                    nc.scalar.copy(folded[n][0][:, c, :], psum[i % 4][:]).then_inc(halved, 1)

            @block.vector
            def _(v):
                v.wait_ge(loaded, 128)
                nc.vector.tensor_copy(bsum[:, 0], bcol[:, 0])
                nc.vector.tensor_tensor(bsum[:, 1], bcol[:, 1], bcol[:, 2], ALU.add).then_inc(step, 1)
                v.wait_ge(step, 1)
                nc.vector.tensor_copy(wide[:], bsum[:].rearrange("p a (c o) -> p (a c) o", o=1).to_broadcast([P, 2 * DC, P])).then_inc(step, 2)
                for i, (n, c) in enumerate(order):
                    v.wait_ge(halved, i + 1)
                    nc.vector.tensor_tensor(folded[n][1][:, c, :], psum[i % 4][:], folded[n][0][:, c, :].bitcast(F32), ALU.subtract).then_inc(split, 1)
                v.wait_ge(constant, 1)
                const_high, const_low = const_halves
                nc.vector.tensor_tensor(brow[:], psum[7][0:1, :], brow[:], ALU.add).then_inc(summed, 1)
                v.wait_ge(summed, 1)
                nc.vector.tensor_copy(const_high[:], brow[:]).then_inc(summed, 1)
                v.wait_ge(summed, 2)
                nc.vector.tensor_tensor(const_low[:], brow[:], const_high[:].bitcast(F32), ALU.subtract)


def sum_messages(nc, t, q, rows, edge_attr, weight, table, name):
    with ExitStack() as ctx:
        ctx.enter_context(nc.cleanup_on_exit())

        def sb(what, shape, dt=F32):
            return ctx.enter_context(nc.sbuf_tensor(f"{name}_{what}", shape, dt))

        def sem(what):
            return nc.alloc_semaphore(f"{name}_{what}")

        index = sb("index", [P, 2, GT, 3], I32)
        x, attr = sb("x", [P, 2, GT, D]), sb("attr", [P, 2, GT, D])
        high, low = sb("high", [P, GT, D], F32R), sb("low", [P, GT, D], F32R)
        same = sb("same", [P, 2, GT, P], F32R)
        ah, al = sb("ah", [P, GT, DC, P], F32R), sb("al", [P, GT, DC, P], F32R)
        out = sb("out", [P, 2, GT, D])
        turn_ps = [ctx.enter_context(nc.psum_tensor(f"{name}_tps{i}", [P, DC, P], F32)) for i in range(4)]
        row_ps = [ctx.enter_context(nc.psum_tensor(f"{name}_rps{i}", [P, D], F32)) for i in range(4)]
        norm = make_norm(nc, ctx, name + "n")
        wh, wl = weight
        indexed, sent = sem("indexed"), sem("sent")
        x_got, attr_got = [sem(f"x_got{p}") for p in range(2)], [sem(f"attr_got{p}") for p in range(2)]
        stored = [sem(f"stored{p}") for p in range(2)]
        x_added = [sem(f"x_added{p}") for p in range(2)]
        relued, formed, halved, split = (sem(s) for s in ("relued", "formed", "halved", "split"))
        widened, summed, t_halved, t_split, produced, copied = (sem(s) for s in ("widened", "summed", "t_halved", "t_split", "produced", "copied"))

        with nc.Block() as block:
            @block.gpsimd
            def _(pl):
                def fetch(g, par, i):
                    pl.wait_ge(split, tiles_two_before(g))
                    nc.gpsimd.tensor_copy(index[:, par], t.fetch[q][:, DS(g * GT, GT), :]).then_inc(indexed, 1)
                    pl.wait_ge(indexed, g + 1)
                    pl.sem_inc(sent, 1)

                    def gather(dst, what, n, done, **how):
                        for k in range(GT):
                            nc.gpsimd.indirect_dma_start(out=dst[:, par, k, :], out_offset=None, in_=what,
                                                         in_offset=bass.IndirectOffsetOnAxis(ap=index[:, par, k, n:n + 1], axis=0), **how).then_inc(done[par], 16)

                    gather(x, rows, 0, x_got)
                    gather(attr, edge_attr, 2, attr_got)
                    pl.wait_ge(x_got[par], 64 * (i + 1))
                    pl.sem_inc(sent, 1)
                    gather(x, t.seg_in, 1, x_added, compute_op=ALU.add)

                edge_groups(pl, fetch, lambda g, par, i, nxt: nxt and fetch(*nxt))

            @block.vector
            def _(v):
                norm_credit_vector(v, norm)
                for s in (formed, split, t_split):
                    v.sem_inc(s, TILE_CREDIT)

                def coefficients(g, par, i):
                    v.wait_ge(x_added[par], 64 * (i + 1))
                    norm_statistics(nc, v, norm, x[:, par], g, par, GT)
                    norm_coefficients(nc, v, norm, g, par, GT)

                def body(g, par, i, nxt):
                    v.wait_ge(attr_got[par], 64 * (i + 1))
                    for k in range(GT):
                        v.wait_ge(relued, tile_done(g, k))
                        nc.vector.tensor_tensor(x[:, par, k, :], x[:, par, k, :], attr[:, par, k, :], ALU.subtract).then_inc(formed, 1)
                    for k in range(GT):
                        v.wait_ge(halved, tile_done(g, k))
                        nc.vector.tensor_tensor(low[:, k, :], x[:, par, k, :], high[:, k, :].bitcast(F32), ALU.subtract).then_inc(split, 1)
                    for k in range(GT):
                        v.wait_ge(t_halved, tile_done(g, k))
                        nc.vector.tensor_tensor(al[:, k], turn_ps[k][:], ah[:, k].bitcast(F32), ALU.subtract).then_inc(t_split, 1)
                    if nxt:
                        coefficients(*nxt)

                edge_groups(v, coefficients, body)

            @block.scalar
            def _(a):
                norm_credit_scalar(a, norm)
                for s in (relued, halved, t_halved, copied):
                    a.sem_inc(s, TILE_CREDIT)
                a.sem_inc(widened, GROUP_CREDIT)

                def root(g, par, i):
                    a.wait_ge(summed, tiles_two_before(g))
                    nc.scalar.copy(same[:, par], t.same[q][:, DS(g * GT, GT), :]).then_inc(widened, 1)
                    norm_root(nc, a, norm, t, g, par, GT)

                def apply(g, par, i):
                    a.wait_ge(norm.ready, group_done(g))
                    for k in range(GT):
                        nc.scalar.activation(x[:, par, k, :], x[:, par, k, :], ACT.Relu, bias=norm.shift[:, par, k:k + 1],
                                             scale=norm.scale[:, par, k:k + 1]).then_inc(relued, 1)

                def give(g, par, i):
                    wait_uses(a, stored[par], 16 * i)
                    for k in range(GT):
                        a.wait_ge(produced, tile_done(g, k))
                        nc.scalar.copy(out[:, par, k, :], row_ps[k][:]).then_inc(copied, 1)

                def start(g, par, i):
                    root(g, par, i)
                    apply(g, par, i)

                def body(g, par, i, nxt):
                    for k in range(GT):
                        a.wait_ge(formed, tile_done(g, k))
                        a.wait_ge(summed, tile_before(g, k))
                        nc.scalar.copy(high[:, k, :], x[:, par, k, :]).then_inc(halved, 1)
                    for k in range(GT):
                        a.wait_ge(summed, tile_done(g, k))
                        a.wait_ge(produced, tile_before(g, k))
                        nc.scalar.copy(ah[:, k], turn_ps[k][:]).then_inc(t_halved, 1)
                    if nxt:
                        root(*nxt)
                        apply(*nxt)
                    give(g, par, i)

                edge_groups(a, start, body)

            @block.tensor
            def _(pe):
                pe.sem_inc(summed, TILE_CREDIT)
                pe.sem_inc(produced, TILE_CREDIT)

                def total(g, par, i):
                    pe.wait_ge(widened, group_done(g))
                    for k in range(GT):
                        pe.wait_ge(split, tile_done(g, k))
                        pe.wait_ge(t_split, tile_before(g, k))
                        for c in range(DC):
                            nc.tensor.matmul(turn_ps[k][:, c, :], low[:, k, c * P:(c + 1) * P], same[:, par, k, :], start=True, stop=False)
                            mm = nc.tensor.matmul(turn_ps[k][:, c, :], high[:, k, c * P:(c + 1) * P], same[:, par, k, :], start=False, stop=True)
                        mm.then_inc(summed, 1)

                def body(g, par, i, nxt):
                    for k in range(GT):
                        pe.wait_ge(t_split, tile_done(g, k))
                        pe.wait_ge(copied, tile_before(g, k))
                        for c in range(DC):
                            mm = product3(nc, row_ps[k][:], ah[:, k, c, :], al[:, k, c, :], wh[:, c, :], wl[:, c, :], c == 0, c == DC - 1)
                        mm.then_inc(produced, 1)
                    if nxt:
                        total(*nxt)

                edge_groups(pe, total, body)

            @block.sync
            def _(sp):
                def store(g, par, i, nxt):
                    sp.wait_ge(copied, tile_done(g, GT - 1))
                    sp.dma_start(table[DS(g * GR, GR), :].rearrange("(k p) d -> p k d", p=P), out[:, par]).then_inc(stored[par], 16)

                edge_groups(sp, nothing, store)
                for par in range(2):
                    sp.wait_ge(stored[par], 16 * (EG // 2))
    complete_segments(nc, t, q, table, name + "c")


def last_layer(nc, t, rows, weight, const_halves, slope, out_rows):
    name = "last"
    with ExitStack() as ctx:
        ctx.enter_context(nc.cleanup_on_exit())

        def sb(what, shape, dt=F32):
            return ctx.enter_context(nc.sbuf_tensor(f"{name}_{what}", shape, dt))

        def sem(what):
            return nc.alloc_semaphore(f"{name}_{what}")

        wh, wl = weight
        x, h = sb("x", [P, 4, GT, D]), sb("h", [P, GT, D])
        side = [sb(f"side{q}", [P, 2, GT, D]) for q in range(2)]
        ah, al = sb("ah", [P, 2, GT, DC, P], F32R), sb("al", [P, 2, GT, DC, P], F32R)
        out = sb("out", [P, GT, D])
        rest = sb("rest", [P, 1])
        one = sb("one", [1, P], F32R)
        x_index, side_index = sb("x_index", [P, 2, GT], I32), sb("side_index", [P, 2, 2, GT], I32)
        turn_ps = [ctx.enter_context(nc.psum_tensor(f"{name}_tps{i}", [P, DC, P], F32)) for i in range(4)]
        row_ps = [ctx.enter_context(nc.psum_tensor(f"{name}_rps{i}", [P, D], F32)) for i in range(4)]
        norm = make_norm(nc, ctx, name + "n")
        consts, one_ready, rest_ready, indexed, x_indexed, sent = (sem(n) for n in ("consts", "one_ready", "rest_ready", "indexed", "x_indexed", "sent"))
        loaded, x_added = [sem(f"loaded{s}") for s in range(4)], [sem(f"x_added{s}") for s in range(4)]
        gathered, stored = [sem(f"gathered{p}") for p in range(2)], sem("stored")
        relued, turned, halved, split = (sem(n) for n in ("relued", "turned", "halved", "split"))
        produced, added, z_ready, negated, bent, finished = (sem(n) for n in ("produced", "added", "z_ready", "negated", "bent", "finished"))

        with nc.Block() as block:
            @block.sync
            def _(sp):
                sp.dma_start(rest[:], slope.rearrange("(o d) -> o d", o=1).to_broadcast([P, 1])).then_inc(consts, 16)

                def load(g, par, i, slot, lap, tail):
                    wait_uses(sp, finished, tiles_four_before(g))
                    load_group(sp, x[:, slot], rows, g, tail, loaded[slot])

                each_node_group(sp, load)

            @block.gpsimd
            def _(pl):
                def add_segments(g, par, i, slot, lap, tail):
                    tiles = tiles_of(tail)
                    pl.wait_ge(norm.measured, tiles_two_before(g))
                    pl.sem_inc(sent, 1)
                    nc.gpsimd.tensor_copy(x_index[:, par, 0:tiles], t.last[0][:, DS(g * GT, tiles)]).then_inc(x_indexed, 1)
                    pl.wait_ge(loaded[slot], loads_done(lap, tail))
                    pl.wait_ge(x_indexed, g + 1)
                    pl.sem_inc(sent, 1)
                    for k in range(tiles):
                        nc.gpsimd.indirect_dma_start(out=x[:, slot, k, :], out_offset=None, in_=t.seg_in, compute_op=ALU.add,
                                                     in_offset=bass.IndirectOffsetOnAxis(ap=x_index[:, par, k:k + 1], axis=0)).then_inc(x_added[slot], 16)

                def fetch(g, par, i, slot, lap, tail):
                    tiles = tiles_of(tail)
                    pl.wait_ge(finished, tiles_two_before(g))
                    pl.sem_inc(sent, 1)
                    for q in range(2):
                        nc.gpsimd.tensor_copy(side_index[:, par, q, 0:tiles], t.last[q][:, DS(g * GT, tiles)]).then_inc(indexed, 1)
                    pl.wait_ge(indexed, 2 * g + 2)
                    pl.sem_inc(sent, 1)
                    for k in range(tiles):
                        for q, table in enumerate((t.seg_dst, t.seg_src)):
                            nc.gpsimd.indirect_dma_start(out=side[q][:, par, k, :], out_offset=None, in_=table,
                                                         in_offset=bass.IndirectOffsetOnAxis(ap=side_index[:, par, q, k:k + 1], axis=0)).then_inc(gathered[par], 16)

                def body(g, par, i, slot, lap, tail, nxt):
                    if nxt:
                        add_segments(*nxt)
                    fetch(g, par, i, slot, lap, tail)

                node_groups(pl, add_segments, body)

            @block.vector
            def _(v):
                norm_credit_vector(v, norm)
                for s in (split, added, z_ready, bent, finished):
                    v.sem_inc(s, TILE_CREDIT)
                v.wait_ge(consts, 16)
                nc.vector.tensor_scalar(rest[:], rest[:], -1.0, 1.0, ALU.mult, ALU.add).then_inc(rest_ready, 1)
                v.wait_ge(rest_ready, 1)

                def coefficients(g, par, i, slot, lap, tail):
                    v.wait_ge(x_added[slot], 64 * lap + 16 * tiles_of(tail))
                    norm_statistics(nc, v, norm, x[:, slot], g, par, tiles_of(tail))
                    norm_coefficients(nc, v, norm, g, par, tiles_of(tail))

                def lower(g, par, i, slot, lap, tail):
                    for k in range(tiles_of(tail)):
                        v.wait_ge(halved, tile_done(g, k))
                        nc.vector.tensor_tensor(al[:, par, k], turn_ps[k][:], ah[:, par, k].bitcast(F32), ALU.subtract).then_inc(split, 1)

                def start(*group):
                    coefficients(*group)
                    lower(*group)

                def body(g, par, i, slot, lap, tail, nxt):
                    tiles = tiles_of(tail)
                    s0, s1 = side[0][:, par], side[1][:, par]

                    def z_of(k):
                        v.wait_ge(added, tile_done(g, k))
                        nc.vector.scalar_tensor_tensor(s0[:, k, :], s1[:, k, :], t.rcnt[1][:, DS(g * GT + k, 1)], s0[:, k, :], ALU.mult, ALU.add).then_inc(z_ready, 1)

                    if nxt:
                        coefficients(*nxt)
                    v.wait_ge(gathered[par], 128 * i + 32 * tiles)
                    for k in range(tiles):
                        v.wait_ge(produced, tile_done(g, k))
                        nc.vector.scalar_tensor_tensor(s0[:, k, :], s0[:, k, :], t.rcnt[0][:, DS(g * GT + k, 1)], row_ps[k][:], ALU.mult, ALU.add).then_inc(added, 1)
                        if k:
                            z_of(k - 1)
                    z_of(tiles - 1)
                    if nxt:
                        lower(*nxt)
                    for k in range(tiles):
                        v.wait_ge(negated, tile_done(g, k))
                        nc.vector.scalar_tensor_tensor(s0[:, k, :], s1[:, k, :], rest[:], s0[:, k, :], ALU.mult, ALU.add).then_inc(bent, 1)
                    wait_uses(v, stored, 16 * g)
                    for k in range(tiles):
                        v.wait_ge(bent, tile_done(g, k))
                        nc.vector.tensor_tensor(out[:, k, :], x[:, slot, k, :], s0[:, k, :], ALU.add).then_inc(finished, 1)

                node_groups(v, start, body)

            @block.scalar
            def _(a):
                norm_credit_scalar(a, norm)
                for s in (relued, halved, negated):
                    a.sem_inc(s, TILE_CREDIT)
                nc.scalar.copy(one[:], t.ones[0:1, :]).then_inc(one_ready, 1)

                def apply(g, par, i, slot, lap, tail):
                    norm_root(nc, a, norm, t, g, par, tiles_of(tail))
                    a.wait_ge(norm.ready, group_done(g))
                    for k in range(tiles_of(tail)):
                        a.wait_ge(turned, tile_before(g, k))
                        nc.scalar.activation(h[:, k, :], x[:, slot, k, :], ACT.Relu, bias=norm.shift[:, par, k:k + 1],
                                             scale=norm.scale[:, par, k:k + 1]).then_inc(relued, 1)

                def higher(g, par, i, slot, lap, tail):
                    a.wait_ge(produced, tiles_two_before(g))
                    for k in range(tiles_of(tail)):
                        a.wait_ge(turned, tile_done(g, k))
                        nc.scalar.copy(ah[:, par, k], turn_ps[k][:]).then_inc(halved, 1)

                def start(*group):
                    apply(*group)
                    higher(*group)

                def body(g, par, i, slot, lap, tail, nxt):
                    if nxt:
                        apply(*nxt)
                    for k in range(tiles_of(tail)):
                        a.wait_ge(z_ready, tile_done(g, k))
                        nc.scalar.activation(side[1][:, par, k, :], side[0][:, par, k, :], ACT.Relu, scale=-1.0).then_inc(negated, 1)
                    if nxt:
                        higher(*nxt)
                    a.wait_ge(finished, tile_done(g, tiles_of(tail) - 1))
                    store_group(a, out_rows, out[:], g, tail, stored)

                node_groups(a, start, body)
                a.wait_ge(stored, 16 * (NG + 1))

            @block.tensor
            def _(pe):
                pe.sem_inc(turned, TILE_CREDIT)
                pe.sem_inc(produced, TILE_CREDIT)
                pe.wait_ge(one_ready, 1)

                def turn(g, par, i, slot, lap, tail):
                    for k in range(tiles_of(tail)):
                        pe.wait_ge(relued, tile_done(g, k))
                        pe.wait_ge(split, tile_before(g, k))
                        for c in range(DC):
                            mm = nc.tensor.transpose(turn_ps[k][:, c, :], h[:, k, c * P:(c + 1) * P], t.ident[:])
                        mm.then_inc(turned, 1)

                def body(g, par, i, slot, lap, tail, nxt):
                    for k in range(tiles_of(tail)):
                        pe.wait_ge(split, tile_done(g, k))
                        pe.wait_ge(added, tile_before(g, k))
                        for half in range(2):
                            nc.tensor.matmul(row_ps[k][:], one[:], const_halves[1 - half][:], start=half == 0, stop=False)
                        for c in range(DC):
                            mm = product3(nc, row_ps[k][:], ah[:, par, k, c, :], al[:, par, k, c, :], wh[:, c, :], wl[:, c, :], False, c == DC - 1)
                        mm.then_inc(produced, 1)
                    if nxt:
                        turn(*nxt)

                node_groups(pe, turn, body)


def gnn_program(nc, x, src, dst, edge_attr, l0_eps, l0_w1, l0_b1, l0_g1, l0_be1, l0_w2, l0_b2, l0_g2, l0_be2,
                l1_w1, l1_b1, l1_w2, l1_b2, coeffs, paths, wo_w, wo_b, wi_w, wi_b, ws_w, ws_b, mlp_w, mlp_b, slope, out):
    with ExitStack() as ctx:
        t = make_tables(nc, ctx)
        sort_edges(nc, t, src, dst)
        index_edges(nc, t)
        sum_segments(nc, t, x, t.seg_in, "ginseg", True)
        with ExitStack() as layer:
            stats1 = layer.enter_context(nc.sbuf_tensor("stats1", [P, HC, NG, 6], F32))
            stats2 = layer.enter_context(nc.sbuf_tensor("stats2", [P, DC, NG, 6], F32))
            coef1 = layer.enter_context(nc.sbuf_tensor("coef1", [P, 2, HC], F32))
            coef2 = layer.enter_context(nc.sbuf_tensor("coef2", [P, 2, DC], F32))
            gin_up(nc, t, x, l0_eps, l0_w1, l0_b1, stats1)
            batch_norm_coefficients(nc, t, stats1, l0_g1, l0_be1, coef1, HC, "bn1")
            gin_down(nc, t, l0_w2, l0_b2, coef1, stats2)
            batch_norm_coefficients(nc, t, stats2, l0_g2, l0_be2, coef2, DC, "bn2")
            gin_out(nc, t, x, coef2)
        sum_segments(nc, t, t.x1, t.seg_in, "gcnseg0", True, t.dis_other)
        gcn(nc, t, 0, t.x1, l1_w1, l1_b1, t.r1)
        sum_segments(nc, t, t.r1, t.seg_in, "gcnseg1", False)
        gcn(nc, t, 1, t.r1, l1_w2, l1_b2, t.x2, t.x1)
        path_products(nc, t, t.x2, edge_attr, paths, coeffs)
        own = [ctx.enter_context(nc.sbuf_tensor(f"folded_s{half}", [P, DC, D], F32R)) for half in "hl"]
        const_halves = [ctx.enter_context(nc.sbuf_tensor(f"const_{half}", [1, D], F32R)) for half in "hl"]
        with ExitStack() as edges:
            ends = [[edges.enter_context(nc.sbuf_tensor(f"folded_{n}{half}", [P, DC, D], F32R)) for half in "hl"] for n in "oi"]
            fold_weights(nc, t, wo_w, wi_w, ws_w, mlp_w, wo_b, wi_b, ws_b, mlp_b, [own] + ends, const_halves)
            sum_messages(nc, t, 0, t.x2, edge_attr, ends[0], t.seg_dst, "outmsg")
            sum_messages(nc, t, 1, t.x2, edge_attr, ends[1], t.seg_src, "inmsg")
        last_layer(nc, t, t.x2, own, const_halves, slope, out)


NAMES = ["x", "src", "dst", "edge_attr_512", "L0_gnn_eps", "L0_gnn_W1", "L0_gnn_b1", "L0_gnn_g1", "L0_gnn_be1", "L0_gnn_W2",
         "L0_gnn_b2", "L0_gnn_g2", "L0_gnn_be2", "L1_gnn_W1", "L1_gnn_b1", "L1_gnn_W2", "L1_gnn_b2", "L2_gnn_path_coeffs",
         "L2_gnn_path_indices", "L3_gnn_WO_w", "L3_gnn_WO_b", "L3_gnn_WI_w", "L3_gnn_WI_b", "L3_gnn_WS_w", "L3_gnn_WS_b",
         "L3_gnn_mlp_w", "L3_gnn_mlp_b", "L3_gnn_prelu_a"]


def kernel(**inputs):
    import concourse.bacc as bacc
    from concourse.bass_utils import run_bass_kernel_spmd

    nc = bacc.Bacc("TRN2", target_bir_lowering=False, num_devices=1)
    arrays, args = {}, []
    for name in NAMES:
        a = np.ascontiguousarray(inputs[name])
        a = a.reshape(1) if a.ndim == 0 else a
        arrays[f"in_{name}"] = a
        args.append(nc.dram_tensor(f"in_{name}", a.shape, mybir.dt.from_np(a.dtype), kind="ExternalInput").ap())
    out = nc.dram_tensor("out", (N, D), F32, kind="ExternalOutput").ap()
    gnn_program(nc, *args, out)
    result = run_bass_kernel_spmd(nc, [arrays], core_ids=[0])
    return result.results[0]["out"]
```

```python
from contextlib import ExitStack

import numpy as np
import concourse.bass as bass
import concourse.mybir as mybir

F32 = mybir.dt.float32
F32R = mybir.dt.float32r
BF16 = mybir.dt.bfloat16
I32 = mybir.dt.int32
ALU = mybir.AluOpType
ACT = mybir.ActivationFunctionType
DS = bass.ds

P = 128
N = 10000
E = 5000
D = 512
H = 1024
DC = D // P
HC = H // P
GT = 4
GR = GT * P
NG = -(-N // GR)
TAIL = N - (NG - 1) * GR
TAIL_T = -(-TAIL // P)
TURNS = NG // 4
ET = -(-E // P)
EP = ET * P
EG = ET // GT
NB = 80
PADKEY = (NB - 1) * P
SLOTS = 3
ZROW = EP
SPARE = EP + 1
TROWS = EP + 1 + ET
TAB = 8
SEG, EXT, PATHS = 16, 32, 64
LN_EPS = 1e-5


def tiles_of(g_is_tail):
    return TAIL_T if g_is_tail else GT


def load_group(eng, dst, dram, g, tail, sem, width=D):
    if not tail:
        eng.dma_start(dst, dram[DS(g * GR, GR), 0:width].rearrange("(k p) d -> p k d", p=P)).then_inc(sem, 16)
        return
    full = TAIL // P
    eng.dma_start(dst[:, 0:full], dram[g * GR:g * GR + full * P, 0:width].rearrange("(k p) d -> p k d", p=P)).then_inc(sem, 16)
    eng.dma_start(dst[0:TAIL - full * P, full], dram[g * GR + full * P:N, 0:width]).then_inc(sem, 16)


def store_group(eng, dram, src, g, tail, sem):
    if not tail:
        eng.dma_start(dram[DS(g * GR, GR), :].rearrange("(k p) d -> p k d", p=P), src).then_inc(sem, 16)
        return
    full = TAIL // P
    eng.dma_start(dram[g * GR:g * GR + full * P, :].rearrange("(k p) d -> p k d", p=P), src[:, 0:full]).then_inc(sem, 16)
    eng.dma_start(dram[g * GR + full * P:N, :], src[0:TAIL - full * P, full]).then_inc(sem, 16)


def loads_done(i, tail):
    return 16 * (i + 1) + (16 if tail else 0)


def node_groups(eng, start, body):
    def turn_of_four(turn, first_of_next):
        four = [(4 * turn + j, j % 2, 2 * turn + j // 2, j, turn, False) for j in range(4)]
        for group, nxt in zip(four, four[1:] + [first_of_next]):
            body(*group, nxt)

    def first(turn):
        return (4 * turn, 0, 2 * turn, 0, turn, False)

    start(*first(0))
    turn_of_four(0, first(1))
    with eng.Fori(1, TURNS - 1) as turn:
        turn_of_four(turn, first(turn + 1))
    last = TURNS - 1
    rest = [(4 * last + j, j % 2, 2 * last + j // 2, j, last, j == 3) for j in range(4)]
    for group, nxt in zip(rest, rest[1:] + [None]):
        body(*group, nxt)


def each_node_group(eng, step):
    node_groups(eng, nothing, lambda g, par, i, slot, lap, tail, nxt: step(g, par, i, slot, lap, tail))


def edge_groups(eng, start, body):
    start(0, 0, 0)
    for g in range(EG):
        body(g, g % 2, g // 2, (g + 1, (g + 1) % 2, (g + 1) // 2) if g + 1 < EG else None)


def wait_uses(eng, sem, value):
    if not isinstance(value, int) or value > 0:
        eng.wait_ge(sem, value)


def nothing(*_):
    return None


def product3(nc, out, wh, wl, ah, al, first, last):
    nc.tensor.matmul(out, wl, ah, start=first, stop=False)
    nc.tensor.matmul(out, wh, al, start=False, stop=False)
    return nc.tensor.matmul(out, wh, ah, start=False, stop=last)


class Tables:
    pass


def make_tables(nc, ctx):
    t = Tables()

    def sb(name, shape, dt):
        return ctx.enter_context(nc.sbuf_tensor(name, shape, dt))

    t.ident = sb("ident", [P, P], F32)
    t.ones = sb("ones", [P, P], F32)
    t.eps = sb("eps", [P, 1], F32)
    t.rowiota = sb("rowiota", [P, P], F32)
    t.partiota = sb("partiota", [P, 1], F32)
    t.same = [sb(f"same{q}", [P, ET, P], BF16) for q in range(2)]
    t.last = [sb(f"last{q}", [P, NB], I32) for q in range(2)]
    t.dis = sb("dis", [P, NB], F32)
    t.pack = sb("pack", [P, 2, ET, 5], I32)
    t.other = [sb(f"other{q}", [P, ET], I32) for q in range(2)]
    t.eid = [sb(f"eid{q}", [P, ET], I32) for q in range(2)]
    t.key = [sb(f"key{q}", [P, ET], I32) for q in range(2)]
    t.etab = [sb(f"etab{q}", [P, ET, TAB], I32) for q in range(2)]
    t.share = [sb(f"share{q}", [P, ET], F32) for q in range(2)]
    t.fetch = [sb(f"fetch{q}", [P, ET, 3], I32) for q in range(2)]
    t.dis_other = sb("dis_other", [P, ET], F32)
    t.cut_rows = [sb(f"cut_rows{q}", [ET, 1], I32) for q in range(2)]
    t.cut_dest = [sb(f"cut_dest{q}", [ET, 1], I32) for q in range(2)]
    t.cut_same = [sb(f"cut_same{q}", [ET, ET], F32) for q in range(2)]

    def dram(name, shape, dt=F32):
        return nc.dram_tensor(name, shape, dt).ap()

    t.smeta = [dram(f"smeta{q}", [EP + 1, 4], I32) for q in range(2)]
    t.tab = dram("tab", [NB * P, TAB], I32)
    t.seg_in = dram("seg_a", [TROWS, D])
    t.seg_dst = dram("seg_b", [TROWS, D])
    t.seg_src = dram("seg_c", [TROWS, D])
    t.y1 = dram("y1", [NG, P, HC, GR])
    t.y2 = dram("y2", [NG, P, DC, GR])
    t.x1 = dram("x1", [N, D])
    t.r1 = dram("r1", [N, D])
    t.x2 = dram("x2", [N, D])
    return t


def sort_edges(nc, t, src, dst):
    keys = (dst, src)
    with ExitStack() as ctx:
        ctx.enter_context(nc.cleanup_on_exit())
        def sb(name, shape, dt=F32):
            return ctx.enter_context(nc.sbuf_tensor(name, shape, dt))

        ktile = sb("ktile", [ET, 2, P], I32)
        ktile_f = sb("ktile_f", [ET, 2, P])
        kcol = sb("kcol", [P, 2, ET])
        kcol_i = sb("kcol_i", [P, 2, ET], I32)
        hi_i = sb("hi_i", [P, 2, ET], I32)
        lo_i = sb("lo_i", [P, 2, ET], I32)
        hi_f = sb("hi_f", [P, 2, ET])
        lo_f = sb("lo_f", [P, 2, ET])
        eid_f = sb("eid_f", [P, ET])
        krow_i = sb("krow_i", [P, 2, EP], I32)
        hrow_i = sb("hrow_i", [NB, 2, EP], I32)
        hit = hrow_i[:].bitcast(F32)
        later = sb("later", [P, P])
        before = sb("before", [NB, NB])
        hot_hi = sb("hot_hi", [P, 2, ET, NB], BF16)
        hot_lo = sb("hot_lo", [P, 2, ET, P], BF16)
        unit = sb("unit", [P, 2], BF16)
        count = sb("count", [NB, 2, P, ET])
        rowsum, offset = sb("rowsum", [NB, 2]), sb("offset", [NB, 2])
        total = sb("total", [NB, 2, P])
        endf = sb("endf", [NB, 2, P])
        lastf = sb("lastf", [NB, 2, P])
        some = sb("some", [NB, 2, P])
        disf = sb("disf", [NB, P])
        tabs = sb("tabs", [NB, P, TAB], I32)
        zeros = sb("zeros", [P, D])
        tie_scratch, scratch = sb("tie_scratch", [P, 8, P]), sb("scratch", [P, 8, P])
        upto = sb("upto", [P, 2, ET])
        tie = sb("tie", [P, 2, ET])
        rank = sb("rank", [P, 2, ET])
        pack = t.pack
        psum = [ctx.enter_context(nc.psum_tensor(f"sort_ps{i}", [P, 512], F32)) for i in range(8)]

        def sem(name):
            return nc.alloc_semaphore(name)

        padded, loaded, rows_loaded, made = sem("padded"), sem("loaded"), sem("rows_loaded"), sem("made")
        step, turned, zstored = sem("sort_step"), sem("turned"), sem("zstored")
        evacuated, counted, row_counted, fenced = sem("evacuated"), sem("counted"), sem("row_counted"), sem("fenced")
        with nc.Block() as block:
            @block.sync
            def _(sp):
                sp.wait_ge(padded, 1)
                full = E // P
                for q in range(2):
                    sp.dma_start(ktile[0:full, q, :], keys[q][0:full * P].rearrange("(t p) -> t p", p=P)).then_inc(loaded, 16)
                    sp.dma_start(ktile[full:ET, q, 0:E - full * P], keys[q][full * P:E].rearrange("(t p) -> t p", t=1)).then_inc(loaded, 16)
                sp.wait_ge(padded, 2)
                for q in range(2):
                    sp.dma_start(krow_i[:, q, 0:E], keys[q].rearrange("(o e) -> o e", o=1).to_broadcast([P, E])).then_inc(rows_loaded, 16)
                sp.wait_ge(made, 1)
                for q, table in enumerate((t.seg_in, t.seg_dst, t.seg_src)):
                    sp.dma_start(table[ZROW:TROWS, :], zeros[0:TROWS - ZROW, :]).then_inc(zstored, 16)
                sp.wait_ge(zstored, 48)

            @block.gpsimd
            def _(pl):
                nc.gpsimd.memset(ktile[:], PADKEY).then_inc(padded, 1)
                nc.gpsimd.memset(krow_i[:, :, E:EP], PADKEY).then_inc(padded, 1)
                nc.gpsimd.memset(zeros[:], 0.0).then_inc(made, 1)
                nc.gpsimd.memset(t.ident[:], 1.0)
                nc.gpsimd.memset(t.ones[:], 1.0)
                nc.gpsimd.memset(later[:], 1.0)
                nc.gpsimd.memset(before[:], 1.0)
                nc.gpsimd.memset(unit[:, 0:1], 0.0)
                nc.gpsimd.memset(unit[:, 1:2], 1.0)
                nc.gpsimd.memset(t.eps[:], LN_EPS)
                nc.gpsimd.iota(t.rowiota[:], pattern=[[1, P]], base=0, channel_multiplier=0, allow_small_or_imprecise_dtypes=True)
                nc.gpsimd.iota(t.partiota[:], pattern=[[1, 1]], base=0, channel_multiplier=1, allow_small_or_imprecise_dtypes=True)
                nc.gpsimd.iota(eid_f[:], pattern=[[P, ET]], base=0, channel_multiplier=1, allow_small_or_imprecise_dtypes=True).then_inc(made, 1)
                pl.wait_ge(made, 2)
                nc.gpsimd.affine_select(out=t.ident[:], in_=t.ident[:], compare_op=ALU.is_equal, fill=0.0, base=0, pattern=[[-1, P]], channel_multiplier=1)
                nc.gpsimd.affine_select(out=later[:], in_=later[:], compare_op=ALU.is_gt, fill=0.0, base=0, pattern=[[1, P]], channel_multiplier=-1)
                nc.gpsimd.affine_select(out=before[:], in_=before[:], compare_op=ALU.is_gt, fill=0.0, base=0, pattern=[[1, NB]], channel_multiplier=-1).then_inc(made, 1)

            @block.tensor
            def _(pe):
                pe.wait_ge(made, 3)
                pe.wait_ge(step, 1)
                for q in range(2):
                    mm = nc.tensor.transpose(psum[q][:, 0:ET], ktile_f[:, q, :], t.ident[0:ET, 0:ET])
                mm.then_inc(turned, 1)
                pe.sem_inc(evacuated, 4)
                for q in range(2):
                    pe.wait_ge(step, 10 + 2 * q)
                    nc.tensor.matmul(psum[6][0:NB, q:q + 1], hot_hi[:, q, 0, :], unit[:, 0:1], start=True, stop=False)
                    with pe.Fori(0, ET // 8) as i:
                        for b in range(2):
                            pe.wait_ge(evacuated, 10 * q + 2 * i + b + 3)
                            for j in range(4):
                                tile = DS(8 * i + 4 * b + j, 1)
                                nc.tensor.matmul(psum[6][0:NB, q:q + 1], hot_hi[:, q, tile, :].rearrange("p o n -> p (o n)"), unit[:, 1:2], start=False, stop=False)
                                mm = nc.tensor.matmul(psum[2 + 2 * q + b][0:NB, j * P:(j + 1) * P], hot_hi[:, q, tile, :].rearrange("p o n -> p (o n)"),
                                                      hot_lo[:, q, tile, :].rearrange("p o n -> p (o n)"), start=True, stop=True)
                            mm.then_inc(counted, 1)
                    nc.tensor.matmul(psum[6][0:NB, q:q + 1], hot_hi[:, q, 0, :], unit[:, 0:1], start=False, stop=True).then_inc(row_counted, 1)

            @block.scalar
            def _(a):
                for q in range(2):
                    with a.Fori(0, ET // 8) as i:
                        for b in range(2):
                            a.wait_ge(counted, 10 * q + 2 * i + b + 1)
                            a.sem_inc(fenced, 1)
                            nc.scalar.copy(count[:, q, :, DS(8 * i + 4 * b, 4)], psum[2 + 2 * q + b][0:NB, :].rearrange("p (t n) -> p n t", n=P)).then_inc(evacuated, 1)

            @block.vector
            def _(v):
                n = [0]

                def link(ins):
                    n[0] += 1
                    ins.then_inc(step, 1)
                    v.wait_ge(step, n[0])

                v.wait_ge(padded, 1)
                v.wait_ge(loaded, 64)
                link(nc.vector.tensor_copy(ktile_f[:], ktile[:]))
                v.wait_ge(turned, 1)
                for q in range(2):
                    link(nc.vector.tensor_copy(kcol[:, q, :], psum[q][:, 0:ET]))
                link(nc.vector.tensor_copy(kcol_i[:], kcol[:]))
                link(nc.vector.tensor_scalar(hi_i[:], kcol_i[:], 7, None, ALU.logical_shift_right))
                link(nc.vector.tensor_scalar(lo_i[:], kcol_i[:], P - 1, None, ALU.bitwise_and))
                link(nc.vector.tensor_copy(hi_f[:], hi_i[:]))
                link(nc.vector.tensor_copy(lo_f[:], lo_i[:]))
                v.wait_ge(made, 3)
                for q in range(2):
                    link(nc.vector.tensor_tensor(
                        hot_hi[:, q], t.rowiota[:, 0:NB].rearrange("p (o n) -> p o n", o=1).to_broadcast([P, ET, NB]),
                        hi_f[:, q, :].rearrange("p (t o) -> p t o", o=1).to_broadcast([P, ET, NB]), ALU.is_equal))
                    link(nc.vector.tensor_tensor(
                        hot_lo[:, q], t.rowiota[:, :].rearrange("p (o n) -> p o n", o=1).to_broadcast([P, ET, P]),
                        lo_f[:, q, :].rearrange("p (t o) -> p t o", o=1).to_broadcast([P, ET, P]), ALU.is_equal))
                v.wait_ge(padded, 2)
                v.wait_ge(rows_loaded, 32)
                for q in range(2):
                    link(nc.vector.tensor_scalar(hrow_i[:, q, :], krow_i[0:NB, q, :], 7, None, ALU.logical_shift_right))
                    link(nc.vector.tensor_scalar(hit[:, q, :], hrow_i[:, q, :], t.partiota[0:NB, :], None, ALU.is_equal))
                link(nc.vector.memset(pack[:], 0))
                for q in range(2):
                    link(nc.vector.tensor_copy(pack[:, q, :, 1], kcol[:, q, :]))
                    link(nc.vector.scalar_tensor_tensor(pack[:, q, :, 2], kcol[:, 1 - q, :], float(PADKEY), kcol[:, 1 - q, :], ALU.is_lt, ALU.mult))
                    link(nc.vector.scalar_tensor_tensor(pack[:, q, :, 3], eid_f[:], float(E), eid_f[:], ALU.is_lt, ALU.mult))

        pstep, prowed, pturned, sq, tabbed = sem("pstep"), sem("prowed"), sem("pturned"), sem("sq"), sem("tabbed")
        tied, picked, ranked = sem("tied"), sem("picked"), sem("ranked")
        with nc.Block() as block:
            @block.vector
            def _(v):
                n = [0]

                def link(ins):
                    n[0] += 1
                    ins.then_inc(pstep, 1)
                    v.wait_ge(pstep, n[0])

                v.sem_inc(tied, 8)
                v.sem_inc(ranked, 8)
                v.wait_ge(row_counted, 2)
                link(nc.vector.tensor_copy(rowsum[:], psum[6][0:NB, 0:2]))
                v.wait_ge(prowed, 1)
                link(nc.vector.tensor_copy(offset[:], psum[7][0:NB, 0:2]))
                v.wait_ge(evacuated, 2 * (ET // 4) + 4)
                for q in range(2):
                    running = count[:, q].rearrange("p n t -> p (n t)")
                    link(nc.vector.tensor_tensor_scan(running, t.ones[0:NB, 0:1].to_broadcast([NB, P * ET]), running, offset[:, q:q + 1], ALU.mult, ALU.add))
                with v.Fori(0, ET // 4) as i:
                    for q in range(2):
                        for j in range(4):
                            v.wait_ge(tied, 8 * i + 4 * q + j + 1)
                            nc.vector.scalar_tensor_tensor(tie_scratch[:, 4 * q + j, :], krow_i[:, q, DS((4 * i + j) * P, P)], kcol[:, q, DS(4 * i + j, 1)], later[:],
                                                           ALU.is_equal, ALU.mult, accum_out=tie[:, q, DS(4 * i + j, 1)]).then_inc(tied, 1)
                link(nc.vector.tensor_copy(endf[:], count[:, :, :, ET - 1]))
                link(nc.vector.tensor_tensor(total[:, :, 1:P], endf[:, :, 1:P], endf[:, :, 0:P - 1], ALU.subtract))
                link(nc.vector.tensor_tensor(total[:, :, 0], endf[:, :, 0], offset[:], ALU.subtract))
                link(nc.vector.tensor_scalar(lastf[:], endf[:], -1.0 - ZROW, None, ALU.add))
                link(nc.vector.tensor_scalar(some[:], total[:], 0.0, None, ALU.is_gt))
                link(nc.vector.tensor_tensor(lastf[:], lastf[:], some[:], ALU.mult))
                link(nc.vector.tensor_scalar(lastf[:], lastf[:], float(ZROW), None, ALU.add))
                link(nc.vector.memset(tabs[:], 0))
                for q in range(2):
                    link(nc.vector.tensor_copy(tabs[:, :, q], lastf[:, q, :]))
                link(nc.vector.tensor_scalar(endf[:], total[:], 1.0, None, ALU.max))
                link(nc.vector.reciprocal(endf[:], endf[:]))
                for q in range(2):
                    link(nc.vector.tensor_copy(tabs[:, :, 4 + q].bitcast(F32), endf[:, q, :]))
                v.wait_ge(sq, 1)
                link(nc.vector.reciprocal(disf[:], disf[:]))
                finish_rsqrt(nc, link, disf[:], some[:, 0, :], total[:, 0, :], 1.0)
                link(nc.vector.tensor_copy(tabs[:, :, 2].bitcast(F32), disf[:]))
                with v.Fori(0, ET // 8) as i:
                    for s in range(4):
                        q, tile = s % 2, 8 * i + 4 * (s // 2)
                        v.wait_ge(picked, 4 * i + s + 1)
                        for j in range(4):
                            v.wait_ge(ranked, 16 * i + 4 * s + j + 1)
                            nc.vector.scalar_tensor_tensor(scratch[:, 4 * q + j, :], psum[s][:, j * P:(j + 1) * P], 1.0,
                                                           hot_lo[:, q, DS(tile + j, 1), :].rearrange("p o n -> p (o n)"),
                                                           ALU.mult, ALU.mult, accum_out=upto[:, q, DS(tile + j, 1)]).then_inc(ranked, 1)
                v.wait_ge(ranked, 2 * ET + 8)
                v.wait_ge(tied, 2 * ET + 8)
                link(nc.vector.scalar_tensor_tensor(rank[:], upto[:], -1.0, tie[:], ALU.add, ALU.subtract))
                link(nc.vector.tensor_copy(pack[:, :, :, 0], rank[:]))
                v.wait_ge(pturned, 1)
                for q in range(2):
                    link(nc.vector.tensor_copy(t.last[q][:], psum[4][:, q * P:q * P + NB]))
                link(nc.vector.tensor_copy(t.dis[:], psum[6][:, 0:NB]))

            @block.scalar
            def _(a):
                a.wait_ge(pstep, 7)
                nc.scalar.activation(disf[:], total[:, 0, :], ACT.Sqrt, bias=t.ones[0:NB, 0:1]).then_inc(sq, 1)

            @block.tensor
            def _(pe):
                pe.wait_ge(pstep, 1)
                nc.tensor.matmul(psum[7][0:NB, 0:2], before[:], rowsum[:], start=True, stop=True).then_inc(prowed, 1)
                pe.wait_ge(pstep, 4)
                for bank in range(2 * ET // 4):
                    q, tile = bank % 2, 4 * (bank // 2)
                    if bank >= 4:
                        pe.wait_ge(ranked, 4 * (bank - 3) + 8)
                    for j in range(4):
                        mm = nc.tensor.matmul(psum[bank % 4][:, j * P:(j + 1) * P], hit[:, q, (tile + j) * P:(tile + j + 1) * P], count[:, q, :, tile + j], start=True, stop=True)
                    mm.then_inc(picked, 1)
                pe.wait_ge(pstep, 24)
                for q in range(2):
                    nc.tensor.transpose(psum[4][:, q * P:q * P + NB], lastf[:, q, :], t.ident[0:NB, 0:NB])
                nc.tensor.transpose(psum[6][:, 0:NB], disf[:], t.ident[0:NB, 0:NB]).then_inc(pturned, 1)

            @block.sync
            def _(sp):
                sp.wait_ge(pstep, 24)
                sp.dma_start(t.tab.rearrange("(a b) c -> a (b c)", b=P), tabs[:].rearrange("a b c -> a (b c)")).then_inc(tabbed, 16)
                sp.wait_ge(tabbed, 16)

        placed, closed = sem("placed"), sem("closed")
        with nc.Block() as block:
            @block.gpsimd
            def _(pl):
                scatter_edges(nc, pl, t, 0, placed)

            @block.sync
            def _(sp):
                for q in range(2):
                    sp.dma_start(t.smeta[q][EP:EP + 1, :], zeros[0:1, 0:4].bitcast(I32)).then_inc(closed, 16)
                sp.wait_ge(closed, 32)


def scatter_edges(nc, pl, t, q, placed):
    for tile in range(ET):
        nc.gpsimd.indirect_dma_start(out=t.smeta[q], out_offset=bass.IndirectOffsetOnAxis(ap=t.pack[:, q, tile, 0:1], axis=0),
                                     in_=t.pack[:, q, tile, 1:5], in_offset=None).then_inc(placed, 16)
    pl.wait_ge(placed, 16 * ET)


def fetch_other_ends(nc, pl, t, q, fetched, listed):
    for tile in range(ET):
        nc.gpsimd.indirect_dma_start(out=t.etab[q][:, tile, :], out_offset=None, in_=t.tab,
                                     in_offset=bass.IndirectOffsetOnAxis(ap=t.other[q][:, tile:tile + 1], axis=0)).then_inc(fetched, 16)
    pl.wait_ge(fetched, 16 * ET)
    for n, what in enumerate((t.other[q][:], t.etab[q][:, :, 0], t.eid[q][:])):
        nc.gpsimd.tensor_copy(t.fetch[q][:, :, n], what).then_inc(listed, 1)
    if q == 0:
        nc.gpsimd.tensor_copy(t.dis_other[:], t.etab[0][:, :, 2].bitcast(F32)).then_inc(listed, 1)
    pl.wait_ge(listed, 4 if q == 0 else 3)
    for tile in range(ET):
        nc.gpsimd.indirect_dma_start(out=t.etab[q][:, tile, :], out_offset=None, in_=t.tab,
                                     in_offset=bass.IndirectOffsetOnAxis(ap=t.key[q][:, tile:tile + 1], axis=0)).then_inc(fetched, 16)
    pl.wait_ge(fetched, 32 * ET)
    nc.gpsimd.tensor_copy(t.share[q][:], t.etab[q][:, :, 4 + q].bitcast(F32)).then_inc(listed, 1)


def index_edges(nc, t, q):
    with ExitStack() as ctx:
        ctx.enter_context(nc.cleanup_on_exit())

        def sb(name, shape, dt=F32):
            return ctx.enter_context(nc.sbuf_tensor(f"{name}{q}", shape, dt))

        def sem(name):
            return nc.alloc_semaphore(f"{name}{q}")

        keyf = sb("keyf", [P, ET])
        diag = sb("diag", [P, 2, 4, P])
        meta = sb("meta", [P, ET, 4], I32)
        end_i = sb("end_i", [ET, 4], I32)
        next_i = sb("next_i", [ET, 4], I32)
        cut_tab = sb("cut_tab", [ET, TAB], I32)
        end_f, next_f, runs_on, final = (sb(n, [ET, 1]) for n in ("end_f", "next_f", "runs_on", "final"))
        rowf, limit, spare, destf = (sb(n, [ET, 1]) for n in ("rowf", "limit", "spare", "destf"))
        diag_end = sb("diag_end", [ET, ET])
        psum = [ctx.enter_context(nc.psum_tensor(f"index{q}_ps{i}", [P, 4, P], F32)) for i in range(3)]
        back, ends, cut_got, made = sem("back"), sem("ends"), sem("cut_got"), sem("imade")
        step, ended, diagd, spread, same_made = sem("istep"), sem("iended"), sem("diagd"), sem("spread"), sem("same_made")

        with nc.Block() as block:
            @block.sync
            def _(sp):
                tiles = t.smeta[q][0:EP, :].rearrange("(t p) c -> p t c", p=P)
                sp.dma_start(meta[:], tiles).then_inc(back, 16)
                sp.dma_start(end_i[:], tiles[P - 1]).then_inc(ends, 16)
                sp.dma_start(next_i[:], t.smeta[q][1:EP + 1, :].rearrange("(t p) c -> p t c", p=P)[P - 1]).then_inc(ends, 16)

            @block.gpsimd
            def _(pl):
                nc.gpsimd.iota(limit[:], pattern=[[1, 1]], base=2 * P, channel_multiplier=P, allow_small_or_imprecise_dtypes=True)
                nc.gpsimd.iota(spare[:], pattern=[[1, 1]], base=SPARE, channel_multiplier=1, allow_small_or_imprecise_dtypes=True).then_inc(made, 1)
                pl.wait_ge(ends, 32)
                nc.gpsimd.indirect_dma_start(out=cut_tab[:], out_offset=None, in_=t.tab,
                                             in_offset=bass.IndirectOffsetOnAxis(ap=end_i[:, 0:1], axis=0)).then_inc(cut_got, 16)
                pl.wait_ge(cut_got, 16)

            @block.vector
            def _(v):
                n = [0]

                def link(ins):
                    n[0] += 1
                    ins.then_inc(step, 1)
                    v.wait_ge(step, n[0])

                v.wait_ge(back, 16)
                link(nc.vector.tensor_copy(keyf[:], meta[:, :, 0]))
                for four in range(ET // 4 + 1):
                    if four < ET // 4:
                        if four >= 2:
                            v.wait_ge(spread, four - 1)
                        keys = keyf[:, 4 * four:4 * four + 4].rearrange("p (t o) -> p t o", o=1).to_broadcast([P, 4, P])
                        nc.vector.tensor_tensor(diag[:, four % 2], t.ident[:].rearrange("p (o n) -> p o n", o=1).to_broadcast([P, 4, P]), keys, ALU.mult).then_inc(diagd, 1)
                    if four:
                        v.wait_ge(spread, four)
                        keys = keyf[:, 4 * four - 4:4 * four].rearrange("p (t o) -> p t o", o=1).to_broadcast([P, 4, P])
                        nc.vector.tensor_tensor(t.same[q][:, 4 * four - 4:4 * four, :], psum[(four - 1) % 2][:], keys, ALU.is_equal).then_inc(same_made, 1)
                link(nc.vector.tensor_copy(t.other[q][:], meta[:, :, 1]))
                link(nc.vector.tensor_copy(t.eid[q][:], meta[:, :, 2]))
                v.wait_ge(ends, 32)
                nc.vector.tensor_copy(t.key[q][:], meta[:, :, 0])
                link(nc.vector.tensor_copy(end_f[:], end_i[:, 0:1]))
                link(nc.vector.tensor_copy(next_f[:], next_i[:, 0:1]))
                link(nc.vector.tensor_tensor(runs_on[:], end_f[:], next_f[:], ALU.is_equal))
                link(nc.vector.tensor_scalar(diag_end[:], t.ident[0:ET, 0:ET], end_f[:], None, ALU.mult))
                v.wait_ge(ended, 1)
                link(nc.vector.tensor_scalar(t.cut_same[q][:], psum[2][0:ET, 0, 0:ET], end_f[:], runs_on[:], ALU.is_equal, ALU.mult))
                v.wait_ge(cut_got, 16)
                v.wait_ge(made, 1)
                link(nc.vector.tensor_copy(t.cut_rows[q][:], cut_tab[:, q:q + 1]))
                link(nc.vector.tensor_copy(rowf[:], cut_tab[:, q:q + 1]))
                link(nc.vector.tensor_scalar(final[:], rowf[:], limit[:], runs_on[:], ALU.is_lt, ALU.mult))
                link(nc.vector.tensor_tensor(destf[:], rowf[:], spare[:], ALU.subtract))
                link(nc.vector.tensor_tensor(destf[:], destf[:], final[:], ALU.mult))
                link(nc.vector.tensor_tensor(destf[:], destf[:], spare[:], ALU.add))
                link(nc.vector.tensor_copy(t.cut_dest[q][:], destf[:]))

            @block.tensor
            def _(pe):
                for four in range(ET // 4):
                    pe.wait_ge(diagd, four + 1)
                    if four >= 2:
                        pe.wait_ge(same_made, four - 1)
                    nc.tensor.matmul(psum[four % 2][:], t.ones[:], diag[:, four % 2], start=True, stop=True).then_inc(spread, 1)
                pe.wait_ge(step, 7)
                nc.tensor.matmul(psum[2][0:ET, 0, 0:ET], t.ones[0:ET, 0:ET], diag_end[:], start=True, stop=True).then_inc(ended, 1)


def tile_done(g, k):
    return 4 * g + k + 9


def tile_before(g, k):
    return 4 * g + k + 5


def tiles_two_before(g):
    return 4 * g + 4


def tiles_four_before(g):
    return 4 * g - 4


def group_done(g):
    return g + 3


TILE_CREDIT, GROUP_CREDIT = 8, 2


def finish_rsqrt(nc, link, y, half, var, eps):
    link(nc.vector.tensor_tensor(half, y, y, ALU.mult))
    link(nc.vector.scalar_tensor_tensor(half, var, eps, half, ALU.add, ALU.mult))
    link(nc.vector.tensor_scalar(half, half, -0.5, 1.5, ALU.mult, ALU.add))
    link(nc.vector.tensor_tensor(y, y, half, ALU.mult))


def make_norm(nc, ctx, name):
    norm = Tables()

    def sb(what, shape):
        return ctx.enter_context(nc.sbuf_tensor(f"{name}_{what}", shape, F32))

    norm.stats, norm.mv = sb("stats", [P, 2, GT, 6]), sb("mv", [P, 2, GT, 2])
    norm.root, norm.half = sb("root", [P, 2, GT]), sb("half", [P, 2, GT])
    norm.scale, norm.shift = sb("scale", [P, 2, GT]), sb("shift", [P, 2, GT])
    norm.measured, norm.pooling, norm.pooled, norm.rooted, norm.step, norm.ready = (
        nc.alloc_semaphore(f"{name}_{s}") for s in ("measured", "pooling", "pooled", "rooted", "step", "ready"))
    return norm


def norm_credit_vector(v, norm):
    v.sem_inc(norm.measured, TILE_CREDIT)
    v.sem_inc(norm.pooled, TILE_CREDIT)
    v.sem_inc(norm.ready, GROUP_CREDIT)


def norm_credit_scalar(a, norm):
    a.sem_inc(norm.rooted, GROUP_CREDIT)


def norm_statistics(nc, v, norm, x, g, par, tiles):
    for k in range(tiles):
        nc.vector.bn_stats(norm.stats[:, par, k, :], x[:, k, :]).then_inc(norm.measured, 1)
    v.wait_ge(norm.measured, tile_done(g, tiles - 1))
    v.sem_inc(norm.pooling, 1)
    for k in range(tiles):
        nc.vector.bn_aggr(norm.mv[:, par, k, :], norm.stats[:, par, k, :]).then_inc(norm.pooled, 1)


def norm_root(nc, a, norm, t, g, par, tiles):
    a.wait_ge(norm.pooled, tile_done(g, tiles - 1))
    nc.scalar.activation(norm.root[:, par, 0:tiles], norm.mv[:, par, 0:tiles, 1], ACT.Sqrt, bias=t.eps[:]).then_inc(norm.rooted, 1)


def norm_coefficients(nc, v, norm, g, par, tiles, times=None):
    y, half = norm.scale[:, par, 0:tiles], norm.half[:, par, 0:tiles]
    v.wait_ge(norm.rooted, group_done(g))
    steps = 6 if times is not None else 5
    n = [0]

    def link(ins):
        n[0] += 1
        ins.then_inc(norm.step, 1)
        v.wait_ge(norm.step, g * steps + n[0])

    link(nc.vector.reciprocal(y, norm.root[:, par, 0:tiles]))
    finish_rsqrt(nc, link, y, half, norm.mv[:, par, 0:tiles, 1], LN_EPS)
    if times is not None:
        link(nc.vector.tensor_tensor(y, y, times, ALU.mult))
    nc.vector.scalar_tensor_tensor(norm.shift[:, par, 0:tiles], norm.mv[:, par, 0:tiles, 0], -1.0, y, ALU.mult, ALU.mult).then_inc(norm.ready, 1)


def make_completion(nc, ctx, q, table, name, psum=None):
    c = Tables()
    c.q, c.table = q, table
    c.ends = ctx.enter_context(nc.sbuf_tensor(f"{name}_ends", [ET, D], F32))
    c.finals = ctx.enter_context(nc.sbuf_tensor(f"{name}_finals", [ET, D], F32))
    c.psum = ctx.enter_context(nc.psum_tensor(f"{name}_cut_ps", [P, D], F32)) if psum is None else psum
    c.got, c.fetched, c.added, c.completed, c.written = (nc.alloc_semaphore(f"{name}_{s}") for s in ("got", "fetched", "added", "completed", "written"))
    return c


def load_ends(sp, c):
    sp.dma_start(c.ends[:], c.table[0:EP, :].rearrange("(t p) d -> p t d", p=P)[P - 1]).then_inc(c.got, 16)


def rewrite_finals(nc, pl, t, completions):
    for c in completions:
        nc.gpsimd.indirect_dma_start(out=c.finals[:], out_offset=None, in_=c.table,
                                     in_offset=bass.IndirectOffsetOnAxis(ap=t.cut_rows[c.q][:, 0:1], axis=0)).then_inc(c.fetched, 16)
    for c in completions:
        pl.wait_ge(c.completed, 1)
        nc.gpsimd.indirect_dma_start(out=c.table, out_offset=bass.IndirectOffsetOnAxis(ap=t.cut_dest[c.q][:, 0:1], axis=0),
                                     in_=c.finals[:], in_offset=None).then_inc(c.written, 16)
    for c in completions:
        pl.wait_ge(c.written, 16)


def sum_ends(nc, pe, t, c):
    pe.wait_ge(c.got, 16)
    nc.tensor.matmul(c.psum[0:ET, :], t.cut_same[c.q][:], c.ends[:], start=True, stop=True).then_inc(c.added, 1)


def add_ends(nc, v, c):
    v.wait_ge(c.added, 1)
    v.wait_ge(c.fetched, 16)
    nc.vector.tensor_tensor(c.finals[:], c.finals[:], c.psum[0:ET, :], ALU.add).then_inc(c.completed, 1)


def split_weights(nc, v, parts, raw, loaded, halved):
    v.wait_ge(loaded, 16 * len(parts))
    for n, ((_, high, low), view) in enumerate(zip(parts, raw)):
        nc.vector.tensor_copy(high, view).then_inc(halved, 1)
        v.wait_ge(halved, n + 1)
        nc.vector.tensor_tensor(low, view, high.bitcast(F32), ALU.subtract)


def complete_and_load(nc, t, name, tables, parts):
    with ExitStack() as ctx:
        ctx.enter_context(nc.cleanup_on_exit())
        raw = [ctx.enter_context(nc.sbuf_tensor(f"{name}_raw{n}", list(part[0].shape), F32)) for n, part in enumerate(parts)]
        completions = [make_completion(nc, ctx, q, table, f"{name}_cut{q}") for q, table in tables]
        loaded, halved = nc.alloc_semaphore(f"{name}_loaded"), nc.alloc_semaphore(f"{name}_halved")
        with nc.Block() as block:
            @block.sync
            def _(sp):
                for c in completions:
                    load_ends(sp, c)
                for view, part in zip(raw, parts):
                    sp.dma_start(view[:], part[0]).then_inc(loaded, 16)

            @block.gpsimd
            def _(pl):
                rewrite_finals(nc, pl, t, completions)

            @block.tensor
            def _(pe):
                for c in completions:
                    sum_ends(nc, pe, t, c)

            @block.vector
            def _(v):
                for c in completions:
                    add_ends(nc, v, c)
                if parts:
                    split_weights(nc, v, parts, [view[:] for view in raw], loaded, halved)


def sum_segments(nc, t, rows, table, name, normed, times=None):
    q = 0
    with ExitStack() as ctx:
        ctx.enter_context(nc.cleanup_on_exit())
        def sb(what, shape, dt=F32):
            return ctx.enter_context(nc.sbuf_tensor(f"{name}_{what}", shape, dt))

        def sem(what):
            return nc.alloc_semaphore(f"{name}_{what}")

        x = sb("x", [P, SLOTS, GT, D])
        z = sb("z", [P, 2, GT, D]) if normed else None
        same = sb("same", [P, 2, GT, P])
        out = sb("out", [P, 2, GT, D])
        psum = [ctx.enter_context(nc.psum_tensor(f"{name}_ps{i}", [P, D], F32)) for i in range(8)]
        norm = make_norm(nc, ctx, name + "n") if normed else None
        gathered, stored = [sem(f"gathered{s}") for s in range(SLOTS)], [sem(f"stored{p}") for p in range(2)]
        relued, widened, summed, copied = (sem(s) for s in ("relued", "widened", "summed", "copied"))
        used = relued if normed else summed

        with nc.Block() as block:
            @block.gpsimd
            def _(pl):
                for g in range(EG):
                    if g >= SLOTS:
                        pl.wait_ge(used, tile_done(g - SLOTS, GT - 1))
                    for k in range(GT):
                        nc.gpsimd.indirect_dma_start(out=x[:, g % SLOTS, k, :], out_offset=None, in_=rows,
                                                     in_offset=bass.IndirectOffsetOnAxis(ap=t.other[q][:, g * GT + k:g * GT + k + 1], axis=0)).then_inc(gathered[g % SLOTS], 16)

            if normed:
                @block.vector
                def _(v):
                    norm_credit_vector(v, norm)

                    def coefficients(g, par, i):
                        v.wait_ge(gathered[g % SLOTS], 64 * (g // SLOTS + 1))
                        norm_statistics(nc, v, norm, x[:, g % SLOTS], g, par, GT)
                        norm_coefficients(nc, v, norm, g, par, GT, times[:, DS(g * GT, GT)] if times is not None else None)

                    edge_groups(v, coefficients, lambda g, par, i, nxt: nxt and coefficients(*nxt))

            @block.scalar
            def _(a):
                a.sem_inc(copied, TILE_CREDIT)
                a.sem_inc(widened, GROUP_CREDIT)
                if normed:
                    norm_credit_scalar(a, norm)
                    a.sem_inc(relued, TILE_CREDIT)

                def prepare(g, par, i):
                    a.wait_ge(summed, tiles_two_before(g))
                    nc.scalar.copy(same[:, par], t.same[q][:, DS(g * GT, GT), :]).then_inc(widened, 1)
                    if normed:
                        norm_root(nc, a, norm, t, g, par, GT)
                        a.wait_ge(norm.ready, group_done(g))
                        a.wait_ge(summed, tiles_two_before(g))
                        for k in range(GT):
                            nc.scalar.activation(z[:, par, k, :], x[:, g % SLOTS, k, :], ACT.Relu, bias=norm.shift[:, par, k:k + 1],
                                                 scale=norm.scale[:, par, k:k + 1]).then_inc(relued, 1)

                def body(g, par, i, nxt):
                    if nxt:
                        prepare(*nxt)
                    wait_uses(a, stored[par], 16 * i)
                    for k in range(GT):
                        a.wait_ge(summed, tile_done(g, k))
                        nc.scalar.copy(out[:, par, k, :], psum[4 * par + k][:]).then_inc(copied, 1)

                edge_groups(a, prepare, body)

            @block.tensor
            def _(pe):
                pe.sem_inc(summed, TILE_CREDIT)

                def body(g, par, i, nxt):
                    pe.wait_ge(widened, group_done(g))
                    pe.wait_ge(copied, tiles_two_before(g))
                    if not normed:
                        pe.wait_ge(gathered[g % SLOTS], 64 * (g // SLOTS + 1))
                    for k in range(GT):
                        if normed:
                            pe.wait_ge(relued, tile_done(g, k))
                        nc.tensor.matmul(psum[4 * par + k][:], same[:, par, k, :], z[:, par, k, :] if normed else x[:, g % SLOTS, k, :], start=True, stop=True).then_inc(summed, 1)

                edge_groups(pe, nothing, body)

            @block.sync
            def _(sp):
                def store(g, par, i, nxt):
                    sp.wait_ge(copied, tile_done(g, GT - 1))
                    sp.dma_start(table[DS(g * GR, GR), :].rearrange("(k p) d -> p k d", p=P), out[:, par]).then_inc(stored[par], 16)

                edge_groups(sp, nothing, store)
                for par in range(2):
                    sp.wait_ge(stored[par], 16 * (EG // 2))


def column_loads(eng, dst, vectors, sem):
    for n, vec in enumerate(vectors):
        eng.dma_start(dst[:, n, :], vec.rearrange("(c p) -> p c", p=P), allow_slow_non_contiguous=True).then_inc(sem, 16)


def gin_up(nc, t, x, eps, w1, b1, stats):
    with ExitStack() as ctx:
        ctx.enter_context(nc.cleanup_on_exit())
        def sb(what, shape, dt=F32):
            return ctx.enter_context(nc.sbuf_tensor(f"up_{what}", shape, dt))

        def sem(what):
            return nc.alloc_semaphore(f"up_{what}")

        wh, wl = sb("wh", [P, DC, H], F32R), sb("wl", [P, DC, H], F32R)
        complete_and_load(nc, t, "upw", [(0, t.seg_in)], [(w1.rearrange("(c p) n -> p c n", p=P), wh[:], wl[:])])
        bias, own = sb("bias", [P, 1, HC]), sb("own", [P, 1])
        xin, agg, h = sb("x", [P, 2, GT, D]), sb("agg", [P, 2, GT, D]), sb("h", [P, 2, GT, D])
        ah, al = sb("ah", [P, 2, DC, GR], F32R), sb("al", [P, 2, DC, GR], F32R)
        y = sb("y", [P, HC, GR])
        index = sb("index", [P, 2, GT], I32)
        turn_ps = [ctx.enter_context(nc.psum_tensor(f"up_tps{i}", [P, DC, P], F32)) for i in range(4)]
        y_ps = [ctx.enter_context(nc.psum_tensor(f"up_yps{i}", [P, GR], F32)) for i in range(4)]
        norm = make_norm(nc, ctx, "upn")
        consts, own_ready, indexed, sent = sem("consts"), sem("own_ready"), sem("indexed"), sem("sent")
        loaded, gathered = [sem(f"loaded{p}") for p in range(2)], [sem(f"gathered{p}") for p in range(2)]
        stored = [sem(f"stored{p}") for p in range(2)]
        relued, combined, turned, halved, split = (sem(s) for s in ("relued", "combined", "turned", "halved", "split"))
        produced, biased, measured = sem("produced"), sem("biased"), sem("measured")
        HALF = HC // 2

        with nc.Block() as block:
            @block.sync
            def _(sp):
                column_loads(sp, bias[:], [b1], consts)
                sp.dma_start(own[:], eps.to_broadcast([P, 1])).then_inc(consts, 16)

                def load(g, par, i, slot, lap, tail):
                    sp.wait_ge(relued, tiles_two_before(g))
                    load_group(sp, xin[:, par], x, g, tail, loaded[par])

                each_node_group(sp, load)

            @block.gpsimd
            def _(pl):
                def fetch(g, par, i, slot, lap, tail):
                    pl.wait_ge(turned, tiles_two_before(g))
                    tiles = tiles_of(tail)
                    nc.gpsimd.tensor_copy(index[:, par, 0:tiles], t.last[0][:, DS(g * GT, tiles)]).then_inc(indexed, 1)
                    pl.wait_ge(indexed, g + 1)
                    pl.sem_inc(sent, 1)
                    for k in range(tiles):
                        nc.gpsimd.indirect_dma_start(out=agg[:, par, k, :], out_offset=None, in_=t.seg_in,
                                                     in_offset=bass.IndirectOffsetOnAxis(ap=index[:, par, k:k + 1], axis=0)).then_inc(gathered[par], 16)

                each_node_group(pl, fetch)

            @block.vector
            def _(v):
                v.sem_inc(combined, TILE_CREDIT)
                v.sem_inc(split, TILE_CREDIT)
                v.sem_inc(measured, HC)
                norm_credit_vector(v, norm)
                v.wait_ge(consts, 32)
                nc.vector.tensor_scalar(own[:], own[:], 1.0, None, ALU.add).then_inc(own_ready, 1)

                def combine(g, par, i, slot, lap, tail):
                    tiles = tiles_of(tail)
                    v.wait_ge(loaded[par], loads_done(i, tail))
                    norm_statistics(nc, v, norm, xin[:, par], g, par, tiles)
                    norm_coefficients(nc, v, norm, g, par, tiles)
                    v.wait_ge(gathered[par], 64 * i + 16 * tiles)
                    v.wait_ge(own_ready, 1)
                    for k in range(tiles):
                        v.wait_ge(relued, tile_done(g, k))
                        nc.vector.scalar_tensor_tensor(agg[:, par, k, :], h[:, par, k, :], own[:], agg[:, par, k, :], ALU.mult, ALU.add).then_inc(combined, 1)

                def lows(g, par, tail):
                    for k in range(tiles_of(tail)):
                        v.wait_ge(halved, tile_done(g, k))
                        cols = slice(k * P, (k + 1) * P)
                        nc.vector.tensor_tensor(al[:, par, :, cols], turn_ps[k][:], ah[:, par, :, cols].bitcast(F32), ALU.subtract).then_inc(split, 1)

                def measure_y(g, tail, chunks):
                    for m in chunks:
                        v.wait_ge(biased, HC * g + m + 5)
                        nc.vector.bn_stats(stats[:, m, DS(g, 1), :].rearrange("p o s -> p (o s)"), y[:, m, 0:(TAIL if tail else GR)]).then_inc(measured, 1)

                def start(g, par, i, slot, lap, tail):
                    combine(g, par, i, slot, lap, tail)
                    lows(g, par, tail)

                def body(g, par, i, slot, lap, tail, nxt):
                    if nxt:
                        combine(*nxt)
                    measure_y(g, tail, range(HALF))
                    if nxt:
                        lows(nxt[0], nxt[1], nxt[-1])
                    measure_y(g, tail, range(HALF, HC))

                node_groups(v, start, body)

            @block.scalar
            def _(a):
                norm_credit_scalar(a, norm)
                a.sem_inc(relued, TILE_CREDIT)
                a.sem_inc(halved, TILE_CREDIT)
                a.sem_inc(biased, 4)
                a.wait_ge(consts, 32)

                def apply(g, par, i, slot, lap, tail):
                    norm_root(nc, a, norm, t, g, par, tiles_of(tail))
                    a.wait_ge(norm.ready, group_done(g))
                    a.wait_ge(combined, tiles_two_before(g))
                    for k in range(tiles_of(tail)):
                        nc.scalar.activation(h[:, par, k, :], xin[:, par, k, :], ACT.Relu, bias=norm.shift[:, par, k:k + 1],
                                             scale=norm.scale[:, par, k:k + 1]).then_inc(relued, 1)

                def highs(g, par, tail):
                    a.wait_ge(produced, HC * g + 4)
                    for k in range(tiles_of(tail)):
                        a.wait_ge(turned, tile_done(g, k))
                        nc.scalar.copy(ah[:, par, :, k * P:(k + 1) * P], turn_ps[k][:]).then_inc(halved, 1)

                def finish(g, i, tail, half):
                    cols = TAIL if tail else GR
                    wait_uses(a, stored[half], 16 * g)
                    for m in range(half * HALF, (half + 1) * HALF):
                        a.wait_ge(produced, HC * g + m + HC + 5)
                        a.wait_ge(measured, HC * g + m + 1)
                        nc.scalar.activation(y[:, m, 0:cols], y_ps[m % 4][:, 0:cols], ACT.Identity, bias=bias[:, 0, m:m + 1]).then_inc(biased, 1)
                    a.wait_ge(biased, HC * g + (half + 1) * HALF + 4)
                    a.dma_start(t.y1[DS(g, 1), :, half * HALF:(half + 1) * HALF, 0:cols].rearrange("o p c n -> p (o c) n"),
                                y[:, half * HALF:(half + 1) * HALF, 0:cols]).then_inc(stored[half], 16)

                def start(g, par, i, slot, lap, tail):
                    apply(g, par, i, slot, lap, tail)
                    highs(g, par, tail)

                def body(g, par, i, slot, lap, tail, nxt):
                    if nxt:
                        apply(*nxt)
                    finish(g, i, tail, 0)
                    if nxt:
                        highs(nxt[0], nxt[1], nxt[-1])
                    finish(g, i, tail, 1)

                node_groups(a, start, body)
                for half in range(2):
                    a.wait_ge(stored[half], 16 * NG)

            @block.tensor
            def _(pe):
                pe.sem_inc(turned, TILE_CREDIT)
                pe.sem_inc(produced, HC + 4)

                def turn(g, par, i, slot, lap, tail):
                    for k in range(tiles_of(tail)):
                        pe.wait_ge(combined, tile_done(g, k))
                        pe.wait_ge(split, tile_before(g, k))
                        for c in range(DC):
                            mm = nc.tensor.transpose(turn_ps[k][:, c, :], agg[:, par, k, c * P:(c + 1) * P], t.ident[:])
                        mm.then_inc(turned, 1)

                def product(g, par, tail, chunks):
                    cols = TAIL if tail else GR
                    for m in chunks:
                        pe.wait_ge(biased, HC * g + m + 1)
                        for c in range(DC):
                            mm = product3(nc, y_ps[m % 4][:, 0:cols], wh[:, c, m * P:(m + 1) * P], wl[:, c, m * P:(m + 1) * P],
                                          ah[:, par, c, 0:cols], al[:, par, c, 0:cols], c == 0, c == DC - 1)
                        mm.then_inc(produced, 1)

                def body(g, par, i, slot, lap, tail, nxt):
                    pe.wait_ge(split, tile_done(g, tiles_of(tail) - 1))
                    product(g, par, tail, range(HALF))
                    if nxt:
                        turn(*nxt)
                    product(g, par, tail, range(HALF, HC))

                node_groups(pe, turn, body)


def batch_norm_coefficients(nc, t, stats, gamma, beta, coef, chunks, name, parts=()):
    with ExitStack() as ctx:
        ctx.enter_context(nc.cleanup_on_exit())
        def sb(what, shape):
            return ctx.enter_context(nc.sbuf_tensor(f"{name}_{what}", shape, F32))

        def sem(what):
            return nc.alloc_semaphore(f"{name}_{what}")

        gb, mv = sb("gb", [P, 2, chunks]), sb("mv", [P, chunks, 2])
        root, half = sb("root", [P, chunks]), sb("half", [P, chunks])
        raw = [ctx.enter_context(nc.sbuf_tensor(f"{name}_raw{n}", list(part[0].shape), F32)) for n, part in enumerate(parts)]
        loaded, step, rooted = sem("loaded"), sem("step"), sem("rooted")
        w_loaded, w_halved = sem("w_loaded"), sem("w_halved")
        with nc.Block() as block:
            @block.sync
            def _(sp):
                column_loads(sp, gb[:], [gamma, beta], loaded)
                for view, part in zip(raw, parts):
                    sp.dma_start(view[:], part[0]).then_inc(w_loaded, 16)

            @block.scalar
            def _(a):
                a.wait_ge(step, chunks)
                nc.scalar.activation(root[:], mv[:, :, 1], ACT.Sqrt, bias=t.eps[:]).then_inc(rooted, 1)

            @block.vector
            def _(v):
                n = [0]

                def link(ins):
                    n[0] += 1
                    ins.then_inc(step, 1)
                    v.wait_ge(step, n[0])

                for m in range(chunks):
                    link(nc.vector.bn_aggr(mv[:, m, :], stats[:, m].rearrange("p g s -> p (g s)")))
                v.wait_ge(rooted, 1)
                v.wait_ge(loaded, 32)
                link(nc.vector.reciprocal(root[:], root[:]))
                finish_rsqrt(nc, link, root[:], half[:], mv[:, :, 1], LN_EPS)
                link(nc.vector.tensor_tensor(coef[:, 0, :], gb[:, 0, :], root[:], ALU.mult))
                link(nc.vector.tensor_tensor(half[:], mv[:, :, 0], coef[:, 0, :], ALU.mult))
                link(nc.vector.tensor_tensor(coef[:, 1, :], gb[:, 1, :], half[:], ALU.subtract))
                if parts:
                    split_weights(nc, v, parts, [view[:] for view in raw], w_loaded, w_halved)


def gin_down(nc, t, up_stats, g1, be1, w2, b2, coef, stats):
    with ExitStack() as ctx:
        ctx.enter_context(nc.cleanup_on_exit())
        def sb(what, shape, dt=F32):
            return ctx.enter_context(nc.sbuf_tensor(f"down_{what}", shape, dt))

        def sem(what):
            return nc.alloc_semaphore(f"down_{what}")

        wh, wl = sb("wh", [P, HC, D], F32R), sb("wl", [P, HC, D], F32R)
        batch_norm_coefficients(nc, t, up_stats, g1, be1, coef, HC, "bn1", [(w2.rearrange("(c p) n -> p c n", p=P), wh[:], wl[:])])
        bias = sb("bias", [P, 1, DC])
        z = sb("z", [P, 2, HC, GR])
        zh, zl = sb("zh", [P, HC, GR], F32R), sb("zl", [P, HC, GR], F32R)
        y = sb("y", [P, 2, DC, GR])
        psum = [ctx.enter_context(nc.psum_tensor(f"down_ps{i}", [P, GR], F32)) for i in range(8)]
        consts, placed, fetched, listed = sem("consts"), sem("placed"), sem("fetched"), sem("listed")
        loaded, stored = [sem(f"loaded{p}") for p in range(2)], [sem(f"stored{p}") for p in range(2)]
        relued, halved, split, used = sem("relued"), sem("halved"), sem("split"), sem("used")
        produced, biased, measured = sem("produced"), sem("biased"), sem("measured")

        with nc.Block() as block:
            @block.sync
            def _(sp):
                column_loads(sp, bias[:], [b2], consts)

                def load(g, par, i, slot, lap, tail):
                    cols = TAIL if tail else GR
                    sp.wait_ge(split, HC * g + HC)
                    sp.dma_start(z[:, par, :, 0:cols], t.y1[DS(g, 1), :, :, 0:cols].rearrange("o p c n -> p (o c) n")).then_inc(loaded[par], 16)

                each_node_group(sp, load)

            @block.gpsimd
            def _(pl):
                scatter_edges(nc, pl, t, 1, placed)
                fetch_other_ends(nc, pl, t, 0, fetched, listed)

            @block.scalar
            def _(a):
                a.sem_inc(relued, HC)
                a.sem_inc(biased, TILE_CREDIT)
                a.wait_ge(consts, 16)

                def apply(g, par, i, slot, lap, tail):
                    cols = TAIL if tail else GR
                    a.wait_ge(loaded[par], 16 * (i + 1))
                    for m in range(HC):
                        nc.scalar.activation(z[:, par, m, 0:cols], z[:, par, m, 0:cols], ACT.Relu, bias=coef[:, 1, m:m + 1],
                                             scale=coef[:, 0, m:m + 1]).then_inc(relued, 1)

                def body(g, par, i, slot, lap, tail, nxt):
                    cols = TAIL if tail else GR
                    if nxt:
                        apply(*nxt)
                    wait_uses(a, stored[par], 16 * i)
                    a.wait_ge(measured, tiles_two_before(g))
                    for m in range(DC):
                        a.wait_ge(produced, tile_done(g, m))
                        nc.scalar.activation(y[:, par, m, 0:cols], psum[4 * par + m][:, 0:cols], ACT.Identity, bias=bias[:, 0, m:m + 1]).then_inc(biased, 1)
                    a.wait_ge(biased, tile_done(g, DC - 1))
                    a.dma_start(t.y2[DS(g, 1), :, :, 0:cols].rearrange("o p c n -> p (o c) n"), y[:, par, :, 0:cols]).then_inc(stored[par], 16)

                node_groups(a, apply, body)
                for par in range(2):
                    a.wait_ge(stored[par], 16 * (NG // 2))

            @block.vector
            def _(v):
                v.sem_inc(halved, HC)
                v.sem_inc(split, 2 * HC)
                v.sem_inc(measured, TILE_CREDIT)

                def halve(g, par, i, slot, lap, tail):
                    cols = TAIL if tail else GR
                    for m in range(HC):
                        v.wait_ge(relued, HC * g + m + HC + 1)
                        if m < HC - 1:
                            v.wait_ge(used, (HC - 1) * g + m + 1)
                        else:
                            v.wait_ge(produced, tile_before(g, DC - 1))
                        nc.vector.tensor_copy(zh[:, m, 0:cols], z[:, par, m, 0:cols]).then_inc(halved, 1)
                        if m > 0:
                            lower(g, par, m - 1, cols)
                    lower(g, par, HC - 1, cols)

                def lower(g, par, m, cols):
                    v.wait_ge(halved, HC * g + m + HC + 1)
                    nc.vector.tensor_tensor(zl[:, m, 0:cols], z[:, par, m, 0:cols], zh[:, m, 0:cols].bitcast(F32), ALU.subtract).then_inc(split, 1)

                def body(g, par, i, slot, lap, tail, nxt):
                    if nxt:
                        halve(*nxt)
                    for m in range(DC):
                        v.wait_ge(biased, tile_done(g, m))
                        nc.vector.bn_stats(stats[:, m, DS(g, 1), :].rearrange("p o s -> p (o s)"), y[:, par, m, 0:(TAIL if tail else GR)]).then_inc(measured, 1)

                node_groups(v, halve, body)

            @block.tensor
            def _(pe):
                pe.sem_inc(used, HC - 1)
                pe.sem_inc(produced, TILE_CREDIT)

                def body(g, par, i, slot, lap, tail, nxt):
                    cols = TAIL if tail else GR
                    pe.wait_ge(biased, tiles_two_before(g))
                    for c in range(HC):
                        pe.wait_ge(split, HC * g + c + 2 * HC + 1)
                        for m in range(DC):
                            mm = product3(nc, psum[4 * par + m][:, 0:cols], wh[:, c, m * P:(m + 1) * P], wl[:, c, m * P:(m + 1) * P],
                                          zh[:, c, 0:cols], zl[:, c, 0:cols], c == 0, c == HC - 1)
                            if c == HC - 1:
                                mm.then_inc(produced, 1)
                            elif m == DC - 1:
                                mm.then_inc(used, 1)

                node_groups(pe, nothing, body)


def gin_out(nc, t, x, coef):
    with ExitStack() as ctx:
        ctx.enter_context(nc.cleanup_on_exit())
        def sb(what, shape, dt=F32):
            return ctx.enter_context(nc.sbuf_tensor(f"out_{what}", shape, dt))

        def sem(what):
            return nc.alloc_semaphore(f"out_{what}")

        xin, h, u = sb("x", [P, 4, GT, D]), sb("h", [P, 2, GT, D]), sb("u", [P, 4, DC, GR])
        out = sb("out", [P, 2, GT, D])
        psum = [ctx.enter_context(nc.psum_tensor(f"out_ps{i}", [P, DC, P], F32)) for i in range(8)]
        norm = make_norm(nc, ctx, "outn")
        loaded, stored = [sem(f"loaded{s}") for s in range(4)], [sem(f"stored{p}") for p in range(2)]
        u_loaded = [sem(f"u_loaded{s}") for s in range(4)]
        fetched, listed = sem("fetched"), sem("listed")
        activated, relued, turned, added, finished = (sem(s) for s in ("activated", "relued", "turned", "added", "finished"))

        with nc.Block() as block:
            @block.sync
            def _(sp):
                def load(g, par, i, slot, lap, tail):
                    cols = TAIL if tail else GR
                    wait_uses(sp, finished, tiles_four_before(g))
                    load_group(sp, xin[:, slot], x, g, tail, loaded[slot])
                    wait_uses(sp, turned, tiles_four_before(g))
                    sp.dma_start(u[:, slot, :, 0:cols], t.y2[DS(g, 1), :, :, 0:cols].rearrange("o p c n -> p (o c) n")).then_inc(u_loaded[slot], 16)

                each_node_group(sp, load)

            @block.gpsimd
            def _(pl):
                fetch_other_ends(nc, pl, t, 1, fetched, listed)

            @block.scalar
            def _(a):
                norm_credit_scalar(a, norm)
                a.sem_inc(activated, TILE_CREDIT)
                a.sem_inc(relued, TILE_CREDIT)

                def apply(g, par, i, slot, lap, tail):
                    cols = TAIL if tail else GR
                    a.wait_ge(u_loaded[slot], 16 * (lap + 1))
                    for c in range(DC):
                        nc.scalar.activation(u[:, slot, c, 0:cols], u[:, slot, c, 0:cols], ACT.Relu, bias=coef[:, 1, c:c + 1],
                                             scale=coef[:, 0, c:c + 1]).then_inc(activated, 1)
                    norm_root(nc, a, norm, t, g, par, tiles_of(tail))
                    a.wait_ge(norm.ready, group_done(g))
                    a.wait_ge(added, tiles_two_before(g))
                    for k in range(tiles_of(tail)):
                        nc.scalar.activation(h[:, par, k, :], xin[:, slot, k, :], ACT.Relu, bias=norm.shift[:, par, k:k + 1],
                                             scale=norm.scale[:, par, k:k + 1]).then_inc(relued, 1)

                def body(g, par, i, slot, lap, tail, nxt):
                    if nxt:
                        apply(*nxt)
                    a.wait_ge(finished, tile_done(g, tiles_of(tail) - 1))
                    store_group(a, t.x1, out[:, par], g, tail, stored[par])

                node_groups(a, apply, body)
                a.wait_ge(stored[0], 16 * (NG // 2))
                a.wait_ge(stored[1], 16 * (NG // 2 + 1))

            @block.tensor
            def _(pe):
                pe.sem_inc(turned, TILE_CREDIT)

                def body(g, par, i, slot, lap, tail, nxt):
                    pe.wait_ge(activated, tile_done(g, DC - 1))
                    pe.wait_ge(added, tiles_two_before(g))
                    for k in range(tiles_of(tail)):
                        for c in range(DC):
                            mm = nc.tensor.transpose(psum[4 * par + k][:, c, :], u[:, slot, c, k * P:(k + 1) * P], t.ident[:])
                        mm.then_inc(turned, 1)

                node_groups(pe, nothing, body)

            @block.vector
            def _(v):
                norm_credit_vector(v, norm)
                v.sem_inc(added, TILE_CREDIT)
                v.sem_inc(finished, TILE_CREDIT)

                def measure(g, par, i, slot, lap, tail):
                    v.wait_ge(loaded[slot], loads_done(lap, tail))
                    norm_statistics(nc, v, norm, xin[:, slot], g, par, tiles_of(tail))
                    norm_coefficients(nc, v, norm, g, par, tiles_of(tail))

                def body(g, par, i, slot, lap, tail, nxt):
                    if nxt:
                        measure(*nxt)
                    tiles = tiles_of(tail)
                    wait_uses(v, stored[par], 16 * i)
                    for k in range(tiles):
                        v.wait_ge(turned, tile_done(g, k))
                        v.wait_ge(relued, tile_done(g, k))
                        nc.vector.tensor_tensor(h[:, par, k, :], h[:, par, k, :], psum[4 * par + k][:].rearrange("p c n -> p (c n)"), ALU.add).then_inc(added, 1)
                    for k in range(tiles):
                        v.wait_ge(added, tile_done(g, k))
                        nc.vector.tensor_tensor(out[:, par, k, :], xin[:, slot, k, :], h[:, par, k, :], ALU.add).then_inc(finished, 1)

                node_groups(v, measure, body)


def row_broadcast(eng, dst, vec, sem):
    eng.dma_start(dst, vec.rearrange("(o d) -> o d", o=1).to_broadcast([P, vec.shape[0]])).then_inc(sem, 16)


def gcn(nc, t, layer, rows, w, b, out_rows, residual=None):
    normed = layer == 0
    name = f"gcn{layer}"
    with ExitStack() as ctx:
        ctx.enter_context(nc.cleanup_on_exit())
        def sb(what, shape, dt=F32):
            return ctx.enter_context(nc.sbuf_tensor(f"{name}_{what}", shape, dt))

        def sem(what):
            return nc.alloc_semaphore(f"{name}_{what}")

        wh, wl = sb("wh", [P, DC, D], F32R), sb("wl", [P, DC, D], F32R)
        complete_and_load(nc, t, name + "w", [(0, t.seg_in)], [(w.rearrange("(c p) n -> p c n", p=P), wh[:], wl[:])])
        bias = sb("bias", [P, D])
        xin, agg = sb("x", [P, 4, GT, D]), sb("agg", [P, 2, GT, D])
        s = sb("s", [P, 2, GT, D]) if normed else None
        res = sb("res", [P, 2, GT, D]) if residual is not None else None
        ah, al = sb("ah", [P, 2, GT, DC, P], F32R), sb("al", [P, 2, GT, DC, P], F32R)
        tmp, out = sb("tmp", [P, GT, D]), sb("out", [P, 2, GT, D])
        index = sb("index", [P, 2, GT], I32)
        turn_ps = [ctx.enter_context(nc.psum_tensor(f"{name}_tps{i}", [P, DC, P], F32)) for i in range(4)]
        row_ps = [ctx.enter_context(nc.psum_tensor(f"{name}_rps{i}", [P, D], F32)) for i in range(4)]
        norm = make_norm(nc, ctx, name + "n") if normed else None
        consts, indexed, sent = sem("consts"), sem("indexed"), sem("sent")
        loaded, gathered = [sem(f"loaded{s}") for s in range(4)], [sem(f"gathered{p}") for p in range(2)]
        res_loaded, stored = [sem(f"res_loaded{p}") for p in range(2)], [sem(f"stored{p}") for p in range(2)]
        relued, combined, turned, halved, split = (sem(n) for n in ("relued", "combined", "turned", "halved", "split"))
        produced, scaled, finished = sem("produced"), sem("scaled"), sem("finished")
        used = relued if normed else combined

        with nc.Block() as block:
            @block.sync
            def _(sp):
                row_broadcast(sp, bias[:], b, consts)

                def load(g, par, i, slot, lap, tail):
                    wait_uses(sp, used, tiles_four_before(g))
                    load_group(sp, xin[:, slot], rows, g, tail, loaded[slot])
                    if residual is not None:
                        sp.wait_ge(finished, tiles_two_before(g))
                        load_group(sp, res[:, par], residual, g, tail, res_loaded[par])

                each_node_group(sp, load)

            @block.gpsimd
            def _(pl):
                def fetch(g, par, i, slot, lap, tail):
                    tiles = tiles_of(tail)
                    pl.wait_ge(turned, tiles_two_before(g))
                    nc.gpsimd.tensor_copy(index[:, par, 0:tiles], t.last[0][:, DS(g * GT, tiles)]).then_inc(indexed, 1)
                    pl.wait_ge(indexed, g + 1)
                    pl.sem_inc(sent, 1)
                    for k in range(tiles):
                        nc.gpsimd.indirect_dma_start(out=agg[:, par, k, :], out_offset=None, in_=t.seg_in,
                                                     in_offset=bass.IndirectOffsetOnAxis(ap=index[:, par, k:k + 1], axis=0)).then_inc(gathered[par], 16)

                each_node_group(pl, fetch)

            @block.vector
            def _(v):
                v.sem_inc(combined, TILE_CREDIT)
                v.sem_inc(split, TILE_CREDIT)
                v.sem_inc(scaled, TILE_CREDIT)
                if normed:
                    norm_credit_vector(v, norm)
                else:
                    v.sem_inc(finished, TILE_CREDIT)
                v.wait_ge(consts, 16)

                def combine(g, par, i, slot, lap, tail):
                    tiles = tiles_of(tail)
                    v.wait_ge(loaded[slot], loads_done(lap, tail))
                    if normed:
                        norm_statistics(nc, v, norm, xin[:, slot], g, par, tiles)
                        norm_coefficients(nc, v, norm, g, par, tiles, t.dis[:, DS(g * GT, tiles)])
                    v.wait_ge(gathered[par], 64 * i + 16 * tiles)
                    for k in range(tiles):
                        if normed:
                            v.wait_ge(relued, tile_done(g, k))
                        nc.vector.tensor_tensor(agg[:, par, k, :], agg[:, par, k, :], (s[:, par, k, :] if normed else xin[:, slot, k, :]), ALU.add).then_inc(combined, 1)

                def lower(g, par, i, slot, lap, tail):
                    for k in range(tiles_of(tail)):
                        v.wait_ge(halved, tile_done(g, k))
                        nc.vector.tensor_tensor(al[:, par, k], turn_ps[k][:], ah[:, par, k].bitcast(F32), ALU.subtract).then_inc(split, 1)

                def start(g, par, i, slot, lap, tail):
                    combine(g, par, i, slot, lap, tail)
                    lower(g, par, i, slot, lap, tail)

                def body(g, par, i, slot, lap, tail, nxt):
                    if nxt:
                        combine(*nxt)
                    if nxt and not normed:
                        lower(*nxt)
                    if not normed:
                        wait_uses(v, stored[par], 16 * i)
                        v.wait_ge(res_loaded[par], loads_done(i, tail))
                    for k in range(tiles_of(tail)):
                        v.wait_ge(produced, tile_done(g, k))
                        v.wait_ge(finished, tile_before(g, k))
                        nc.vector.scalar_tensor_tensor(tmp[:, k, :], row_ps[k][:], t.dis[:, DS(g * GT + k, 1)], bias[:], ALU.mult, ALU.add).then_inc(scaled, 1)
                    if nxt and normed:
                        lower(*nxt)
                    if not normed:
                        for k in range(tiles_of(tail)):
                            v.wait_ge(scaled, tile_done(g, k))
                            nc.vector.tensor_tensor(out[:, par, k, :], tmp[:, k, :], res[:, par, k, :], ALU.add).then_inc(finished, 1)

                node_groups(v, start, body)

            @block.scalar
            def _(a):
                a.sem_inc(halved, TILE_CREDIT)
                if normed:
                    a.sem_inc(relued, TILE_CREDIT)
                    a.sem_inc(finished, TILE_CREDIT)
                    norm_credit_scalar(a, norm)

                def apply(g, par, i, slot, lap, tail):
                    if normed:
                        norm_root(nc, a, norm, t, g, par, tiles_of(tail))
                        a.wait_ge(norm.ready, group_done(g))
                        a.wait_ge(combined, tiles_two_before(g))
                        for k in range(tiles_of(tail)):
                            nc.scalar.activation(s[:, par, k, :], xin[:, slot, k, :], ACT.Relu, bias=norm.shift[:, par, k:k + 1],
                                                 scale=norm.scale[:, par, k:k + 1]).then_inc(relued, 1)

                def higher(g, par, i, slot, lap, tail):
                    a.wait_ge(produced, tiles_two_before(g))
                    for k in range(tiles_of(tail)):
                        a.wait_ge(turned, tile_done(g, k))
                        nc.scalar.copy(ah[:, par, k], turn_ps[k][:]).then_inc(halved, 1)

                def start(g, par, i, slot, lap, tail):
                    apply(g, par, i, slot, lap, tail)
                    higher(g, par, i, slot, lap, tail)

                def body(g, par, i, slot, lap, tail, nxt):
                    if nxt:
                        apply(*nxt)
                    if nxt:
                        higher(*nxt)
                    if normed:
                        wait_uses(a, stored[par], 16 * i)
                        for k in range(tiles_of(tail)):
                            a.wait_ge(scaled, tile_done(g, k))
                            nc.scalar.activation(out[:, par, k, :], tmp[:, k, :], ACT.Relu, scale=t.dis[:, DS(g * GT + k, 1)]).then_inc(finished, 1)
                    a.wait_ge(finished, tile_done(g, tiles_of(tail) - 1))
                    store_group(a, out_rows, out[:, par], g, tail, stored[par])

                node_groups(a, start, body)
                a.wait_ge(stored[0], 16 * (NG // 2))
                a.wait_ge(stored[1], 16 * (NG // 2 + 1))

            @block.tensor
            def _(pe):
                pe.sem_inc(turned, TILE_CREDIT)
                pe.sem_inc(produced, TILE_CREDIT)

                def turn(g, par, i, slot, lap, tail):
                    for k in range(tiles_of(tail)):
                        pe.wait_ge(combined, tile_done(g, k))
                        pe.wait_ge(split, tile_before(g, k))
                        for c in range(DC):
                            mm = nc.tensor.transpose(turn_ps[k][:, c, :], agg[:, par, k, c * P:(c + 1) * P], t.ident[:])
                        mm.then_inc(turned, 1)

                def body(g, par, i, slot, lap, tail, nxt):
                    for k in range(tiles_of(tail)):
                        pe.wait_ge(split, tile_done(g, k))
                        pe.wait_ge(scaled, tile_before(g, k))
                        for c in range(DC):
                            mm = product3(nc, row_ps[k][:], ah[:, par, k, c, :], al[:, par, k, c, :], wh[:, c, :], wl[:, c, :], c == 0, c == DC - 1)
                        mm.then_inc(produced, 1)
                        if nxt and k == (tiles_of(tail) - 1 if normed else 1):
                            turn(*nxt)

                node_groups(pe, turn, body)


BT = ET // 2
TERMS = 8
BG = BT // GT


def path_products(nc, t, rows, edge_attr, paths, coeffs):
    with ExitStack() as ctx:
        ctx.enter_context(nc.cleanup_on_exit())

        def sb(what, shape, dt=F32):
            return ctx.enter_context(nc.sbuf_tensor(f"path_{what}", shape, dt))

        def sem(what):
            return nc.alloc_semaphore(f"path_{what}")

        h, attr, o = sb("h", [P, BT, D]), sb("attr", [P, BT, D]), sb("o", [P, BT, D])
        term = sb("term", [P, TERMS, BT, EXT])
        same = sb("same", [P, 2, GT, P])
        out = sb("out", [P, 2, GT, D])
        coef, ids, code = sb("coef", [P, PATHS]), sb("ids", [1, PATHS, 3], I32), sb("code", [1, PATHS // 2], I32)
        code_f = sb("code_f", [1, 2, PATHS])
        psum = [ctx.enter_context(nc.psum_tensor(f"path_ps{i}", [P, D], F32)) for i in range(8)]
        norm = make_norm(nc, ctx, "pathn")
        consts, coded_step = sem("consts"), sem("coded_step")
        gathered, attr_got, stored = [sem(f"gathered{b}") for b in range(BG)], sem("attr_got"), sem("stored")
        relued, cleared, multiplied, accumulated = sem("relued"), sem("cleared"), sem("multiplied"), sem("accumulated")
        widened, summed, copied = sem("widened"), sem("summed"), sem("copied")
        ALL = 2 * BG

        with nc.Block() as block:
            @block.sync
            def _(sp):
                sp.dma_start(coef[:], coeffs.rearrange("(o d) -> o d", o=1).to_broadcast([P, PATHS])).then_inc(consts, 16)
                sp.dma_start(ids[:].rearrange("o a b -> o (a b)"), paths.rearrange("(o a) b -> o (a b)", o=1)).then_inc(consts, 16)
                for g in range(ALL):
                    sp.wait_ge(copied, GT * (g + 1))
                    if g:
                        sp.wait_ge(stored, 16 * g)
                    sp.dma_start(t.seg_in[g * GR:(g + 1) * GR, :].rearrange("(k p) d -> p k d", p=P), out[:, g % 2]).then_inc(stored, 16)
                sp.wait_ge(stored, 16 * ALL)

            @block.gpsimd
            def _(pl):
                for batch in range(2):
                    if batch:
                        pl.wait_ge(accumulated, PATHS + TERMS)
                    for k in range(BT):
                        col = batch * BT + k
                        nc.gpsimd.indirect_dma_start(out=h[:, k, :], out_offset=None, in_=rows,
                                                     in_offset=bass.IndirectOffsetOnAxis(ap=t.other[0][:, col:col + 1], axis=0)).then_inc(gathered[k // GT], 16)
                    for k in range(BT):
                        col = batch * BT + k
                        nc.gpsimd.indirect_dma_start(out=attr[:, k, :], out_offset=None, in_=edge_attr,
                                                     in_offset=bass.IndirectOffsetOnAxis(ap=t.eid[0][:, col:col + 1], axis=0)).then_inc(attr_got, 16)

            @block.vector
            def _(v):
                norm_credit_vector(v, norm)
                v.sem_inc(accumulated, TERMS)
                v.wait_ge(consts, 32)
                nc.vector.tensor_scalar(code_f[:, 0], ids[:, :, 2], float(SEG), None, ALU.mult).then_inc(coded_step, 1)
                v.wait_ge(coded_step, 1)
                nc.vector.tensor_tensor(code_f[:, 1], code_f[:, 0], ids[:, :, 1], ALU.add).then_inc(coded_step, 1)
                v.wait_ge(coded_step, 2)
                nc.vector.tensor_scalar(code_f[:, 0], code_f[:, 1], float(SEG), None, ALU.mult).then_inc(coded_step, 1)
                v.wait_ge(coded_step, 3)
                nc.vector.tensor_tensor(code_f[:, 1], code_f[:, 0], ids[:, :, 0], ALU.add).then_inc(coded_step, 1)
                v.wait_ge(coded_step, 4)
                pairs = code_f[:, 1].rearrange("o (a two) -> o a two", two=2)
                nc.vector.tensor_scalar(code_f[:, 0, 0:PATHS // 2], pairs[:, :, 1], float(SEG ** 3), None, ALU.mult).then_inc(coded_step, 1)
                v.wait_ge(coded_step, 5)
                nc.vector.tensor_tensor(code[:], code_f[:, 0, 0:PATHS // 2], pairs[:, :, 0], ALU.add).then_inc(coded_step, 1)
                v.wait_ge(coded_step, 6)
                hv, av, ov = (x[:].rearrange("p t (s k) -> p t s k", k=EXT) for x in (h, attr, o))
                for batch in range(2):
                    if batch:
                        v.wait_ge(summed, BT)
                    nc.vector.memset(o[:], 0.0).then_inc(cleared, 1)
                    for b in range(BG):
                        g = batch * BG + b
                        v.wait_ge(gathered[b], GT * 16 * (batch + 1))
                        norm_statistics(nc, v, norm, h[:, b * GT:(b + 1) * GT], g, g % 2, GT)
                        norm_coefficients(nc, v, norm, g, g % 2, GT)
                    v.wait_ge(relued, BT * (batch + 1))
                    v.wait_ge(attr_got, BT * 16 * (batch + 1))
                    v.wait_ge(cleared, batch + 1)
                    with v.Fori(0, PATHS // TERMS) as i:
                        path = TERMS * i
                        done = PATHS * batch + path
                        third = []

                        def multiply(j):
                            if j % 2 == 0:
                                word.append(v.value_load(code[0:1, DS(i * (TERMS // 2) + j // 2, 1)], min_val=0, max_val=SEG ** 6 - 1))
                            own = word[-1] % SEG ** 3 if j % 2 == 0 else word[-1] // SEG ** 3
                            first, second = own % SEG, (own // SEG) % SEG
                            third.append(own // SEG ** 2)
                            v.wait_ge(accumulated, done + j + 1)
                            nc.vector.scalar_tensor_tensor(term[:, j], hv[:, :, DS(first, 1), :].rearrange("p t o k -> p t (o k)"), coef[:, DS(path + j, 1)],
                                                           av[:, :, DS(second, 1), :].rearrange("p t o k -> p t (o k)"), ALU.mult, ALU.mult).then_inc(multiplied, 1)

                        word = []
                        multiply(0)
                        for j in range(TERMS):
                            if j + 1 < TERMS:
                                multiply(j + 1)
                            v.wait_ge(multiplied, done + j + 1)
                            v.wait_ge(accumulated, done + j + TERMS)
                            there = ov[:, :, DS(third[j], 1), :].rearrange("p t o k -> p t (o k)")
                            nc.vector.tensor_tensor(there, there, term[:, j], ALU.add).then_inc(accumulated, 1)

            @block.scalar
            def _(a):
                norm_credit_scalar(a, norm)
                for batch in range(2):
                    for b in range(BG):
                        g = batch * BG + b
                        norm_root(nc, a, norm, t, g, g % 2, GT)
                        a.wait_ge(norm.ready, group_done(g))
                        for k in range(GT):
                            n = b * GT + k
                            nc.scalar.activation(h[:, n, :], h[:, n, :], ACT.Relu, bias=norm.shift[:, g % 2, k:k + 1],
                                                 scale=norm.scale[:, g % 2, k:k + 1]).then_inc(relued, 1)
                    a.wait_ge(accumulated, PATHS * (batch + 1) + TERMS)
                    for b in range(BG):
                        g = batch * BG + b
                        if g >= 2:
                            a.wait_ge(summed, GT * (g - 1))
                        nc.scalar.copy(same[:, g % 2], t.same[0][:, g * GT:(g + 1) * GT, :]).then_inc(widened, 1)
                        if g >= 2:
                            a.wait_ge(stored, 16 * (g - 1))
                        for k in range(GT):
                            a.wait_ge(summed, GT * g + k + 1)
                            nc.scalar.copy(out[:, g % 2, k, :], psum[4 * (g % 2) + k][:]).then_inc(copied, 1)

            @block.tensor
            def _(pe):
                for g in range(ALL):
                    if g % BG == 0:
                        pe.wait_ge(accumulated, PATHS * (g // BG + 1) + TERMS)
                    pe.wait_ge(widened, g + 1)
                    for k in range(GT):
                        if g >= 2:
                            pe.wait_ge(copied, GT * (g - 2) + k + 1)
                        nc.tensor.matmul(psum[4 * (g % 2) + k][:], same[:, g % 2, k, :], o[:, (g % BG) * GT + k, :], start=True, stop=True).then_inc(summed, 1)


def fold_weights(nc, t, wo_w, wi_w, ws_w, mlp_w, wo_b, wi_b, ws_b, mlp_b, folded, const_halves):
    with ExitStack() as ctx:
        ctx.enter_context(nc.cleanup_on_exit())

        def sb(what, shape, dt=F32):
            return ctx.enter_context(nc.sbuf_tensor(f"fold_{what}", shape, dt))

        def sem(what):
            return nc.alloc_semaphore(f"fold_{what}")

        mlp, mlp_t = sb("mlp", [P, DC, 2 * D]), sb("mlp_t", [P, 2 * DC, D])
        w = sb("w", [P, 3, DC, D])
        bcol, bsum, wide = sb("bcol", [P, 3, DC]), sb("bsum", [P, 2, DC]), sb("wide", [P, 2 * DC, P])
        brow = sb("brow", [1, D])
        psum = [ctx.enter_context(nc.psum_tensor(f"fold_ps{i}", [P, D], F32)) for i in range(8)]
        loaded, turned, copied, produced, halved, split = (sem(s) for s in ("loaded", "turned", "copied", "produced", "halved", "split"))
        completion = make_completion(nc, ctx, 0, t.seg_in, "fold", psum[7])
        step, constant, summed = sem("step"), sem("constant"), sem("summed")
        order = [(n, c) for n in range(3) for c in range(DC)]

        with nc.Block() as block:
            @block.sync
            def _(sp):
                load_ends(sp, completion)
                sp.dma_start(mlp[:], mlp_w.rearrange("(c p) n -> p c n", p=P)).then_inc(loaded, 16)
                for n, x in enumerate((ws_w, wo_w, wi_w)):
                    sp.dma_start(w[:, n], x.rearrange("(c p) n -> p c n", p=P)).then_inc(loaded, 16)
                column_loads(sp, bcol[:], [ws_b, wo_b, wi_b], loaded)
                sp.dma_start(brow[:], mlp_b.rearrange("(o d) -> o d", o=1)).then_inc(loaded, 16)

            @block.gpsimd
            def _(pl):
                rewrite_finals(nc, pl, t, [completion])

            @block.tensor
            def _(pe):
                sum_ends(nc, pe, t, completion)
                pe.wait_ge(loaded, 128)
                pe.wait_ge(completion.completed, 1)
                for j in range(2 * DC):
                    for m in range(DC):
                        mm = nc.tensor.transpose(psum[j][:, m * P:(m + 1) * P], mlp[:, m, j * P:(j + 1) * P], t.ident[:])
                    mm.then_inc(turned, 1)
                pe.wait_ge(copied, 2 * DC)
                for i, (n, c) in enumerate(order):
                    if i >= 4:
                        pe.wait_ge(split, i - 3)
                    for j in range(DC):
                        mm = nc.tensor.matmul(psum[i % 4][:], w[:, n, j, c * P:(c + 1) * P], mlp_t[:, (DC if n else 0) + j, :], start=j == 0, stop=j == DC - 1)
                    mm.then_inc(produced, 1)
                pe.wait_ge(step, 3)
                for j in range(2 * DC):
                    mm = nc.tensor.matmul(psum[7][:], wide[:, j, :], mlp_t[:, j, :], start=j == 0, stop=j == 2 * DC - 1)
                mm.then_inc(constant, 1)

            @block.scalar
            def _(a):
                for j in range(2 * DC):
                    a.wait_ge(turned, j + 1)
                    nc.scalar.copy(mlp_t[:, j, :], psum[j][:]).then_inc(copied, 1)
                for i, (n, c) in enumerate(order):
                    a.wait_ge(produced, i + 1)
                    nc.scalar.copy(folded[n][0][:, c, :], psum[i % 4][:]).then_inc(halved, 1)

            @block.vector
            def _(v):
                add_ends(nc, v, completion)
                v.wait_ge(loaded, 128)
                nc.vector.tensor_copy(bsum[:, 0], bcol[:, 0])
                nc.vector.tensor_tensor(bsum[:, 1], bcol[:, 1], bcol[:, 2], ALU.add).then_inc(step, 1)
                v.wait_ge(step, 1)
                nc.vector.tensor_copy(wide[:], bsum[:].rearrange("p a (c o) -> p (a c) o", o=1).to_broadcast([P, 2 * DC, P])).then_inc(step, 2)
                for i, (n, c) in enumerate(order):
                    v.wait_ge(halved, i + 1)
                    nc.vector.tensor_tensor(folded[n][1][:, c, :], psum[i % 4][:], folded[n][0][:, c, :].bitcast(F32), ALU.subtract).then_inc(split, 1)
                v.wait_ge(constant, 1)
                const_high, const_low = const_halves
                nc.vector.tensor_tensor(brow[:], psum[7][0:1, :], brow[:], ALU.add).then_inc(summed, 1)
                v.wait_ge(summed, 1)
                nc.vector.tensor_copy(const_high[:], brow[:]).then_inc(summed, 1)
                v.wait_ge(summed, 2)
                nc.vector.tensor_tensor(const_low[:], brow[:], const_high[:].bitcast(F32), ALU.subtract)


def sum_messages(nc, t, q, rows, edge_attr, weight, table, name):
    with ExitStack() as ctx:
        ctx.enter_context(nc.cleanup_on_exit())

        def sb(what, shape, dt=F32):
            return ctx.enter_context(nc.sbuf_tensor(f"{name}_{what}", shape, dt))

        def sem(what):
            return nc.alloc_semaphore(f"{name}_{what}")

        x, z, attr = sb("x", [P, SLOTS, GT, D]), sb("z", [P, 2, GT, D]), sb("attr", [P, SLOTS, GT, D])
        same = sb("same", [P, 2, GT, P])
        ah, al = sb("ah", [P, GT, DC, P], F32R), sb("al", [P, GT, DC, P], F32R)
        out = sb("out", [P, 2, GT, D])
        turn_ps = [ctx.enter_context(nc.psum_tensor(f"{name}_tps{i}", [P, DC, P], F32)) for i in range(4)]
        row_ps = [ctx.enter_context(nc.psum_tensor(f"{name}_rps{i}", [P, D], F32)) for i in range(4)]
        norm = make_norm(nc, ctx, name + "n")
        wh, wl = weight
        fenced = sem("fenced")
        x_got, attr_got = [sem(f"x_got{s}") for s in range(SLOTS)], [sem(f"attr_got{s}") for s in range(SLOTS)]
        stored = [sem(f"stored{p}") for p in range(2)]
        x_added = [sem(f"x_added{s}") for s in range(SLOTS)]
        relued, formed = sem("relued"), sem("formed")
        widened, summed, t_halved, t_split, produced, copied = (sem(s) for s in ("widened", "summed", "t_halved", "t_split", "produced", "copied"))

        with nc.Block() as block:
            @block.gpsimd
            def _(pl):
                def gather(dst, what, n, g, done, **how):
                    for k in range(GT):
                        index = t.fetch[q][:, g * GT + k, n:n + 1]
                        nc.gpsimd.indirect_dma_start(out=dst[:, g % SLOTS, k, :], out_offset=None, in_=what,
                                                     in_offset=bass.IndirectOffsetOnAxis(ap=index, axis=0), **how).then_inc(done[g % SLOTS], 16)

                for g in range(EG):
                    if g >= SLOTS:
                        pl.wait_ge(formed, tile_done(g - SLOTS, GT - 1))
                    gather(x, rows, 0, g, x_got)
                    gather(attr, edge_attr, 2, g, attr_got)
                    pl.wait_ge(x_got[g % SLOTS], 64 * (g // SLOTS + 1))
                    gather(x, t.seg_in, 1, g, x_added, compute_op=ALU.add)

            @block.vector
            def _(v):
                norm_credit_vector(v, norm)
                for s in (formed, t_split):
                    v.sem_inc(s, TILE_CREDIT)

                def coefficients(g, par, i):
                    v.wait_ge(x_added[g % SLOTS], 64 * (g // SLOTS + 1))
                    norm_statistics(nc, v, norm, x[:, g % SLOTS], g, par, GT)
                    norm_coefficients(nc, v, norm, g, par, GT)

                def body(g, par, i, nxt):
                    v.wait_ge(attr_got[g % SLOTS], 64 * (g // SLOTS + 1))
                    for k in range(GT):
                        v.wait_ge(relued, tile_done(g, k))
                        nc.vector.tensor_tensor(z[:, par, k, :], z[:, par, k, :], attr[:, g % SLOTS, k, :], ALU.subtract).then_inc(formed, 1)
                    if nxt:
                        coefficients(*nxt)
                    for k in range(GT):
                        v.wait_ge(t_halved, tile_done(g, k))
                        nc.vector.tensor_tensor(al[:, k], turn_ps[k][:], ah[:, k].bitcast(F32), ALU.subtract).then_inc(t_split, 1)

                edge_groups(v, coefficients, body)

            @block.scalar
            def _(a):
                norm_credit_scalar(a, norm)
                for s in (relued, t_halved, copied):
                    a.sem_inc(s, TILE_CREDIT)
                a.sem_inc(widened, GROUP_CREDIT)

                def root(g, par, i):
                    a.wait_ge(summed, tiles_two_before(g))
                    nc.scalar.copy(same[:, par], t.same[q][:, DS(g * GT, GT), :]).then_inc(widened, 1)
                    norm_root(nc, a, norm, t, g, par, GT)

                def apply(g, par, i):
                    a.wait_ge(norm.ready, group_done(g))
                    a.wait_ge(summed, tiles_two_before(g))
                    for k in range(GT):
                        nc.scalar.activation(z[:, par, k, :], x[:, g % SLOTS, k, :], ACT.Relu, bias=norm.shift[:, par, k:k + 1],
                                             scale=norm.scale[:, par, k:k + 1]).then_inc(relued, 1)

                def give(g, par, i, k):
                    if k == 0:
                        wait_uses(a, stored[par], 16 * i)
                    a.wait_ge(produced, tile_done(g, k))
                    a.sem_inc(fenced, 1)
                    nc.scalar.activation(out[:, par, k, :], row_ps[k][:], ACT.Identity, scale=t.share[q][:, DS(g * GT + k, 1)]).then_inc(copied, 1)

                def start(g, par, i):
                    root(g, par, i)
                    apply(g, par, i)

                def body(g, par, i, nxt):
                    if nxt:
                        root(*nxt)
                        apply(*nxt)
                    for k in range(GT):
                        a.wait_ge(summed, tile_done(g, k))
                        a.wait_ge(produced, tile_before(g, k))
                        nc.scalar.copy(ah[:, k], turn_ps[k][:]).then_inc(t_halved, 1)
                        if g:
                            give(g - 1, 1 - par, i - 1 + par, k)
                    if not nxt:
                        for k in range(GT):
                            give(g, par, i, k)

                edge_groups(a, start, body)

            @block.tensor
            def _(pe):
                pe.sem_inc(summed, TILE_CREDIT)
                pe.sem_inc(produced, TILE_CREDIT)

                def total(g, par, i):
                    pe.wait_ge(widened, group_done(g))
                    for k in range(GT):
                        pe.wait_ge(formed, tile_done(g, k))
                        pe.wait_ge(t_split, tile_before(g, k))
                        for c in range(DC):
                            mm = nc.tensor.matmul(turn_ps[k][:, c, :], z[:, par, k, c * P:(c + 1) * P], same[:, par, k, :], start=True, stop=True)
                        mm.then_inc(summed, 1)

                def body(g, par, i, nxt):
                    for k in range(GT):
                        pe.wait_ge(t_split, tile_done(g, k))
                        pe.wait_ge(copied, tile_before(g, k))
                        for c in range(DC):
                            mm = product3(nc, row_ps[k][:], ah[:, k, c, :], al[:, k, c, :], wh[:, c, :], wl[:, c, :], c == 0, c == DC - 1)
                        mm.then_inc(produced, 1)
                        if nxt and k == 1:
                            total(*nxt)

                edge_groups(pe, total, body)

            @block.sync
            def _(sp):
                def store(g, par, i, nxt):
                    sp.wait_ge(copied, tile_done(g, GT - 1))
                    sp.dma_start(table[DS(g * GR, GR), :].rearrange("(k p) d -> p k d", p=P), out[:, par]).then_inc(stored[par], 16)

                edge_groups(sp, nothing, store)
                for par in range(2):
                    sp.wait_ge(stored[par], 16 * (EG // 2))


def last_layer(nc, t, rows, weight, const_halves, slope, out_rows):
    name = "last"
    with ExitStack() as ctx:
        ctx.enter_context(nc.cleanup_on_exit())

        def sb(what, shape, dt=F32):
            return ctx.enter_context(nc.sbuf_tensor(f"{name}_{what}", shape, dt))

        def sem(what):
            return nc.alloc_semaphore(f"{name}_{what}")

        wh, wl = weight
        x, h = sb("x", [P, 4, GT, D]), sb("h", [P, GT, D])
        side, bend = sb("side", [P, 2, GT, D]), sb("bend", [P, GT, D])
        ah, al = sb("ah", [P, 2, GT, DC, P], F32R), sb("al", [P, 2, GT, DC, P], F32R)
        out = sb("out", [P, GT, D])
        rest = sb("rest", [P, 1])
        one = sb("one", [1, P], F32R)
        x_index, side_index = sb("x_index", [P, 2, GT], I32), sb("side_index", [P, 2, 2, GT], I32)
        turn_ps = [ctx.enter_context(nc.psum_tensor(f"{name}_tps{i}", [P, DC, P], F32)) for i in range(4)]
        row_ps = [ctx.enter_context(nc.psum_tensor(f"{name}_rps{i}", [P, D], F32)) for i in range(4)]
        norm = make_norm(nc, ctx, name + "n")
        consts, one_ready, rest_ready, indexed, x_indexed, sent = (sem(n) for n in ("consts", "one_ready", "rest_ready", "indexed", "x_indexed", "sent"))
        loaded, x_added = [sem(f"loaded{s}") for s in range(4)], [sem(f"x_added{s}") for s in range(4)]
        side_got, side_added = [sem(f"side_got{p}") for p in range(2)], [sem(f"side_added{p}") for p in range(2)]
        stored = sem("stored")
        relued, turned, halved, split = (sem(n) for n in ("relued", "turned", "halved", "split"))
        produced, z_ready, negated, bent, finished = (sem(n) for n in ("produced", "z_ready", "negated", "bent", "finished"))

        with nc.Block() as block:
            @block.sync
            def _(sp):
                sp.dma_start(rest[:], slope.rearrange("(o d) -> o d", o=1).to_broadcast([P, 1])).then_inc(consts, 16)

                def load(g, par, i, slot, lap, tail):
                    wait_uses(sp, finished, tiles_four_before(g))
                    load_group(sp, x[:, slot], rows, g, tail, loaded[slot])

                each_node_group(sp, load)

            @block.gpsimd
            def _(pl):
                def add_segments(g, par, i, slot, lap, tail):
                    tiles = tiles_of(tail)
                    pl.wait_ge(norm.measured, tiles_two_before(g))
                    pl.sem_inc(sent, 1)
                    nc.gpsimd.tensor_copy(x_index[:, par, 0:tiles], t.last[0][:, DS(g * GT, tiles)]).then_inc(x_indexed, 1)
                    pl.wait_ge(loaded[slot], loads_done(lap, tail))
                    pl.wait_ge(x_indexed, g + 1)
                    pl.sem_inc(sent, 1)
                    for k in range(tiles):
                        nc.gpsimd.indirect_dma_start(out=x[:, slot, k, :], out_offset=None, in_=t.seg_in, compute_op=ALU.add,
                                                     in_offset=bass.IndirectOffsetOnAxis(ap=x_index[:, par, k:k + 1], axis=0)).then_inc(x_added[slot], 16)

                def fetch(g, par, i, slot, lap, tail):
                    tiles = tiles_of(tail)
                    pl.wait_ge(finished, tiles_two_before(g))
                    pl.sem_inc(sent, 1)
                    for q in range(2):
                        nc.gpsimd.tensor_copy(side_index[:, par, q, 0:tiles], t.last[q][:, DS(g * GT, tiles)]).then_inc(indexed, 1)
                    pl.wait_ge(indexed, 2 * g + 2)
                    pl.sem_inc(sent, 1)
                    for k in range(tiles):
                        nc.gpsimd.indirect_dma_start(out=side[:, par, k, :], out_offset=None, in_=t.seg_dst,
                                                     in_offset=bass.IndirectOffsetOnAxis(ap=side_index[:, par, 0, k:k + 1], axis=0)).then_inc(side_got[par], 16)

                def add_other_side(g, par, i, slot, lap, tail):
                    pl.wait_ge(side_got[par], 64 * i + 16 * tiles_of(tail))
                    pl.sem_inc(sent, 1)
                    for k in range(tiles_of(tail)):
                        nc.gpsimd.indirect_dma_start(out=side[:, par, k, :], out_offset=None, in_=t.seg_src, compute_op=ALU.add,
                                                     in_offset=bass.IndirectOffsetOnAxis(ap=side_index[:, par, 1, k:k + 1], axis=0)).then_inc(side_added[par], 16)

                def body(g, par, i, slot, lap, tail, nxt):
                    fetch(g, par, i, slot, lap, tail)
                    if nxt:
                        add_segments(*nxt)
                    add_other_side(g, par, i, slot, lap, tail)

                node_groups(pl, add_segments, body)

            @block.vector
            def _(v):
                norm_credit_vector(v, norm)
                for s in (split, z_ready, bent, finished):
                    v.sem_inc(s, TILE_CREDIT)
                v.wait_ge(consts, 16)
                nc.vector.tensor_scalar(rest[:], rest[:], -1.0, 1.0, ALU.mult, ALU.add).then_inc(rest_ready, 1)
                v.wait_ge(rest_ready, 1)

                def coefficients(g, par, i, slot, lap, tail):
                    v.wait_ge(x_added[slot], 64 * lap + 16 * tiles_of(tail))
                    norm_statistics(nc, v, norm, x[:, slot], g, par, tiles_of(tail))
                    norm_coefficients(nc, v, norm, g, par, tiles_of(tail))

                def lower(g, par, i, slot, lap, tail):
                    for k in range(tiles_of(tail)):
                        v.wait_ge(halved, tile_done(g, k))
                        nc.vector.tensor_tensor(al[:, par, k], turn_ps[k][:], ah[:, par, k].bitcast(F32), ALU.subtract).then_inc(split, 1)

                def start(*group):
                    coefficients(*group)
                    lower(*group)

                def body(g, par, i, slot, lap, tail, nxt):
                    tiles = tiles_of(tail)
                    if nxt:
                        coefficients(*nxt)
                    v.wait_ge(side_added[par], 64 * i + 16 * tiles)
                    for k in range(tiles):
                        v.wait_ge(produced, tile_done(g, k))
                        nc.vector.tensor_tensor(side[:, par, k, :], side[:, par, k, :], row_ps[k][:], ALU.add).then_inc(z_ready, 1)
                    if nxt:
                        lower(*nxt)
                    for k in range(tiles):
                        v.wait_ge(negated, tile_done(g, k))
                        nc.vector.scalar_tensor_tensor(side[:, par, k, :], bend[:, k, :], rest[:], side[:, par, k, :], ALU.mult, ALU.add).then_inc(bent, 1)
                    wait_uses(v, stored, 16 * g)
                    for k in range(tiles):
                        v.wait_ge(bent, tile_done(g, k))
                        nc.vector.tensor_tensor(out[:, k, :], x[:, slot, k, :], side[:, par, k, :], ALU.add).then_inc(finished, 1)

                node_groups(v, start, body)

            @block.scalar
            def _(a):
                norm_credit_scalar(a, norm)
                for s in (relued, halved, negated):
                    a.sem_inc(s, TILE_CREDIT)
                nc.scalar.copy(one[:], t.ones[0:1, :]).then_inc(one_ready, 1)

                def apply(g, par, i, slot, lap, tail):
                    norm_root(nc, a, norm, t, g, par, tiles_of(tail))
                    a.wait_ge(norm.ready, group_done(g))
                    for k in range(tiles_of(tail)):
                        a.wait_ge(turned, tile_before(g, k))
                        nc.scalar.activation(h[:, k, :], x[:, slot, k, :], ACT.Relu, bias=norm.shift[:, par, k:k + 1],
                                             scale=norm.scale[:, par, k:k + 1]).then_inc(relued, 1)

                def higher(g, par, i, slot, lap, tail):
                    a.wait_ge(produced, tiles_two_before(g))
                    for k in range(tiles_of(tail)):
                        a.wait_ge(turned, tile_done(g, k))
                        nc.scalar.copy(ah[:, par, k], turn_ps[k][:]).then_inc(halved, 1)

                def start(*group):
                    apply(*group)
                    higher(*group)

                def body(g, par, i, slot, lap, tail, nxt):
                    if nxt:
                        apply(*nxt)
                    if nxt:
                        higher(*nxt)
                    for k in range(tiles_of(tail)):
                        a.wait_ge(z_ready, tile_done(g, k))
                        a.wait_ge(bent, tile_before(g, k))
                        nc.scalar.activation(bend[:, k, :], side[:, par, k, :], ACT.Relu, scale=-1.0).then_inc(negated, 1)
                    a.wait_ge(finished, tile_done(g, tiles_of(tail) - 1))
                    store_group(a, out_rows, out[:], g, tail, stored)

                node_groups(a, start, body)
                a.wait_ge(stored, 16 * (NG + 1))

            @block.tensor
            def _(pe):
                pe.sem_inc(turned, TILE_CREDIT)
                pe.sem_inc(produced, TILE_CREDIT)
                pe.wait_ge(one_ready, 1)

                def turn(g, par, i, slot, lap, tail):
                    for k in range(tiles_of(tail)):
                        pe.wait_ge(relued, tile_done(g, k))
                        pe.wait_ge(split, tile_before(g, k))
                        for c in range(DC):
                            mm = nc.tensor.transpose(turn_ps[k][:, c, :], h[:, k, c * P:(c + 1) * P], t.ident[:])
                        mm.then_inc(turned, 1)

                def body(g, par, i, slot, lap, tail, nxt):
                    for k in range(tiles_of(tail)):
                        pe.wait_ge(split, tile_done(g, k))
                        pe.wait_ge(z_ready, tile_before(g, k))
                        for half in range(2):
                            nc.tensor.matmul(row_ps[k][:], one[:], const_halves[1 - half][:], start=half == 0, stop=False)
                        for c in range(DC):
                            mm = product3(nc, row_ps[k][:], ah[:, par, k, c, :], al[:, par, k, c, :], wh[:, c, :], wl[:, c, :], False, c == DC - 1)
                        mm.then_inc(produced, 1)
                    if nxt:
                        turn(*nxt)

                node_groups(pe, turn, body)


def gnn_program(nc, x, src, dst, edge_attr, l0_eps, l0_w1, l0_b1, l0_g1, l0_be1, l0_w2, l0_b2, l0_g2, l0_be2,
                l1_w1, l1_b1, l1_w2, l1_b2, coeffs, paths, wo_w, wo_b, wi_w, wi_b, ws_w, ws_b, mlp_w, mlp_b, slope, out):
    with ExitStack() as ctx:
        t = make_tables(nc, ctx)
        sort_edges(nc, t, src, dst)
        index_edges(nc, t, 0)
        sum_segments(nc, t, x, t.seg_in, "ginseg", True)
        with ExitStack() as layer:
            stats1 = layer.enter_context(nc.sbuf_tensor("stats1", [P, HC, NG, 6], F32))
            stats2 = layer.enter_context(nc.sbuf_tensor("stats2", [P, DC, NG, 6], F32))
            coef1 = layer.enter_context(nc.sbuf_tensor("coef1", [P, 2, HC], F32))
            coef2 = layer.enter_context(nc.sbuf_tensor("coef2", [P, 2, DC], F32))
            gin_up(nc, t, x, l0_eps, l0_w1, l0_b1, stats1)
            gin_down(nc, t, stats1, l0_g1, l0_be1, l0_w2, l0_b2, coef1, stats2)
            batch_norm_coefficients(nc, t, stats2, l0_g2, l0_be2, coef2, DC, "bn2")
            index_edges(nc, t, 1)
            gin_out(nc, t, x, coef2)
        sum_segments(nc, t, t.x1, t.seg_in, "gcnseg0", True, t.dis_other)
        gcn(nc, t, 0, t.x1, l1_w1, l1_b1, t.r1)
        sum_segments(nc, t, t.r1, t.seg_in, "gcnseg1", False)
        gcn(nc, t, 1, t.r1, l1_w2, l1_b2, t.x2, t.x1)
        path_products(nc, t, t.x2, edge_attr, paths, coeffs)
        own = [ctx.enter_context(nc.sbuf_tensor(f"folded_s{half}", [P, DC, D], F32R)) for half in "hl"]
        const_halves = [ctx.enter_context(nc.sbuf_tensor(f"const_{half}", [1, D], F32R)) for half in "hl"]
        with ExitStack() as edges:
            ends = [[edges.enter_context(nc.sbuf_tensor(f"folded_{n}{half}", [P, DC, D], F32R)) for half in "hl"] for n in "oi"]
            fold_weights(nc, t, wo_w, wi_w, ws_w, mlp_w, wo_b, wi_b, ws_b, mlp_b, [own] + ends, const_halves)
            sum_messages(nc, t, 0, t.x2, edge_attr, ends[0], t.seg_dst, "outmsg")
            sum_messages(nc, t, 1, t.x2, edge_attr, ends[1], t.seg_src, "inmsg")
        complete_and_load(nc, t, "ends", [(0, t.seg_dst), (1, t.seg_src)], [])
        last_layer(nc, t, t.x2, own, const_halves, slope, out)


NAMES = ["x", "src", "dst", "edge_attr_512", "L0_gnn_eps", "L0_gnn_W1", "L0_gnn_b1", "L0_gnn_g1", "L0_gnn_be1", "L0_gnn_W2",
         "L0_gnn_b2", "L0_gnn_g2", "L0_gnn_be2", "L1_gnn_W1", "L1_gnn_b1", "L1_gnn_W2", "L1_gnn_b2", "L2_gnn_path_coeffs",
         "L2_gnn_path_indices", "L3_gnn_WO_w", "L3_gnn_WO_b", "L3_gnn_WI_w", "L3_gnn_WI_b", "L3_gnn_WS_w", "L3_gnn_WS_b",
         "L3_gnn_mlp_w", "L3_gnn_mlp_b", "L3_gnn_prelu_a"]


def kernel(**inputs):
    import concourse.bacc as bacc
    from concourse.bass_utils import run_bass_kernel_spmd

    nc = bacc.Bacc("TRN2", target_bir_lowering=False, num_devices=1)
    arrays, args = {}, []
    for name in NAMES:
        a = np.ascontiguousarray(inputs[name])
        a = a.reshape(1) if a.ndim == 0 else a
        arrays[f"in_{name}"] = a
        args.append(nc.dram_tensor(f"in_{name}", a.shape, mybir.dt.from_np(a.dtype), kind="ExternalInput").ap())
    out = nc.dram_tensor("out", (N, D), F32, kind="ExternalOutput").ap()
    gnn_program(nc, *args, out)
    result = run_bass_kernel_spmd(nc, [arrays], core_ids=[0])
    return result.results[0]["out"]
```
